# Optimizing a Trainium2 kernel written in Bass

```python
import numpy as np
import jax
import jax.numpy as jnp

def _softmax(x, axis=-1):
    return jax.nn.softmax(x, axis=axis)

def _gelu(x):
    return jax.nn.gelu(x, approximate=True)

def _silu(x):
    return jax.nn.silu(x)

def _sigmoid(x):
    return jax.nn.sigmoid(x)

def _layernorm(x, axis=-1, eps=1e-05):
    m = jnp.mean(x, axis=axis, keepdims=True)
    v = jnp.var(x, axis=axis, keepdims=True)
    return (x - m) / jnp.sqrt(v + eps)

def _scatter_add(tgt, idx, src, axis=0):
    return tgt.at[idx].add(src)

def _segment_sum(src, seg, n):
    return jax.ops.segment_sum(src, seg, n)
kernel_name = 'mk_decoder_preln_d2_seqx_r8_af3dd3'

def setup_inputs(seed: int=0):
    np.random.seed(seed)
    _w = jnp.asarray

    def _rec_inputs():
        import jax
        import jax.numpy as jnp
        _rk = jax.random.key(seed)
        x = 7.22e-05 + 1 * jax.random.normal(jax.random.fold_in(_rk, 1), (4, 512, 128), jnp.float32)
        _lenS = 512 - jax.random.randint(jax.random.fold_in(_rk, 7), (4,), 0, max(1, 512 // 4) + 1, jnp.int32)
        _lenS2 = 77 - jax.random.randint(jax.random.fold_in(_rk, 8), (4,), 0, max(1, 77 // 4) + 1, jnp.int32)
        _ctx_1024P = jax.random.normal(jax.random.fold_in(_rk, 11), (4, 16, 128), jnp.float32)
        _ctx_1024c = jax.random.dirichlet(jax.random.fold_in(_rk, 511), 0.3 * jnp.ones((16,), jnp.float32), (4, 77))
        _ctx_1024t = jnp.einsum('bsk,bkd->bsd', _ctx_1024c, _ctx_1024P)
        _ctx_1024t = _ctx_1024t * jax.lax.rsqrt(jnp.mean(jnp.square(_ctx_1024t)) + 1e-12) * 0.953939
        ctx_1024 = 4.13588e-05 + 0.999923 * (_ctx_1024t + 0.3 * jax.random.normal(jax.random.fold_in(_rk, 611), (4, 77, 128), jnp.float32))
        fside_BxSxS2_0 = -1.47943e-05 + 1.00017 * jax.random.normal(jax.random.fold_in(_rk, 12), (4, 512, 77), jnp.float32)
        return (x, ctx_1024, fside_BxSxS2_0)
    x, ctx_1024, fside_BxSxS2_0 = _rec_inputs()

    def _L0_attn_setup():
        import math
        import jax, jax.numpy as jnp
        import numpy as np
        N_HEADS = 16
        D_EMBED = 128
        key = jax.random.key(seed)
        ks = jax.random.split(key, 5)
        b, l, d = (2, 256, D_EMBED)
        return {'x': jax.random.normal(ks[0], (b, l, d), dtype=jnp.float32), 'w_in': jax.random.normal(ks[1], (3 * d, d), dtype=jnp.float32) * 0.02, 'b_in': jax.random.normal(ks[2], (3 * d,), dtype=jnp.float32) * 0.02, 'w_out': jax.random.normal(ks[3], (d, d), dtype=jnp.float32) * 0.02, 'b_out': jax.random.normal(ks[4], (d,), dtype=jnp.float32) * 0.02}
    _L0_attn_all = _L0_attn_setup()
    _L0_attn_in = {k: v for k, v in _L0_attn_all.items() if k in ('w_in', 'b_in', 'w_out', 'b_out')}
    del _L0_attn_all

    def _L0_xattn_setup():
        import jax, jax.numpy as jnp
        import numpy as np
        D = 128
        key = jax.random.key(seed)
        ks = jax.random.split(key, 13)
        B, S, d = (4, 256, D)
        inp = {'q_in': jax.random.normal(ks[0], (B, S, d), jnp.float32), 'k_in': jax.random.normal(ks[1], (B, S, d), jnp.float32), 'v_in': jax.random.normal(ks[2], (B, S, d), jnp.float32), 'phi_risk': jax.random.normal(ks[3], (B, S, S), jnp.float32), 'phi_prio': jax.random.normal(ks[4], (B, S, S), jnp.float32), 'phi_impl': jax.random.normal(ks[5], (B, S, S), jnp.float32), 'Wq': jax.random.normal(ks[6], (d, d), jnp.float32) / np.sqrt(d), 'bq': jax.random.normal(ks[7], (d,), jnp.float32) * 0.01, 'Wk': jax.random.normal(ks[8], (d, d), jnp.float32) / np.sqrt(d), 'bk': jax.random.normal(ks[9], (d,), jnp.float32) * 0.01, 'Wv': jax.random.normal(ks[10], (d, d), jnp.float32) / np.sqrt(d), 'bv': jax.random.normal(ks[11], (d,), jnp.float32) * 0.01, 'beta_risk': jnp.float32(0.1), 'beta_prio': jnp.float32(0.1), 'beta_impl': jnp.float32(0.1)}
        return inp
    _L0_xattn_all = _L0_xattn_setup()
    _L0_xattn_in = {k: v for k, v in _L0_xattn_all.items() if k in ('Wq', 'bq', 'Wk', 'bk', 'Wv', 'bv', 'beta_risk', 'beta_prio', 'beta_impl')}
    del _L0_xattn_all

    def _L0_ffn_setup():
        import jax, jax.numpy as jnp
        import numpy as np
        H = 128
        M = 64
        E = 16
        TOP_K = 2
        SCALE = 2.5
        NORM_TOPK = True
        B, S = (1, 128)

        def _moe(x, gate_w, w_gate, w_up, w_down, ws_gate, ws_up, ws_down):
            T = x.shape[0]
            shared = jax.nn.silu(x @ ws_gate) * (x @ ws_up) @ ws_down
            scores = jax.nn.sigmoid(x.astype(jnp.float32) @ gate_w.T.astype(jnp.float32))
            topk_w, topk_idx = jax.lax.top_k(scores, TOP_K)
            if NORM_TOPK and TOP_K > 1:
                topk_w = topk_w / (topk_w.sum(-1, keepdims=True) + 1e-20)
            topk_w = topk_w * SCALE
            route = jnp.zeros((T, E), topk_w.dtype).at[jnp.arange(T)[:, None], topk_idx].set(topk_w)
            g = jnp.einsum('th,ehm->etm', x, w_gate)
            u = jnp.einsum('th,ehm->etm', x, w_up)
            eo = jnp.einsum('etm,emh->eth', jax.nn.silu(g) * u, w_down)
            routed = jnp.einsum('te,eth->th', route.astype(x.dtype), eo)
            return routed + shared
        key = jax.random.key(seed)
        ks = jax.random.split(key, 8)
        std = 0.02
        return {'hidden_states': jax.random.normal(ks[0], (B, S, H), jnp.float32), 'gate_w': jax.random.normal(ks[1], (E, H), jnp.float32) * std, 'w_gate': jax.random.normal(ks[2], (E, H, M), jnp.float32) * std, 'w_up': jax.random.normal(ks[3], (E, H, M), jnp.float32) * std, 'w_down': jax.random.normal(ks[4], (E, M, H), jnp.float32) * std, 'ws_gate': jax.random.normal(ks[5], (H, M), jnp.float32) * std, 'ws_up': jax.random.normal(ks[6], (H, M), jnp.float32) * std, 'ws_down': jax.random.normal(ks[7], (M, H), jnp.float32) * std}
    _L0_ffn_all = _L0_ffn_setup()
    _L0_ffn_in = {k: v for k, v in _L0_ffn_all.items() if k in ('gate_w', 'w_gate', 'w_up', 'w_down', 'ws_gate', 'ws_up', 'ws_down')}
    del _L0_ffn_all

    def _L1_attn_setup():
        import jax, jax.numpy as jnp
        from jax import lax
        import numpy as np
        import math
        EMBED_DIM = 128
        NUM_HEADS = 16
        REDUCTION = 2
        key = jax.random.key(seed)
        ks = jax.random.split(key, 11)
        B, N, C = (2, 512, EMBED_DIM)
        s = 1.0 / math.sqrt(C)
        return {'x': jax.random.normal(ks[0], (B, N, C), jnp.float32), 'q_w': jax.random.normal(ks[1], (C, C), jnp.float32) * s, 'q_b': jax.random.normal(ks[2], (C,), jnp.float32) * s, 'k_w': jax.random.normal(ks[3], (C, C), jnp.float32) * s, 'k_b': jax.random.normal(ks[4], (C,), jnp.float32) * s, 'v_w': jax.random.normal(ks[5], (C, C), jnp.float32) * s, 'v_b': jax.random.normal(ks[6], (C,), jnp.float32) * s, 'conv_w': jax.random.normal(ks[7], (C, 1, 3), jnp.float32) * 0.5, 'conv_b': jax.random.normal(ks[8], (C,), jnp.float32) * 0.1, 'out_w': jax.random.normal(ks[9], (C, C), jnp.float32) * s, 'out_b': jax.random.normal(ks[10], (C,), jnp.float32) * s}
    _L1_attn_all = _L1_attn_setup()
    _L1_attn_in = {k: v for k, v in _L1_attn_all.items() if k in ('q_w', 'q_b', 'k_w', 'k_b', 'v_w', 'v_b', 'conv_w', 'conv_b', 'out_w', 'out_b')}
    del _L1_attn_all

    def _L1_xattn_setup():
        import jax, jax.numpy as jnp
        import numpy as np
        B, M, N, DIM, DH, H = (8, 512, 64, 128, 128, 8)
        INNER = DH * H
        EPS = 1e-05

        def _layernorm(x, g, b):
            mu = jnp.mean(x, axis=-1, keepdims=True)
            var = jnp.var(x, axis=-1, keepdims=True)
            return (x - mu) * jax.lax.rsqrt(var + EPS) * g + b
        key = jax.random.key(seed)
        ks = jax.random.split(key, 8)
        sd = 0.02
        return {'x': jax.random.normal(ks[0], (B, M, DIM), jnp.float32), 'latents': jax.random.normal(ks[1], (B, N, DIM), jnp.float32), 'gamma_media': jnp.ones((DIM,), jnp.float32), 'beta_media': jnp.zeros((DIM,), jnp.float32), 'gamma_lat': jnp.ones((DIM,), jnp.float32), 'beta_lat': jnp.zeros((DIM,), jnp.float32), 'Wq': jax.random.normal(ks[2], (DIM, INNER), jnp.float32) * sd, 'bq': jnp.zeros((INNER,), jnp.float32), 'Wkv': jax.random.normal(ks[3], (DIM, 2 * INNER), jnp.float32) * sd, 'bkv': jnp.zeros((2 * INNER,), jnp.float32), 'Wo': jax.random.normal(ks[4], (INNER, DIM), jnp.float32) * sd, 'bo': jnp.zeros((DIM,), jnp.float32)}
    _L1_xattn_all = _L1_xattn_setup()
    _L1_xattn_in = {k: v for k, v in _L1_xattn_all.items() if k in ('gamma_media', 'beta_media', 'gamma_lat', 'beta_lat', 'Wq', 'bq', 'Wkv', 'bkv', 'Wo', 'bo')}
    del _L1_xattn_all

    def _L1_ffn_setup():
        import jax, jax.numpy as jnp
        import numpy as np
        H = 128
        I = 64
        E = 32
        TOP_K = 6
        N_GROUP = 8
        TOPK_GROUP = 4
        SCALE = 2.5
        N_SHARED = 2
        SI = I * N_SHARED
        B, S = (2, 128)
        key = jax.random.key(seed)
        ks = jax.random.split(key, 8)
        x = jax.random.normal(ks[0], (B, S, H), jnp.float32)
        gate_weight = jax.random.normal(ks[1], (E, H), jnp.float32) * 0.02
        e_score_correction_bias = jax.random.normal(ks[2], (E,), jnp.float32) * 0.01
        experts_gate_up = jax.random.normal(ks[3], (E, 2 * I, H), jnp.float32) * 0.02
        experts_down = jax.random.normal(ks[4], (E, H, I), jnp.float32) * 0.02
        shared_gate_w = jax.random.normal(ks[5], (SI, H), jnp.float32) * 0.02
        shared_up_w = jax.random.normal(ks[6], (SI, H), jnp.float32) * 0.02
        shared_down_w = jax.random.normal(ks[7], (H, SI), jnp.float32) * 0.02
        return {'x': x, 'gate_weight': gate_weight, 'e_score_correction_bias': e_score_correction_bias, 'experts_gate_up': experts_gate_up, 'experts_down': experts_down, 'shared_gate_w': shared_gate_w, 'shared_up_w': shared_up_w, 'shared_down_w': shared_down_w}
    _L1_ffn_all = _L1_ffn_setup()
    _L1_ffn_in = {k: v for k, v in _L1_ffn_all.items() if k in ('gate_weight', 'e_score_correction_bias', 'experts_gate_up', 'experts_down', 'shared_gate_w', 'shared_up_w', 'shared_down_w')}
    del _L1_ffn_all
    return {'x': x, 'ctx_1024': ctx_1024, 'fside_BxSxS2_0': fside_BxSxS2_0, 'L0_attn_w_in': _L0_attn_in['w_in'], 'L0_attn_b_in': _L0_attn_in['b_in'], 'L0_attn_w_out': _L0_attn_in['w_out'], 'L0_attn_b_out': _L0_attn_in['b_out'], 'L0_xattn_Wq': _L0_xattn_in['Wq'], 'L0_xattn_bq': _L0_xattn_in['bq'], 'L0_xattn_Wk': _L0_xattn_in['Wk'], 'L0_xattn_bk': _L0_xattn_in['bk'], 'L0_xattn_Wv': _L0_xattn_in['Wv'], 'L0_xattn_bv': _L0_xattn_in['bv'], 'L0_xattn_beta_risk': _L0_xattn_in['beta_risk'], 'L0_xattn_beta_prio': _L0_xattn_in['beta_prio'], 'L0_xattn_beta_impl': _L0_xattn_in['beta_impl'], 'L0_ffn_gate_w': _L0_ffn_in['gate_w'], 'L0_ffn_w_gate': _L0_ffn_in['w_gate'], 'L0_ffn_w_up': _L0_ffn_in['w_up'], 'L0_ffn_w_down': _L0_ffn_in['w_down'], 'L0_ffn_ws_gate': _L0_ffn_in['ws_gate'], 'L0_ffn_ws_up': _L0_ffn_in['ws_up'], 'L0_ffn_ws_down': _L0_ffn_in['ws_down'], 'L1_attn_q_w': _L1_attn_in['q_w'], 'L1_attn_q_b': _L1_attn_in['q_b'], 'L1_attn_k_w': _L1_attn_in['k_w'], 'L1_attn_k_b': _L1_attn_in['k_b'], 'L1_attn_v_w': _L1_attn_in['v_w'], 'L1_attn_v_b': _L1_attn_in['v_b'], 'L1_attn_conv_w': _L1_attn_in['conv_w'], 'L1_attn_conv_b': _L1_attn_in['conv_b'], 'L1_attn_out_w': _L1_attn_in['out_w'], 'L1_attn_out_b': _L1_attn_in['out_b'], 'L1_xattn_gamma_media': _L1_xattn_in['gamma_media'], 'L1_xattn_beta_media': _L1_xattn_in['beta_media'], 'L1_xattn_gamma_lat': _L1_xattn_in['gamma_lat'], 'L1_xattn_beta_lat': _L1_xattn_in['beta_lat'], 'L1_xattn_Wq': _L1_xattn_in['Wq'], 'L1_xattn_bq': _L1_xattn_in['bq'], 'L1_xattn_Wkv': _L1_xattn_in['Wkv'], 'L1_xattn_bkv': _L1_xattn_in['bkv'], 'L1_xattn_Wo': _L1_xattn_in['Wo'], 'L1_xattn_bo': _L1_xattn_in['bo'], 'L1_ffn_gate_weight': _L1_ffn_in['gate_weight'], 'L1_ffn_e_score_correction_bias': _L1_ffn_in['e_score_correction_bias'], 'L1_ffn_experts_gate_up': _L1_ffn_in['experts_gate_up'], 'L1_ffn_experts_down': _L1_ffn_in['experts_down'], 'L1_ffn_shared_gate_w': _L1_ffn_in['shared_gate_w'], 'L1_ffn_shared_up_w': _L1_ffn_in['shared_up_w'], 'L1_ffn_shared_down_w': _L1_ffn_in['shared_down_w']}

def reference(x, ctx_1024, fside_BxSxS2_0, L0_attn_w_in, L0_attn_b_in, L0_attn_w_out, L0_attn_b_out, L0_xattn_Wq, L0_xattn_bq, L0_xattn_Wk, L0_xattn_bk, L0_xattn_Wv, L0_xattn_bv, L0_xattn_beta_risk, L0_xattn_beta_prio, L0_xattn_beta_impl, L0_ffn_gate_w, L0_ffn_w_gate, L0_ffn_w_up, L0_ffn_w_down, L0_ffn_ws_gate, L0_ffn_ws_up, L0_ffn_ws_down, L1_attn_q_w, L1_attn_q_b, L1_attn_k_w, L1_attn_k_b, L1_attn_v_w, L1_attn_v_b, L1_attn_conv_w, L1_attn_conv_b, L1_attn_out_w, L1_attn_out_b, L1_xattn_gamma_media, L1_xattn_beta_media, L1_xattn_gamma_lat, L1_xattn_beta_lat, L1_xattn_Wq, L1_xattn_bq, L1_xattn_Wkv, L1_xattn_bkv, L1_xattn_Wo, L1_xattn_bo, L1_ffn_gate_weight, L1_ffn_e_score_correction_bias, L1_ffn_experts_gate_up, L1_ffn_experts_down, L1_ffn_shared_gate_w, L1_ffn_shared_up_w, L1_ffn_shared_down_w):
    import jax
    import jax.numpy as jnp

    def _L0_attn_ref(x, w_in, b_in, w_out, b_out):
        import math
        import jax, jax.numpy as jnp
        import numpy as np
        N_HEADS = 16
        D_EMBED = 128
        b, l, d = x.shape
        h = N_HEADS
        scale = 1.0 / math.sqrt(d // h)
        x_proj = (x @ w_in.T + b_in).reshape(b, l, h, -1)
        q, k, v = jnp.split(x_proj, 3, axis=-1)
        att = jnp.einsum('blhd,bmhd->blmh', q, k) * scale
        att = jax.nn.softmax(att, axis=2)
        opt = jnp.einsum('blmh,blhd->blhd', att, v).reshape(b, l, d)
        return opt @ w_out.T + b_out

    def _L0_xattn_ref(q_in, k_in, v_in, phi_risk, phi_prio, phi_impl, Wq, bq, Wk, bk, Wv, bv, beta_risk, beta_prio, beta_impl):
        import jax, jax.numpy as jnp
        import numpy as np
        D = 128
        d = q_in.shape[-1]
        scale = jnp.asarray(d, q_in.dtype) ** (-0.5)
        Q = q_in @ Wq.T + bq
        K = k_in @ Wk.T + bk
        V = v_in @ Wv.T + bv
        att = jnp.einsum('bsd,btd->bst', Q, K) * scale
        att = att + beta_risk * phi_risk + beta_prio * phi_prio - beta_impl * phi_impl
        w = jax.nn.softmax(att, axis=-1)
        return jnp.einsum('bst,btd->bsd', w, V)

    def _L0_ffn_ref(hidden_states, gate_w, w_gate, w_up, w_down, ws_gate, ws_up, ws_down):
        import jax, jax.numpy as jnp
        import numpy as np
        H = 128
        M = 64
        E = 16
        TOP_K = 2
        SCALE = 2.5
        NORM_TOPK = True
        B, S = (1, 128)

        def _moe(x, gate_w, w_gate, w_up, w_down, ws_gate, ws_up, ws_down):
            T = x.shape[0]
            shared = jax.nn.silu(x @ ws_gate) * (x @ ws_up) @ ws_down
            scores = jax.nn.sigmoid(x.astype(jnp.float32) @ gate_w.T.astype(jnp.float32))
            topk_w, topk_idx = jax.lax.top_k(scores, TOP_K)
            if NORM_TOPK and TOP_K > 1:
                topk_w = topk_w / (topk_w.sum(-1, keepdims=True) + 1e-20)
            topk_w = topk_w * SCALE
            route = jnp.zeros((T, E), topk_w.dtype).at[jnp.arange(T)[:, None], topk_idx].set(topk_w)
            g = jnp.einsum('th,ehm->etm', x, w_gate)
            u = jnp.einsum('th,ehm->etm', x, w_up)
            eo = jnp.einsum('etm,emh->eth', jax.nn.silu(g) * u, w_down)
            routed = jnp.einsum('te,eth->th', route.astype(x.dtype), eo)
            return routed + shared
        b, s, h = hidden_states.shape
        x = hidden_states.reshape(-1, h)
        out = _moe(x, gate_w, w_gate, w_up, w_down, ws_gate, ws_up, ws_down)
        return out.reshape(b, s, h)

    def _L1_attn_ref(x, q_w, q_b, k_w, k_b, v_w, v_b, conv_w, conv_b, out_w, out_b):
        import jax, jax.numpy as jnp
        from jax import lax
        import numpy as np
        import math
        EMBED_DIM = 128
        NUM_HEADS = 16
        REDUCTION = 2
        B, N, C = x.shape
        H = NUM_HEADS
        D = C // H
        scale = 1.0 / math.sqrt(D)
        q = x @ q_w.T + q_b
        xd = jnp.transpose(x, (0, 2, 1))
        xd = lax.conv_general_dilated(xd, conv_w, window_strides=(REDUCTION,), padding=[(1, 1)], feature_group_count=C, dimension_numbers=('NCH', 'OIH', 'NCH'))
        xd = xd + conv_b[None, :, None]
        xd = jnp.transpose(xd, (0, 2, 1))
        k = xd @ k_w.T + k_b
        v = xd @ v_w.T + v_b
        Nk = k.shape[1]
        q = q.reshape(B, N, H, D).transpose(0, 2, 1, 3)
        k = k.reshape(B, Nk, H, D).transpose(0, 2, 1, 3)
        v = v.reshape(B, Nk, H, D).transpose(0, 2, 1, 3)
        att = jnp.einsum('bhnd,bhmd->bhnm', q, k) * scale
        att = jax.nn.softmax(att, axis=-1)
        out = jnp.einsum('bhnm,bhmd->bhnd', att, v)
        out = out.transpose(0, 2, 1, 3).reshape(B, N, C)
        return out @ out_w.T + out_b

    def _L1_xattn_ref(x, latents, gamma_media, beta_media, gamma_lat, beta_lat, Wq, bq, Wkv, bkv, Wo, bo):
        import jax, jax.numpy as jnp
        import numpy as np
        B, M, N, DIM, DH, H = (8, 512, 64, 128, 128, 8)
        INNER = DH * H
        EPS = 1e-05

        def _layernorm(x, g, b):
            mu = jnp.mean(x, axis=-1, keepdims=True)
            var = jnp.var(x, axis=-1, keepdims=True)
            return (x - mu) * jax.lax.rsqrt(var + EPS) * g + b
        b = x.shape[0]
        xn = _layernorm(x, gamma_media, beta_media)
        ln = _layernorm(latents, gamma_lat, beta_lat)
        q = ln @ Wq + bq
        kv_input = jnp.concatenate([xn, ln], axis=1)
        kv = kv_input @ Wkv + bkv
        k, v = jnp.split(kv, 2, axis=-1)

        def to_heads(t):
            return t.reshape(b, t.shape[1], H, DH).transpose(0, 2, 1, 3)
        q, k, v = (to_heads(q), to_heads(k), to_heads(v))
        q = q * DH ** (-0.5)
        sim = jnp.einsum('bhid,bhjd->bhij', q, k)
        attn = jax.nn.softmax(sim, axis=-1)
        out = jnp.einsum('bhij,bhjd->bhid', attn, v)
        out = out.transpose(0, 2, 1, 3).reshape(b, -1, INNER)
        return out @ Wo + bo

    def _L1_ffn_ref(x, gate_weight, e_score_correction_bias, experts_gate_up, experts_down, shared_gate_w, shared_up_w, shared_down_w):
        import jax, jax.numpy as jnp
        import numpy as np
        H = 128
        I = 64
        E = 32
        TOP_K = 6
        N_GROUP = 8
        TOPK_GROUP = 4
        SCALE = 2.5
        N_SHARED = 2
        SI = I * N_SHARED
        B, S = (2, 128)
        b, s, h = x.shape
        xf = x.reshape(-1, h)
        T = xf.shape[0]
        logits = xf.astype(jnp.float32) @ gate_weight.astype(jnp.float32).T
        scores = jax.nn.sigmoid(logits)
        sfc = scores + e_score_correction_bias[None, :]
        gs = E // N_GROUP
        group_scores = sfc.reshape(T, N_GROUP, gs).max(axis=-1)
        _, gidx = jax.lax.top_k(group_scores, TOPK_GROUP)
        gmask = jnp.zeros((T, N_GROUP), bool).at[jnp.arange(T)[:, None], gidx].set(True)
        smask = jnp.repeat(gmask, gs, axis=1)
        masked = jnp.where(smask, sfc, 0.0)
        _, topk_idx = jax.lax.top_k(masked, TOP_K)
        tw = jnp.take_along_axis(scores, topk_idx, axis=1)
        tw = tw / (tw.sum(-1, keepdims=True) + 1e-20)
        tw = (tw * SCALE).astype(xf.dtype)
        combine = jnp.zeros((T, E), xf.dtype).at[jnp.arange(T)[:, None], topk_idx].add(tw)

        def expert_step(acc, inp):
            gu, dn, c = inp
            g = xf @ gu[:I].T
            u = xf @ gu[I:].T
            o = jax.nn.silu(g) * u @ dn.T
            return (acc + c[:, None] * o, None)
        routed, _ = jax.lax.scan(expert_step, jnp.zeros_like(xf), (experts_gate_up, experts_down, combine.T))
        sh = jax.nn.silu(xf @ shared_gate_w.T) * (xf @ shared_up_w.T)
        shared_out = sh @ shared_down_w.T
        return (routed + shared_out).reshape(b, s, h)
    x = x + _L0_attn_ref(_layernorm(x, axis=-1), L0_attn_w_in, L0_attn_b_in, L0_attn_w_out, L0_attn_b_out)
    x = x + _L0_xattn_ref(_layernorm(x, axis=-1), ctx_1024, ctx_1024, fside_BxSxS2_0, fside_BxSxS2_0, fside_BxSxS2_0, L0_xattn_Wq, L0_xattn_bq, L0_xattn_Wk, L0_xattn_bk, L0_xattn_Wv, L0_xattn_bv, L0_xattn_beta_risk, L0_xattn_beta_prio, L0_xattn_beta_impl)
    x = x + _L0_ffn_ref(_layernorm(x, axis=-1), L0_ffn_gate_w, L0_ffn_w_gate, L0_ffn_w_up, L0_ffn_w_down, L0_ffn_ws_gate, L0_ffn_ws_up, L0_ffn_ws_down)
    x = x + _L1_attn_ref(_layernorm(x, axis=-1), L1_attn_q_w, L1_attn_q_b, L1_attn_k_w, L1_attn_k_b, L1_attn_v_w, L1_attn_v_b, L1_attn_conv_w, L1_attn_conv_b, L1_attn_out_w, L1_attn_out_b)
    x = x + _L1_xattn_ref(ctx_1024, _layernorm(x, axis=-1), L1_xattn_gamma_media, L1_xattn_beta_media, L1_xattn_gamma_lat, L1_xattn_beta_lat, L1_xattn_Wq, L1_xattn_bq, L1_xattn_Wkv, L1_xattn_bkv, L1_xattn_Wo, L1_xattn_bo)
    x = x + _L1_ffn_ref(_layernorm(x, axis=-1), L1_ffn_gate_weight, L1_ffn_e_score_correction_bias, L1_ffn_experts_gate_up, L1_ffn_experts_down, L1_ffn_shared_gate_w, L1_ffn_shared_up_w, L1_ffn_shared_down_w)
    return x

_drawn_inputs = setup_inputs


def setup_inputs(seed=0):
    import zlib

    import numpy as np

    out = dict(_drawn_inputs(seed))
    spreads = {'L1_xattn_gamma_media': (1.0, 0.6),
     'L1_xattn_beta_media': (0.0, 0.8),
     'L1_xattn_gamma_lat': (1.0, 0.6),
     'L1_xattn_beta_lat': (0.0, 0.743),
     'L1_xattn_bq': (0.0, 2.0),
     'L1_xattn_bkv': (0.0, 0.1),
     'L1_xattn_bo': (0.0, 0.1)}
    factors = {'fside_BxSxS2_0': 4.845,
     'L0_attn_b_in': 8.0,
     'L0_xattn_bq': 8.0,
     'L0_xattn_bk': 64.0,
     'L0_xattn_bv': 4.452,
     'L0_ffn_gate_w': 8.0,
     'L0_ffn_w_gate': 8.0,
     'L0_ffn_w_up': 8.0,
     'L0_ffn_w_down': 8.0,
     'L0_ffn_ws_gate': 8.0,
     'L0_ffn_ws_up': 8.0,
     'L0_ffn_ws_down': 8.0,
     'L1_attn_q_b': 8.0,
     'L1_attn_k_b': 64.0,
     'L1_xattn_Wq': 8.0,
     'L1_ffn_gate_weight': 8.0,
     'L1_ffn_e_score_correction_bias': 8.0,
     'L1_ffn_experts_gate_up': 8.0,
     'L1_ffn_experts_down': 8.0,
     'L1_ffn_shared_gate_w': 8.0,
     'L1_ffn_shared_up_w': 8.0,
     'L1_ffn_shared_down_w': 8.0}
    for name, (base, spread) in spreads.items():
        noise = np.random.default_rng([zlib.crc32(name.encode()), seed]).standard_normal(out[name].shape)
        drawn = base * np.exp(spread * noise) if base else spread * noise
        out[name] = jnp.asarray(drawn.astype(out[name].dtype))
    for name, factor in factors.items():
        out[name] = (out[name] * factor).astype(out[name].dtype)
    return out
```

```python
from contextlib import ExitStack

import numpy as np

import concourse.bass as bass
from concourse import mybir

F32 = mybir.dt.float32
F32R = mybir.dt.float32r
BF16 = mybir.dt.bfloat16
U32 = mybir.dt.uint32
ACT = mybir.ActivationFunctionType
ALU = mybir.AluOpType
AX_X = mybir.AxisListType.X

P = 128
B = 4
S = 512
D = 128
QT = S // P
T = B * QT
C = 77
H = 16
HD = D // H
XH = 8
NK = S // 2
KV = S + C
KT = KV // P + 1
EPS = 1e-5
BF16_ONE = 0x3F80
PARTS = 3
TERMS_Q = [0, 0, 0, 1, 1, 2]
TERMS_K = [0, 1, 2, 0, 1, 0]
KROWS = 96
SLOT_E = 33
ROUTE_ROWS = PARTS * SLOT_E

COLS = {}
_n = 0
for _name, _w in [("a_qkv", 3 * D), ("a_out", D), ("b_q", D), ("b_k", D), ("b_v", D), ("c_gate", 16),
                  ("c_gu", 9 * 2 * D), ("c_down", 9 * D), ("d_q", D), ("d_k", D), ("d_v", D), ("d_out", D),
                  ("e_q", XH * D), ("e_k", XH * D), ("e_vT", XH * D), ("e_o", XH * D), ("f_gate", 32),
                  ("f_gu", 17 * 2 * D), ("f_down", 17 * D)]:
    COLS[_name] = (_n, _n + _w)
    _n += _w
W_COLS = _n
COL = {}
for _name, _w in [("a_bq", 1), ("a_bk", 1), ("a_bv", 1), ("b_bq", 1), ("b_bk", 1), ("d_bq", 1), ("d_bk", 1),
                  ("conv_w", 3), ("conv_b", 1), ("g_lat", 1), ("b_lat", 1), ("g_med", 1), ("b_med", 1),
                  ("e_bo", 1), ("e_bq", XH), ("e_bk", XH), ("e_bv", XH)]:
    COL[_name] = (sum(w for _, w in COL.values()), _w)
N_COL = sum(w for _, w in COL.values())
ROW = {}
for _name, _w in [("a_bo", D), ("b_bv", D), ("d_bv", D), ("d_bo", D), ("g_lat", D), ("b_lat", D),
                  ("g_med", D), ("b_med", D), ("e_score", 32), ("betas", 3), ("iota", 32)]:
    ROW[_name] = (sum(w for _, w in ROW.values()), _w)
N_ROW = sum(w for _, w in ROW.values())


class Memory:

    def __init__(self, nc, ctx, prefix):
        self.nc, self.ctx, self.prefix = nc, ctx, prefix

    def sb(self, name, shape, dt=F32):
        return self.ctx.enter_context(self.nc.sbuf_tensor(self.prefix + name, shape, dt))

    def sem(self, name):
        return self.ctx.enter_context(self.nc.semaphore(self.prefix + name))


STAGE_SEMS = 55
SEM_SETS = [range(256 - 2 * STAGE_SEMS, 256 - STAGE_SEMS), range(256 - STAGE_SEMS, 256)]


class Stage(Memory):

    def __init__(self, nc, ctx, prefix, k):
        super().__init__(nc, ctx, prefix)
        self.ids = iter(SEM_SETS[k.stage % 2])
        self.last_set = SEM_SETS[(k.stage + 1) % 2] if k.stage else None
        k.stage += 1

    def sem(self, name):
        return self.ctx.enter_context(self.nc.semaphore(self.prefix + name, next(self.ids)))

    def clear_last(self, pool):
        if self.last_set:
            pool.sem_clear(self.last_set)


class Kept:
    pass


def wait_apart(eng, k, sem, value):
    eng.wait_ge(sem, value)
    eng.sem_inc(k.passed, 1)


def col(k, name, i=0, rows=P):
    at = COL[name][0] + i
    return k.cols[0:rows, at:at + 1]


def row(k, name, rows=P):
    at, w = ROW[name]
    return k.rows[0:rows, at:at + w]


def weight(k, name):
    a, b = COLS[name]
    return k.w[:, a:b]



class Norm:

    def __init__(self, m, name, batches=B, tiles=QT, rows=P):
        self.tiles, self.rows = tiles, rows
        n = batches * tiles
        self.stats = m.sb(name + "_stats", [P, n, 6])
        self.mv = m.sb(name + "_mean_var", [P, n, 2])
        self.var_eps = m.sb(name + "_var_eps", [P, n])
        self.rstd = m.sb(name + "_rstd", [P, n])
        self.out = m.sb(name + "_normed", [P, n, D])
        self.stats_done = m.sem(name + "_stats_done")
        self.aggregated = m.sem(name + "_aggregated")
        self.var_ready = m.sem(name + "_var_ready")
        self.rstd_ready = m.sem(name + "_rstd_ready")
        self.ready = m.sem(name + "_ready")


def norm_statistics(dve, n, x, b):
    r, tiles = n.rows, range(b * n.tiles, (b + 1) * n.tiles)
    for t in tiles:
        last = dve.bn_stats(n.stats[0:r, t, :], x[0:r, t, :])
    last.then_inc(n.stats_done, 1)
    dve.wait_ge(n.stats_done, b + 1)
    for t in tiles:
        last = dve.bn_aggr(n.mv[0:r, t, :], n.stats[0:r, t, :])
    last.then_inc(n.aggregated, 1)
    dve.wait_ge(n.aggregated, b + 1)
    at = slice(b * n.tiles, (b + 1) * n.tiles)
    dve.tensor_scalar(n.var_eps[0:r, at], n.mv[0:r, at, 1], EPS, None, ALU.add).then_inc(n.var_ready, 1)


def norm_rstd(pool, k, n, b):
    r, at = n.rows, slice(b * n.tiles, (b + 1) * n.tiles)
    pool.wait_ge(n.var_ready, b + 1)
    pool.tensor_tensor(n.rstd[0:r, at], n.var_eps[0:r, at], k.minus_half[0:r, 0:n.tiles],
                       ALU.pow).then_inc(n.rstd_ready, 1)


def norm_apply(dve, n, x, b):
    r = n.rows
    dve.wait_ge(n.rstd_ready, b + 1)
    for t in range(b * n.tiles, (b + 1) * n.tiles):
        last = dve.tensor_scalar(n.out[0:r, t, :], x[0:r, t, :], n.mv[0:r, t, 0:1], n.rstd[0:r, t:t + 1],
                                 ALU.subtract, ALU.mult)
    last.then_inc(n.ready, 1)


def norm_all(dve, n, x, waits=None):
    for b in range(B):
        if waits:
            waits(b)
        norm_statistics(dve, n, x, b)
    for b in range(B):
        norm_apply(dve, n, x, b)


def transpose_batch(pe, k, src, b, bank):
    for q in range(QT):
        last = pe.transpose(k.ps[:, bank, q * P:(q + 1) * P], src[:, b * QT + q, :], k.ident[:, :])
    return last



RING = 4
PARTS_RING = 6


class Split:

    def __init__(self, m):
        self.full = m.sb("split_full", [P, RING, S])
        self.rest = m.sb("split_rest", [P, RING, S])
        self.parts = m.sb("split_parts", [P, PARTS_RING, PARTS, S], BF16)
        self.full_ready = m.sem("split_full_ready")
        self.high_ready = m.sem("split_high_ready")
        self.rest_ready = m.sem("split_rest_ready")
        self.mid_ready = m.sem("split_mid_ready")
        self.low_ready = m.sem("split_low_ready")


def split_scalar(act, s, widths, stored):
    for i in range(2 * B + 1):
        if i < 2 * B:
            w = widths[i % 2]
            act.wait_ge(s.full_ready, i + 1)
            if i >= PARTS_RING:
                act.wait_ge(stored[(i - PARTS_RING) // 2], 32)
            act.copy(s.parts[:, i % PARTS_RING, 0, 0:w], s.full[:, i % RING, 0:w]).then_inc(s.high_ready, 1)
        if i >= 1:
            j, w = i - 1, widths[(i - 1) % 2]
            act.wait_ge(s.rest_ready, j + 1)
            act.copy(s.parts[:, j % PARTS_RING, 1, 0:w], s.rest[:, j % RING, 0:w]).then_inc(s.mid_ready, 1)


def split_vector(dve, s, widths, make_full):
    for i in range(2 * B + 3):
        if i < 2 * B:
            if i >= RING:
                dve.wait_ge(s.rest_ready, i - RING + 1)
            make_full(i, s.full[:, i % RING, 0:widths[i % 2]]).then_inc(s.full_ready, 1)
        if 1 <= i <= 2 * B:
            j, w = i - 1, widths[(i - 1) % 2]
            dve.wait_ge(s.high_ready, j + 1)
            if j >= RING:
                dve.wait_ge(s.low_ready, j - RING + 1)
            dve.tensor_tensor(s.rest[:, j % RING, 0:w], s.full[:, j % RING, 0:w], s.parts[:, j % PARTS_RING, 0, 0:w],
                              ALU.subtract).then_inc(s.rest_ready, 1)
        if i >= 3:
            j, w = i - 3, widths[(i - 3) % 2]
            dve.wait_ge(s.mid_ready, j + 1)
            dve.tensor_tensor(s.parts[:, j % PARTS_RING, 2, 0:w], s.rest[:, j % RING, 0:w], s.parts[:, j % PARTS_RING, 1, 0:w],
                              ALU.subtract).then_inc(s.low_ready, 1)


def store_parts(sp, k, s, b, widths, stored):
    for i in (0, 1):
        sp.wait_ge(s.low_ready, 2 * b + i + 1)
        w = widths[i]
        sp.dma_start(k.scratch[i, b, :, :, 0:w].rearrange("c p t -> p c t"),
                     s.parts[:, (2 * b + i) % PARTS_RING, :, 0:w]).then_inc(stored[b], 16)


def load_stacks(sp, k, b, widths, stored, signal):
    sp.wait_ge(stored[b], 32)
    for term in range(len(TERMS_Q)):
        at = slice(HD * term, HD * (term + 1))
        for i, (stack, parts) in enumerate(((k.q_stack, TERMS_Q), (k.k_stack, TERMS_K))):
            w = widths[i]
            sp.dma_start(stack[at, b % 2, :, 0:w],
                         k.scratch[i, b, parts[term], :, 0:w].rearrange("(h d) t -> d h t", d=HD)
                         ).then_inc(signal, 16)


STACK_LOADED = 16 * 2 * len(TERMS_Q)



def attn0_project(nc, k):
    with ExitStack() as ctx:
        m = Stage(nc, ctx, "a_", k)
        n = Norm(m, "norm")
        s = Split(m)
        xT = n.out[:, :, :].rearrange("p (b q) d -> p b (q d)", b=B)
        in_psum, xT_ready = m.sem("x_in_psum"), m.sem("xT_ready")
        q_done, k_done, v_done = m.sem("q_done"), m.sem("k_done"), m.sem("v_done")
        ctx_done, ctx_copied, zeroed = m.sem("ctx_done"), m.sem("ctx_copied"), m.sem("zeroed")
        block = ctx.enter_context(nc.Block())
        scale = float(HD) ** -0.5
        wa = weight(k, "a_qkv")

        @block.sync
        def _(sp):
            x_dram = k.x_dram.rearrange("b (q p) d -> p (b q) d", p=P)
            for b in range(B):
                sp.dma_start(k.x[:, b * QT:(b + 1) * QT, :], x_dram[:, b * QT:(b + 1) * QT, :]
                             ).then_inc(k.x_loaded[b], 16)
            sp.dma_start(k.ident[:, :], k.ident_dram).then_inc(k.small_loaded, 16)
            sp.dma_start(k.cols[:, :], k.cols_dram).then_inc(k.small_loaded, 16)
            sp.dma_start(k.rows[:, :], k.rows_dram.partition_broadcast(P)).then_inc(k.small_loaded, 16)
            sp.dma_start(k.ctxT[:, :], k.ctxT_dram).then_inc(k.small_loaded, 16)
            for name, (lo, hi) in (("ab", (0, COLS["c_gate"][0])), ("cd", (COLS["c_gate"][0], COLS["e_q"][0])),
                                   ("e", (COLS["e_q"][0], COLS["f_gate"][0])), ("f", (COLS["f_gate"][0], W_COLS))):
                sp.dma_start(k.w[:, lo:hi], k.w_dram[:, lo:hi]).then_inc(k.w_loaded[name], 16)
                if name == "ab":
                    sp.dma_start(k.side[:, :, :], k.side_dram.rearrange("b (q p) c -> p (b q) c", p=P)
                                 ).then_inc(k.side_loaded, 16)
                    sp.dma_start(k.sel[:, :, :], k.sel_dram).then_inc(k.side_loaded, 16)
                    sp.dma_start(k.ident16[:, :], k.ident16_dram).then_inc(k.side_loaded, 16)
                    sp.dma_start(k.media[0:C, :, :], k.ctx_dram.rearrange("b c d -> c b d")
                                 ).then_inc(k.media_loaded, 16)
            sp.wait_ge(zeroed, 2)
            for b in range(B):
                store_parts(sp, k, s, b, (S, S), k.a_stored)
                if b < 2:
                    load_stacks(sp, k, b, (S, S), k.a_stored, k.a_loaded[b])

        @block.gpsimd
        def _(pool):
            m.clear_last(pool)
            pool.memset(k.minus_half[:, :], -0.5).then_inc(k.constants_set, 1)
            pool.wait_ge(k.constants_set, 1)
            for b in range(B):
                norm_rstd(pool, k, n, b)
            pool.memset(k.q_stack[0:KROWS, :, :, :].bitcast(F32), 0.0).then_inc(zeroed, 1)
            pool.memset(k.k_stack[0:KROWS, :, :, :].bitcast(F32), 0.0).then_inc(zeroed, 1)

        @block.vector
        def _(dve):
            norm_all(dve, n, k.x, lambda b: dve.wait_ge(k.x_loaded[b], 16))
            dve.wait_ge(ctx_done, 2)
            dve.tensor_tensor(k.ctx_v[0:C, :, :], k.ps[0:C, 5, :].rearrange("c (b d) -> c b d", b=B),
                              row(k, "b_bv", C).unsqueeze(1).broadcast_to([C, B, D]),
                              ALU.add).then_inc(ctx_copied, 1)

            def full(i, out):
                b = i // 2
                if i % 2 == 0:
                    dve.wait_ge(q_done, b + 1)
                    return dve.tensor_scalar(out, k.ps[:, 4 + b, :], col(k, "a_bq"), scale,
                                             ALU.add, ALU.mult)
                dve.wait_ge(k_done, b + 1)
                return dve.tensor_scalar(out, k.ps[:, b, :], col(k, "a_bk"), None, ALU.add)

            split_vector(dve, s, (S, S), full)

        @block.tensor
        def _(pe):
            pe.wait_ge(k.small_loaded, 64)
            pe.wait_ge(k.w_loaded["ab"], 16)
            pe.matmul(k.ps[:, 4, 0:B * C], weight(k, "b_k"), k.ctxT[:, :], start=True,
                      stop=True).then_inc(ctx_done, 1)
            for b in range(B):
                last = pe.matmul(k.ps[0:C, 5, b * D:(b + 1) * D], k.ctxT[:, b * C:(b + 1) * C],
                                 weight(k, "b_v"), start=True, stop=True)
            last.then_inc(ctx_done, 1)
            for b in range(B):
                pe.wait_ge(n.ready, b + 1)
                transpose_batch(pe, k, n.out, b, b).then_inc(in_psum, 1)
            pe.wait_ge(ctx_copied, 2)
            for b in range(B):
                pe.wait_ge(xT_ready, b + 1)
                pe.matmul(k.ps[:, 4 + b, :], wa[:, 0:D], xT[:, b, :], start=True, stop=True).then_inc(q_done, 1)
                pe.matmul(k.ps[:, b, :], wa[:, D:2 * D], xT[:, b, :], start=True, stop=True).then_inc(k_done, 1)
            for b in range(B):
                pe.wait_ge(s.full_ready, 2 * b + 1)
                pe.matmul(k.ps[:, 4 + b, :], wa[:, 2 * D:3 * D], xT[:, b, :], start=True,
                          stop=True).then_inc(v_done, 1)

        @block.scalar
        def _(act):
            act.wait_ge(ctx_done, 1)
            act.activation(k.ctx_kT[:, :], k.ps[:, 4, 0:B * C], ACT.Identity,
                           bias=col(k, "b_bk")).then_inc(ctx_copied, 1)
            for b in range(B):
                act.wait_ge(in_psum, b + 1)
                act.copy(xT[:, b, :], k.ps[:, b, :]).then_inc(xT_ready, 1)
            split_scalar(act, s, (S, S), k.a_stored)
            for b in range(B):
                act.wait_ge(v_done, b + 1)
                act.activation(k.vT[:, b, :], k.ps[:, 4 + b, :], ACT.Identity,
                               bias=col(k, "a_bv")).then_inc(k.v_ready, 1)



def attn0_heads(nc, k):
    with ExitStack() as ctx:
        m = Stage(nc, ctx, "ah_", k)
        minus_max = m.sb("minus_max", [P, B * H, QT])
        scored, max_ready, slots_free = m.sem("scored"), m.sem("max_ready"), m.sem("slots_free")
        stack_used = m.sem("stack_used")
        block = ctx.enter_context(nc.Block())
        PAIRS = H // 2

        @block.gpsimd
        def _(pool):
            m.clear_last(pool)

        @block.sync
        def _(sp):
            for b in range(2, B):
                sp.wait_ge(stack_used, b - 1)
                load_stacks(sp, k, b, (S, S), k.a_stored, k.a_loaded[b])

        @block.tensor
        def _(pe):
            for b in range(B):
                pe.wait_ge(k.a_loaded[b], STACK_LOADED)
                with pe.Fori(0, PAIRS) as pair:
                    for i in range(4):
                        half = (b * PAIRS + pair) * 4 + i
                        head = pair * 2 + i // 2
                        pe.wait_ge(slots_free, half + 1)
                        for j in range(2):
                            q = 2 * (i % 2) + j
                            last = pe.matmul(k.ps[:, 2 * i + j, :],
                                             k.q_stack[0:KROWS, b % 2, bass.ds(head, 1), q * P:(q + 1) * P]
                                             .rearrange("p a t -> p (a t)"),
                                             k.k_stack[0:KROWS, b % 2, bass.ds(head, 1), :]
                                             .rearrange("p a t -> p (a t)"),
                                             start=True, stop=True)
                        last.then_inc(scored, 1)
                pe.wait_ge(scored, (b + 1) * PAIRS * 4)
                pe.sem_inc(stack_used, 1)

        @block.vector
        def _(dve):
            with dve.Fori(0, B * PAIRS) as pair:
                for i in range(4):
                    dve.wait_ge(scored, pair * 4 + i + 1)
                    dve.tensor_reduce(minus_max[:, bass.ds(pair * 2 + i // 2, 1), 2 * (i % 2):2 * (i % 2) + 2]
                                      .rearrange("p a q -> p (a q)"),
                                      k.ps[:, 2 * i:2 * i + 2, :], AX_X, ALU.max,
                                      negate=True).then_inc(max_ready, 1)

        @block.scalar
        def _(act):
            act.sem_inc(slots_free, 4)
            with act.Fori(0, B * PAIRS) as pair:
                for i in range(4):
                    head = pair * 2 + i // 2
                    wait_apart(act, k, max_ready, pair * 4 + i + 1)
                    for j in range(2):
                        q = 2 * (i % 2) + j
                        last = act.activation(k.ps[:, 2 * i + j, :], k.ps[:, 2 * i + j, :], ACT.Exp,
                                              bias=minus_max[:, bass.ds(head, 1), q:q + 1]
                                              .rearrange("p a q -> p (a q)"),
                                              accum_out=k.exp_sum[:, bass.ds(head, 1), q:q + 1]
                                              .rearrange("p a q -> p (a q)"))
                    last.then_inc(slots_free, 1)



class Route:
    def __init__(self, m, experts, top, groups=0):
        self.experts, self.top, self.groups = experts, top, groups
        e = experts
        self.logits_ready = m.sem("logits_ready")
        self.scores_ready = m.sem("route_scores_ready")
        self.step = m.sem("route_step")
        self.parts_ready = m.sem("route_parts_ready")
        self.turned = m.sem("route_turned")
        self.scores = m.sb("route_scores", [P, T, e])
        self.ranked = m.sb("ranked", [P, T, e])
        self.best = m.sb("best", [P, T, 8])
        self.best_at = m.sb("best_at", [P, T, 8], U32)
        self.best_at_f = m.sb("best_at_f", [P, T, 8])
        self.hits = m.sb("hits", [P, T, e, top])
        self.mask = m.sb("mask", [P, T, e])
        self.chosen = m.sb("chosen", [P, T, e])
        self.total = m.sb("total", [P, T])
        self.inverse = m.sb("route_inverse", [P, T])
        self.route = m.sb("route", [P, T, SLOT_E])
        self.rest = m.sb("route_rest", [P, T, SLOT_E])
        self.parts = m.sb("route_parts", [P, T, PARTS, SLOT_E], BF16)
        if groups:
            self.group_score = m.sb("group_score", [P, T, groups])
            self.group_hits = m.sb("group_hits", [P, T, groups, groups // 2])
            self.group_mask = m.sb("group_mask", [P, T, groups])


def route_vector(dve, k, r):
    e, top = r.experts, r.top
    SCALE = 2.5
    done = [0]

    def step(last):
        done[0] += 1
        last.then_inc(r.step, 1)
        dve.wait_ge(r.step, done[0])

    def top_mask(values, n, count, hits, mask):
        for t in range(T):
            last = dve.max(r.best[:, t, :], values[:, t, :])
        step(last)
        for t in range(T):
            last = dve.max_index(r.best_at[:, t, :], r.best[:, t, :], values[:, t, :])
        step(last)
        step(dve.tensor_copy(r.best_at_f[:, :, :], r.best_at[:, :, :]))
        for b in range(B):
            at = slice(b * QT, (b + 1) * QT)
            last = dve.tensor_tensor(
                hits[:, at, :, :],
                row(k, "iota")[:, 0:n].unsqueeze(1).unsqueeze(3).broadcast_to([P, QT, n, count]),
                r.best_at_f[:, at, 0:count].unsqueeze(2).broadcast_to([P, QT, n, count]), ALU.is_equal)
        step(last)
        step(dve.tensor_reduce(mask[:, :, :], hits[:, :, :, :], AX_X, ALU.add))

    step(dve.memset(r.route[:, :, :], 0.0))
    step(dve.memset(r.route[:, :, SLOT_E - 1:SLOT_E], 1.0))
    dve.wait_ge(r.scores_ready, B)
    values = r.scores
    if r.groups:
        size = e // r.groups
        step(dve.tensor_tensor(r.ranked[:, :, :], r.scores[:, :, :],
                               row(k, "e_score").unsqueeze(1).broadcast_to([P, T, e]), ALU.add))
        step(dve.tensor_reduce(r.group_score[:, :, :],
                               r.ranked[:, :, :].rearrange("p t (g s) -> p t g s", s=size), AX_X, ALU.max))
        top_mask(r.group_score, r.groups, r.groups // 2, r.group_hits, r.group_mask)
        step(dve.tensor_tensor(r.ranked[:, :, :].rearrange("p t (g s) -> p t g s", s=size),
                               r.ranked[:, :, :].rearrange("p t (g s) -> p t g s", s=size),
                               r.group_mask[:, :, :].unsqueeze(3).broadcast_to([P, T, r.groups, size]), ALU.mult))
        values = r.ranked
    top_mask(values, e, top, r.hits, r.mask)
    step(dve.tensor_tensor(r.chosen[:, :, :], r.mask[:, :, :], r.scores[:, :, :], ALU.mult))
    step(dve.tensor_reduce(r.total[:, :], r.chosen[:, :, :], AX_X, ALU.add))
    step(dve.tensor_scalar(r.total[:, :], r.total[:, :], 1e-20, None, ALU.add))
    step(dve.reciprocal(r.inverse[:, :], r.total[:, :]))
    step(dve.scalar_tensor_tensor(r.route[:, :, 0:e], r.chosen[:, :, :], SCALE,
                                  r.inverse[:, :].unsqueeze(2).broadcast_to([P, T, e]), ALU.mult, ALU.mult))
    step(dve.tensor_copy(r.parts[:, :, 0, :], r.route[:, :, :]))
    step(dve.tensor_tensor(r.rest[:, :, :], r.route[:, :, :], r.parts[:, :, 0, :], ALU.subtract))
    step(dve.tensor_copy(r.parts[:, :, 1, :], r.rest[:, :, :]))
    dve.tensor_tensor(r.parts[:, :, 2, :], r.rest[:, :, :], r.parts[:, :, 1, :],
                      ALU.subtract).then_inc(r.parts_ready, 1)


def route_tensor_logits(pe, k, r, gate, xT, b, bank):
    for q in range(QT):
        last = pe.matmul(k.ps[:, bank, q * r.experts:(q + 1) * r.experts], xT[:, b, q * P:(q + 1) * P],
                         gate, start=True, stop=True)
    last.then_inc(r.logits_ready, 1)


def route_scalar_scores(act, k, r, b, bank):
    act.wait_ge(r.logits_ready, b + 1)
    act.activation(r.scores[:, b * QT:(b + 1) * QT, :],
                   k.ps[:, bank, 0:QT * r.experts].rearrange("p (q e) -> p q e", q=QT),
                   ACT.Sigmoid).then_inc(r.scores_ready, 1)


def route_tensor_turn(pe, k, r, b, bank):
    out = k.ps[:, bank, :].bitcast(BF16)
    for q in range(QT):
        last = pe.transpose(out[0:ROUTE_ROWS, q * P:(q + 1) * P],
                            r.parts[:, b * QT + q, :, :].rearrange("p c e -> p (c e)"), k.ident16[:, :])
    last.then_inc(r.turned, 1)



def attn0_out_xattn0(nc, k):
    with ExitStack() as ctx:
        m = Stage(nc, ctx, "b_", k)
        n, n2 = Norm(m, "norm"), Norm(m, "norm2")
        r = Route(m, 16, 2)
        inverse = m.sb("inverse", [P, B * H, QT])
        weight_sum = m.sb("weight_sum", [P, B * H, QT])
        wide = m.sb("wide", [P, T, D])
        attnT = wide[:, :, :].rearrange("p (b q) d -> p b (q d)", b=B)
        xT = n.out[:, :, :].rearrange("p (b q) d -> p b (q d)", b=B)
        qT = m.sb("qT", [P, B, S])
        scores = m.sb("x_scores", [P, T, C])
        minus_max = m.sb("minus_max", [P, T])
        probs = m.sb("probs", [P, T, C])
        exp_sum = m.sb("exp_sum", [P, T])
        x_inverse = m.sb("x_inverse", [P, T])
        probsT = m.sb("probsT", [P, B, S])
        beta = m.sb("beta", [P, 2])
        names = ["inv_ready", "sum_ready", "wide_ready", "sumT", "attn_ready", "projected", "x_ready", "biased",
                 "in_psum", "xT_ready", "q_done", "q_ready", "scored", "beta_ready", "scores_ready", "max_ready",
                 "exp_done", "probsT_done", "probsT_ready", "x_inv_ready", "attended", "x2_ready",
                 "in_psum2", "high_ready", "x32_ready"]
        sem = {x: m.sem(x) for x in names}
        block = ctx.enter_context(nc.Block())
        scale = float(D) ** -0.5

        @block.gpsimd
        def _(pool):
            m.clear_last(pool)
            for b in range(B):
                at = slice(b * QT, (b + 1) * QT)
                pool.tensor_tensor(k.x[:, at, :], k.x[:, at, :],
                                   row(k, "a_bo").unsqueeze(1).broadcast_to([P, QT, D]),
                                   ALU.add).then_inc(sem["biased"], 1)
            for b in range(B):
                norm_rstd(pool, k, n, b)
            for b in range(B):
                norm_rstd(pool, k, n2, b)

        @block.vector
        def _(dve):
            at = ROW["betas"][0]
            dve.tensor_tensor(beta[:, 0:1], k.rows[:, at:at + 1], k.rows[:, at + 1:at + 2],
                              ALU.add).then_inc(sem["beta_ready"], 1)
            dve.reciprocal(inverse[:, :, :], k.exp_sum[:, :, :]).then_inc(sem["inv_ready"], 1)
            dve.wait_ge(sem["beta_ready"], 1)
            dve.tensor_tensor(beta[:, 1:2], beta[:, 0:1], k.rows[:, at + 2:at + 3],
                              ALU.subtract).then_inc(sem["beta_ready"], 1)
            dve.wait_ge(sem["inv_ready"], 1)
            dve.tensor_tensor(weight_sum[:, :, :], k.exp_sum[:, :, :], inverse[:, :, :],
                              ALU.mult).then_inc(sem["sum_ready"], 1)
            dve.wait_ge(sem["sum_ready"], 1)
            for b in range(B):
                dve.tensor_copy(wide[:, b * QT:(b + 1) * QT, :].rearrange("p q (h d) -> p q h d", d=HD),
                                weight_sum[:, b * H:(b + 1) * H, :].rearrange("p h q -> p q h").unsqueeze(3)
                                .broadcast_to([P, QT, H, HD])).then_inc(sem["wide_ready"], 1)
            for b in range(B):
                dve.wait_ge(sem["sumT"], b + 1)
                dve.tensor_tensor(attnT[:, b, :], k.vT[:, b, :], k.ps[:, b, :],
                                  ALU.mult).then_inc(sem["attn_ready"], 1)
            for b in range(B):
                at = slice(b * QT, (b + 1) * QT)
                dve.wait_ge(sem["projected"], b + 1)
                dve.wait_ge(sem["biased"], b + 1)
                dve.tensor_tensor(k.x[:, at, :], k.x[:, at, :],
                                  k.ps[:, 4 + b, :].rearrange("p (q d) -> p q d", d=D),
                                  ALU.add).then_inc(sem["x_ready"], 1)
            norm_all(dve, n, k.x, lambda b: dve.wait_ge(sem["x_ready"], b + 1))
            for b in range(B):
                dve.wait_ge(sem["q_done"], b + 1)
                dve.tensor_scalar(qT[:, b, :], k.ps[:, 4 + b, :], col(k, "b_bq"), scale, ALU.add,
                                  ALU.mult).then_inc(sem["q_ready"], 1)
            dve.wait_ge(k.side_loaded, 48)
            dve.wait_ge(sem["beta_ready"], 2)
            for b in range(B):
                at = slice(b * QT, (b + 1) * QT)
                dve.wait_ge(sem["scored"], b + 1)
                dve.scalar_tensor_tensor(scores[:, at, :], k.side[:, at, :], beta[:, 1:2],
                                         k.ps[:, b, 0:QT * C].rearrange("p (q c) -> p q c", q=QT),
                                         ALU.mult, ALU.add).then_inc(sem["scores_ready"], 1)
                dve.wait_ge(sem["scores_ready"], b + 1)
                dve.tensor_reduce(minus_max[:, at], scores[:, at, :], AX_X, ALU.max,
                                  negate=True).then_inc(sem["max_ready"], 1)
            for b in range(B):
                at = slice(b * QT, (b + 1) * QT)
                dve.wait_ge(sem["exp_done"], b + 1)
                dve.reciprocal(x_inverse[:, at], exp_sum[:, at]).then_inc(sem["x_inv_ready"], 1)
            for b in range(B):
                dve.wait_ge(sem["attended"], b + 1)
                dve.wait_ge(sem["x_inv_ready"], b + 1)
                for q in range(QT):
                    t = b * QT + q
                    last = dve.scalar_tensor_tensor(k.x[:, t, :], k.ps[:, b, q * D:(q + 1) * D],
                                                    x_inverse[:, t:t + 1], k.x[:, t, :], ALU.mult, ALU.add)
                last.then_inc(sem["x2_ready"], 1)
            norm_all(dve, n2, k.x, lambda b: dve.wait_ge(sem["x2_ready"], b + 1))
            for b in range(B):
                dve.wait_ge(sem["high_ready"], b + 1)
                dve.tensor_tensor(k.x_low[:, b, :], k.xT32[:, b, :], k.x_high[:, b, :],
                                  ALU.subtract).then_inc(k.c_x_ready, 1)
            route_vector(dve, k, r)

        @block.tensor
        def _(pe):
            for b in range(B):
                pe.wait_ge(sem["wide_ready"], b + 1)
                transpose_batch(pe, k, wide, b, b).then_inc(sem["sumT"], 1)
            for b in range(B):
                pe.wait_ge(sem["attn_ready"], b + 1)
                for q in range(QT):
                    last = pe.matmul(k.ps[:, 4 + b, q * D:(q + 1) * D], attnT[:, b, q * P:(q + 1) * P],
                                     weight(k, "a_out"), start=True, stop=True)
                last.then_inc(sem["projected"], 1)
            for b in range(B):
                pe.wait_ge(n.ready, b + 1)
                transpose_batch(pe, k, n.out, b, b).then_inc(sem["in_psum"], 1)
            for b in range(B):
                pe.wait_ge(sem["xT_ready"], b + 1)
                pe.wait_ge(sem["x_ready"], b + 1)
                pe.matmul(k.ps[:, 4 + b, :], weight(k, "b_q"), xT[:, b, :], start=True,
                          stop=True).then_inc(sem["q_done"], 1)
            for b in range(B):
                pe.wait_ge(sem["q_ready"], b + 1)
                for q in range(QT):
                    last = pe.matmul(k.ps[:, b, q * C:(q + 1) * C], qT[:, b, q * P:(q + 1) * P],
                                     k.ctx_kT[:, b * C:(b + 1) * C], start=True, stop=True)
                last.then_inc(sem["scored"], 1)
            for b in range(B):
                pe.wait_ge(sem["exp_done"], b + 1)
                for q in range(QT):
                    last = pe.transpose(k.ps[0:C, 4 + b, q * P:(q + 1) * P], probs[:, b * QT + q, :], k.ident[:, :])
                last.then_inc(sem["probsT_done"], 1)
            for b in range(B):
                pe.wait_ge(sem["probsT_ready"], b + 1)
                for q in range(QT):
                    last = pe.matmul(k.ps[:, b, q * D:(q + 1) * D], probsT[0:C, b, q * P:(q + 1) * P],
                                     k.ctx_v[0:C, b, :], start=True, stop=True)
                last.then_inc(sem["attended"], 1)
            for b in range(B):
                pe.wait_ge(n2.ready, b + 1)
                transpose_batch(pe, k, n2.out, b, b).then_inc(sem["in_psum2"], 1)
            pe.wait_ge(k.w_loaded["cd"], 16)
            for b in range(B):
                pe.wait_ge(sem["x32_ready"], b + 1)
                route_tensor_logits(pe, k, r, weight(k, "c_gate"), k.xT32, b, 4 + b)
            pe.wait_ge(r.parts_ready, 1)
            for b in range(B):
                pe.wait_ge(sem["high_ready"], b + 1)
                route_tensor_turn(pe, k, r, b, b)

        @block.scalar
        def _(act):
            for b in range(B):
                act.wait_ge(sem["in_psum"], b + 1)
                act.copy(xT[:, b, :], k.ps[:, b, :]).then_inc(sem["xT_ready"], 1)
            for b in range(B):
                act.wait_ge(sem["max_ready"], b + 1)
                for q in range(QT):
                    t = b * QT + q
                    last = act.activation(probs[:, t, :], scores[:, t, :], ACT.Exp, bias=minus_max[:, t:t + 1],
                                          accum_out=exp_sum[:, t:t + 1])
                last.then_inc(sem["exp_done"], 1)
            for b in range(B):
                act.wait_ge(sem["probsT_done"], b + 1)
                act.copy(probsT[0:C, b, :], k.ps[0:C, 4 + b, :]).then_inc(sem["probsT_ready"], 1)
            for b in range(B):
                act.wait_ge(sem["in_psum2"], b + 1)
                act.copy(k.xT32[:, b, :], k.ps[:, b, :]).then_inc(sem["x32_ready"], 1)
                act.copy(k.x_high[:, b, :], k.ps[:, b, :]).then_inc(sem["high_ready"], 1)
            for b in range(B):
                route_scalar_scores(act, k, r, b, 4 + b)
            for b in range(B):
                act.wait_ge(r.turned, b + 1)
                act.copy(k.routeT[0:ROUTE_ROWS, b, :],
                         k.ps[:, b, :].bitcast(BF16)[0:ROUTE_ROWS, 0:S]).then_inc(k.c_route_ready, 1)



def moe(nc, k, name, gu_name, down_name, units, x_ready, route_ready, store):
    with ExitStack() as ctx:
        m = Stage(nc, ctx, name, k)
        gu_high = m.sb("gu_high", [P, 2, 2 * D], F32R)
        gu_low = m.sb("gu_low", [P, 2, 2 * D], F32R)
        down = m.sb("down", [P, 2, D])
        gated = m.sb("gated", [P, 2, S])
        inner = m.sb("inner", [P, 2, S])
        yT = m.sb("yT", [P, B, S])
        gate_done, up_done, routed = m.sem("gate_done"), m.sem("up_done"), m.sem("routed")
        silu_done, up_used, inner_ready = m.sem("silu_done"), m.sem("up_used"), m.sem("inner_ready")
        down_done, weights_free, high_ready, weights_ready = (
            m.sem("down_done"), m.sem("weights_free"), m.sem("high_ready"), m.sem("weights_ready"))
        y_ready, turned, x_done, stored = m.sem("y_ready"), m.sem("turned"), m.sem("x_done"), m.sem("stored")
        block = ctx.enter_context(nc.Block())
        gu_at, down_at = COLS[gu_name][0], COLS[down_name][0]
        N = units * B
        PAIRS = (units - 1) // 2

        @block.gpsimd
        def _(pool):
            m.clear_last(pool)
            def split(p, buf):
                pool.wait_ge(weights_free, p + 1)
                raw = k.w[:, bass.ds(gu_at + p * 2 * D, 2 * D)]
                pool.tensor_copy(gu_high[:, buf, :], raw).then_inc(high_ready, 1)
                pool.tensor_copy(down[:, buf, :], k.w[:, bass.ds(down_at + p * D, D)])
                wait_apart(pool, k, high_ready, p + 1)
                pool.tensor_tensor(gu_low[:, buf, :], raw, gu_high[:, buf, :],
                                   ALU.subtract).then_inc(weights_ready, 1)

            split(0, 0)
            with pool.Fori(0, PAIRS) as pair:
                split(pair * 2 + 1, 1)
                split(pair * 2 + 2, 0)

        @block.tensor
        def _(pe):
            pe.sem_inc(weights_free, 2)

            def down_step(n, b, buf, first):
                pe.wait_ge(inner_ready, n + 1)
                pe.matmul(k.ps[:, 4 + b, :], down[:, buf, :], inner[:, b % 2, :], start=first, stop=True,
                          skip_group_check=True).then_inc(down_done, 1)

            def unit(p, buf, first=False):
                pe.wait_ge(weights_ready, p + 1)
                for b in range(B):
                    n = p * B + b
                    slots = [(3 * b + i) % 4 for i in range(3)]
                    if not first or b >= 2:
                        pe.wait_ge(inner_ready, n - 1)
                    for half, (slot, done) in enumerate(((slots[0], gate_done), (slots[1], up_done))):
                        if half == 1 and (not first or b >= 1):
                            pe.wait_ge(silu_done, n)
                        w = slice(half * D, (half + 1) * D)
                        pe.matmul(k.ps[:, slot, :], gu_high[:, buf, w], k.x_high[:, b, :], start=True, stop=False)
                        pe.matmul(k.ps[:, slot, :], gu_high[:, buf, w], k.x_low[:, b, :], start=False, stop=False)
                        pe.matmul(k.ps[:, slot, :], gu_low[:, buf, w], k.x_high[:, b, :], start=False,
                                  stop=True).then_inc(done, 1)
                    if not first or b >= 1:
                        pe.wait_ge(up_used, n)
                    pe.matmul(k.ps[:, slots[2], :],
                              k.sel[0:ROUTE_ROWS, bass.ds(p, 1), :].rearrange("r a c -> r (a c)"),
                              k.routeT[0:ROUTE_ROWS, b, :], start=True, stop=True).then_inc(routed, 1)
                    if b >= 1:
                        down_step(n - 1, b - 1, buf, first)
                    elif not first:
                        down_step(n - 1, B - 1, 1 - buf, False if not isinstance(p, int) else p == 1)
                        pe.wait_ge(down_done, n)
                        pe.sem_inc(weights_free, 1)

            unit(0, 0, first=True)
            unit(1, 1)
            unit(2, 0)
            with pe.Fori(1, PAIRS) as pair:
                unit(pair * 2 + 1, 1)
                unit(pair * 2 + 2, 0)
            down_step(N - 1, B - 1, 0, False)
            for b in range(B):
                pe.wait_ge(y_ready, b + 1)
                for q in range(QT):
                    last = pe.transpose(k.ps[:, b, q * P:(q + 1) * P], yT[:, b, q * P:(q + 1) * P], k.ident[:, :])
                last.then_inc(turned, 1)

        @block.scalar
        def _(act):
            def unit(p, first=False):
                for b in range(B):
                    n = p * B + b
                    act.wait_ge(gate_done, n + 1)
                    if not first or b >= 2:
                        act.wait_ge(inner_ready, n - 1)
                    act.activation(gated[:, b % 2, :], k.ps[:, (3 * b) % 4, :], ACT.Silu).then_inc(silu_done, 1)

            unit(0, first=True)
            with act.Fori(1, units) as p:
                unit(p)
            act.wait_ge(down_done, N)
            for b in range(B):
                act.copy(yT[:, b, :], k.ps[:, 4 + b, :]).then_inc(y_ready, 1)

        @block.vector
        def _(dve):
            def unit(p, first=False):
                for b in range(B):
                    n = p * B + b
                    dve.wait_ge(silu_done, n + 1)
                    dve.wait_ge(up_done, n + 1)
                    dve.tensor_tensor(gated[:, b % 2, :], gated[:, b % 2, :], k.ps[:, (3 * b + 1) % 4, :],
                                      ALU.mult).then_inc(up_used, 1)
                    dve.wait_ge(routed, n + 1)
                    dve.wait_ge(up_used, n + 1)
                    if not first or b >= 2:
                        dve.wait_ge(down_done, n - 1)
                    dve.tensor_tensor(inner[:, b % 2, :], gated[:, b % 2, :], k.ps[:, (3 * b + 2) % 4, :],
                                      ALU.mult).then_inc(inner_ready, 1)

            unit(0, first=True)
            with dve.Fori(1, units) as p:
                unit(p)
            for b in range(B):
                at = slice(b * QT, (b + 1) * QT)
                dve.wait_ge(turned, b + 1)
                dve.tensor_tensor(k.x[:, at, :], k.x[:, at, :], k.ps[:, b, :].rearrange("p (q d) -> p q d", d=D),
                                  ALU.add).then_inc(x_done, 1)

        @block.sync
        def _(sp):
            if store:
                out = k.out_dram.rearrange("b (q p) d -> p (b q) d", p=P)
                for b in range(B):
                    at = slice(b * QT, (b + 1) * QT)
                    sp.wait_ge(x_done, b + 1)
                    sp.dma_start(out[:, at, :], k.x[:, at, :]).then_inc(stored, 16)
                sp.wait_ge(stored, 16 * B)



def attn1_project(nc, k):
    with ExitStack() as ctx:
        m = Stage(nc, ctx, "d_", k)
        n = Norm(m, "norm")
        s = Split(m)
        x_padded = m.sb("x_padded", [P, B, S + 2])
        conv = n.out[:, :, :].rearrange("p (b q) d -> p b (q d)", b=B)[:, :, 0:NK]
        in_psum, xT_ready = m.sem("x_in_psum"), m.sem("xT_ready")
        q_done, k_done, v_done = m.sem("q_done"), m.sem("k_done"), m.sem("v_done")
        zeroed, pad_set, v_copied = m.sem("zeroed"), m.sem("pad_set"), m.sem("v_copied")
        taps = [m.sem(f"tap{i}") for i in range(3)]
        block = ctx.enter_context(nc.Block())
        scale = float(HD) ** -0.5

        @block.sync
        def _(sp):
            sp.wait_ge(zeroed, 3)
            for b in range(B):
                store_parts(sp, k, s, b, (S, NK), k.d_stored)
            load_stacks(sp, k, 0, (S, NK), k.d_stored, k.d_loaded)

        @block.gpsimd
        def _(pool):
            m.clear_last(pool)
            pool.memset(x_padded[:, :, 0:1], 0.0).then_inc(pad_set, 1)
            for b in range(B):
                norm_rstd(pool, k, n, b)
            pool.memset(k.v_padded[:, :, :, :], 0.0).then_inc(zeroed, 1)
            pool.memset(k.q_stack[0:KROWS, :, :, :].bitcast(F32), 0.0).then_inc(zeroed, 1)
            pool.memset(k.k_stack[0:KROWS, :, :, :].bitcast(F32), 0.0).then_inc(zeroed, 1)

        @block.vector
        def _(dve):
            norm_all(dve, n, k.x)
            for b in range(B):
                dve.wait_ge(taps[1], b + 1)
                if b == 0:
                    dve.wait_ge(pad_set, 1)
                dve.scalar_tensor_tensor(conv[:, b, :], x_padded[:, b, 0:S:2], col(k, "conv_w", 0), conv[:, b, :],
                                         ALU.mult, ALU.add).then_inc(taps[0], 1)
                dve.wait_ge(taps[0], b + 1)
                dve.scalar_tensor_tensor(conv[:, b, :], x_padded[:, b, 2:S + 2:2], col(k, "conv_w", 2),
                                         conv[:, b, :], ALU.mult, ALU.add).then_inc(taps[2], 1)

            def full(i, out):
                b = i // 2
                if i % 2 == 0:
                    dve.wait_ge(q_done, b + 1)
                    return dve.tensor_scalar(out, k.ps[:, 4 + b, :], col(k, "d_bq"), scale, ALU.add, ALU.mult)
                dve.wait_ge(k_done, b + 1)
                return dve.tensor_scalar(out, k.ps[:, b, 0:NK], col(k, "d_bk"), None, ALU.add)

            split_vector(dve, s, (S, NK), full)
            dve.wait_ge(zeroed, 1)
            bias = row(k, "d_bv").rearrange("p (g j d) -> p g j d", g=4, j=4)
            for b in range(B):
                dve.wait_ge(v_done, b + 1)
                for t in range(NK // P):
                    out = k.v_padded[:, b, t, :].rearrange("p (g x) -> p g x", g=4)[:, :, 0:D]
                    last = dve.tensor_tensor(
                        out.rearrange("p g (j y) -> p g j y", j=4)[:, :, :, 0:HD],
                        k.ps[:, b, t * D:(t + 1) * D].rearrange("p (g j d) -> p g j d", g=4, j=4), bias, ALU.add)
                last.then_inc(v_copied, 1)

        @block.tensor
        def _(pe):
            for b in range(B):
                pe.wait_ge(n.ready, b + 1)
                transpose_batch(pe, k, n.out, b, b).then_inc(in_psum, 1)
            for b in range(B):
                pe.wait_ge(xT_ready, b + 1)
                pe.matmul(k.ps[:, 4 + b, :], weight(k, "d_q"), x_padded[:, b, 1:S + 1], start=True,
                          stop=True).then_inc(q_done, 1)
            for b in range(B):
                pe.wait_ge(taps[2], b + 1)
                pe.matmul(k.ps[:, b, 0:NK], weight(k, "d_k"), conv[:, b, :], start=True,
                          stop=True).then_inc(k_done, 1)
            for b in range(B):
                pe.wait_ge(s.full_ready, 2 * b + 2)
                for t in range(NK // P):
                    last = pe.matmul(k.ps[:, b, t * D:(t + 1) * D], conv[:, b, t * P:(t + 1) * P],
                                     weight(k, "d_v"), start=True, stop=True)
                last.then_inc(v_done, 1)

        @block.scalar
        def _(act):
            for b in range(B):
                act.wait_ge(in_psum, b + 1)
                act.copy(x_padded[:, b, 1:S + 1], k.ps[:, b, :]).then_inc(xT_ready, 1)
                act.wait_ge(xT_ready, b + 1)
                act.activation(conv[:, b, :], x_padded[:, b, 1:S + 1:2], ACT.Identity, bias=col(k, "conv_b"),
                               scale=col(k, "conv_w", 1)).then_inc(taps[1], 1)
            split_scalar(act, s, (S, NK), k.d_stored)



def attn1_heads(nc, k):
    with ExitStack() as ctx:
        m = Stage(nc, ctx, "dh_", k)
        N, BODY = B * H, 8
        minus_max = m.sb("minus_max", [P, N, QT])
        probs = m.sb("probs", [P, 2, QT, NK])
        probsT = m.sb("probsT", [P, 2, NK // P, S])
        v = m.sb("v", [P, 4, NK // P, 32])
        scored, max_ready, exp_done = m.sem("scored"), m.sem("max_ready"), m.sem("exp_done")
        turned = [m.sem("turned0"), m.sem("turned1")]
        copied = [m.sem("copied0"), m.sem("copied1")]
        v_ready, attended, quad_added = m.sem("v_ready"), m.sem("attended"), m.sem("quad_added")
        out_zeroed, stacks_ready = m.sem("out_zeroed"), m.sem("stacks_ready")
        block = ctx.enter_context(nc.Block())

        def scores_of(i):
            return k.ps[:, 2 * (i % 2):2 * (i % 2) + 2, :].rearrange("p a (q t) -> p (a q) t", t=NK)

        def bodies(eng, body):
            body(0, True)
            with eng.Fori(1, N // BODY) as i:
                body(i, False)

        @block.sync
        def _(sp):
            for b in range(B):
                if b >= 2:
                    sp.wait_ge(scored, H * (b - 1))
                if b >= 1:
                    load_stacks(sp, k, b, (S, NK), k.d_stored, k.d_loaded)
                sp.wait_ge(k.d_loaded, STACK_LOADED * (b + 1))
                sp.sem_inc(stacks_ready, H // BODY)

        @block.gpsimd
        def _(pool):
            m.clear_last(pool)
            def body(it, first):
                for i in range(BODY):
                    n = it * BODY + i
                    if not first or i >= 4:
                        pool.wait_ge(attended, n - 3)
                    b, at = it // 2, (i // 4 + 2 * (it % 2)) * P + 32 * (i % 4)
                    pool.tensor_copy(v[:, i % 4, :, :],
                                     k.v_padded[:, bass.ds(b, 1), :, bass.ds(at, 32)]
                                     .rearrange("p a t c -> p (a t) c")).then_inc(v_ready, 1)

            pool.memset(k.attended[:, :, :], 0.0).then_inc(out_zeroed, 1)
            bodies(pool, body)

        @block.tensor
        def _(pe):
            def scores(it, i, first):
                n, b = it * BODY + i, it // 2
                head = (it % 2) * BODY + i
                if i == 0:
                    pe.wait_ge(stacks_ready, it + 1)
                if not first or i >= 2:
                    pe.wait_ge(exp_done, n - 1)
                at = (b % 2) * H + head
                q_rows = k.q_stack[0:KROWS, :, :, :].rearrange("p a h t -> p (a h) t")
                k_rows = k.k_stack[0:KROWS, :, :, :].rearrange("p a h t -> p (a h) t")
                for q in range(QT):
                    last = pe.matmul(scores_of(i)[:, q, :],
                                     q_rows[:, bass.ds(at, 1), q * P:(q + 1) * P].rearrange("p a t -> p (a t)"),
                                     k_rows[:, bass.ds(at, 1), :].rearrange("p a t -> p (a t)"),
                                     start=True, stop=True)
                last.then_inc(scored, 1)

            def turn(n, i, first):
                pe.wait_ge(exp_done, n + 1)
                for t in range(NK // P):
                    if not first:
                        pe.wait_ge(copied[t], n)
                    for q in range(QT):
                        last = pe.transpose(k.ps[:, 4 + t, q * P:(q + 1) * P],
                                            probs[:, i % 2, q, t * P:(t + 1) * P], k.ident[:, :])
                    last.then_inc(turned[t], 1)

            def attend(n, i, quad, first):
                j, bank = i % 4, 6 + i // 4
                if j == 0 and not first:
                    pe.wait_ge(quad_added, quad - 1)
                pe.wait_ge(v_ready, n + 1)
                for t in range(NK // P):
                    pe.wait_ge(copied[t], n + 1)
                    last = pe.matmul(k.ps[32 * j:32 * j + 32, bank, :], v[:, j, t, :], probsT[:, i % 2, t, :],
                                     start=(t == 0), stop=(t == NK // P - 1))
                last.then_inc(attended, 1)

            def body(it, first):
                for i in range(BODY):
                    n = it * BODY + i
                    scores(it, i, first)
                    if not first or i >= 1:
                        turn(n - 1, (i - 1) % BODY, first and i == 1)
                    if not first or i >= 2:
                        attend(n - 2, (i - 2) % BODY, it * 2 + (i - 2) // 4, first)

            bodies(pe, body)
            turn(N - 1, BODY - 1, False)
            attend(N - 2, BODY - 2, N // 4 - 1, False)
            attend(N - 1, BODY - 1, N // 4 - 1, False)

        def copy_turned(eng, copy, n, i, t, first):
            eng.wait_ge(turned[t], n + 1)
            if not first:
                eng.wait_ge(attended, n - 1)
            copy(probsT[:, i % 2, t, :], k.ps[:, 4 + t, :]).then_inc(copied[t], 1)

        @block.vector
        def _(dve):
            def copies(n, i, first):
                copy_turned(dve, dve.tensor_copy, n, i, 0, first)
                if i % 2 == 0:
                    copy_turned(dve, dve.tensor_copy, n, i, 1, first)

            def add_quad(n, i, b):
                dve.wait_ge(attended, n + 1)
                bank = 6 + i // 4
                out = k.attended[:, bass.ds(b, 1), :].rearrange("p a t -> p (a t)")
                dve.tensor_tensor(out, out, k.ps[:, bank, :], ALU.add).then_inc(quad_added, 1)

            def body(it, first):
                for i in range(BODY):
                    n = it * BODY + i
                    dve.wait_ge(scored, n + 1)
                    dve.tensor_reduce(minus_max[:, bass.ds(n, 1), :].rearrange("p a q -> p (a q)"),
                                      scores_of(i), AX_X, ALU.max, negate=True).then_inc(max_ready, 1)
                    if not first or i >= 1:
                        copies(n - 1, (i - 1) % BODY, first and i <= 2)
                    if i % 4 == 2 and (not first or i >= 6):
                        if first:
                            dve.wait_ge(out_zeroed, 1)
                        if not first:
                            dve.wait_ge(quad_added, it * 2 + (i - 3) // 4)
                        add_quad(n - 3, (i - 3) % BODY, (it - 1) // 2 if i == 2 else it // 2)

            bodies(dve, body)
            copies(N - 1, BODY - 1, False)
            dve.wait_ge(quad_added, N // 4 - 1)
            add_quad(N - 1, BODY - 1, B - 1)

        @block.scalar
        def _(act):
            def copies(n, i, first):
                if i % 2 == 1:
                    copy_turned(act, act.copy, n, i, 1, first)

            def body(it, first):
                for i in range(BODY):
                    n = it * BODY + i
                    if not first or i >= 2:
                        act.wait_ge(turned[1], n - 1)
                    wait_apart(act, k, max_ready, n + 1)
                    for q in range(QT):
                        last = act.activation(probs[:, i % 2, q, :], scores_of(i)[:, q, :], ACT.Exp,
                                              bias=minus_max[:, bass.ds(n, 1), q:q + 1]
                                              .rearrange("p a q -> p (a q)"),
                                              accum_out=k.exp_sum[:, bass.ds(n, 1), q:q + 1]
                                              .rearrange("p a q -> p (a q)"))
                    last.then_inc(exp_done, 1)
                    if not first or i >= 1:
                        copies(n - 1, (i - 1) % BODY, first and i <= 2)

            bodies(act, body)
            copies(N - 1, BODY - 1, False)



def attn1_out_latents(nc, k):
    with ExitStack() as ctx:
        m = Stage(nc, ctx, "e0_", k)
        n, n2 = Norm(m, "norm"), Norm(m, "latent")
        nm = Norm(m, "media", tiles=1, rows=C)
        inverse = m.sb("inverse", [P, B * H, QT])
        wide = m.sb("wide", [P, T, D])
        attnT = wide[:, :, :].rearrange("p (b q) d -> p b (q d)", b=B)
        out_bias = m.sb("out_bias", [P, 1])
        names = ["inv_ready", "wide_ready", "invT", "attn_ready", "projected", "x_ready", "biased", "scaled_w",
                 "scaled", "shifted", "media_scaled", "media_shifted", "in_psum", "media_in_psum", "high", "low",
                 "media_high", "media_low", "token_high", "media_token_high", "folded", "bias_sum", "pad_set"]
        sem = {x: m.sem(x) for x in names}
        block = ctx.enter_context(nc.Block())
        scale = float(D) ** -0.5

        @block.gpsimd
        def _(pool):
            m.clear_last(pool)
            for b in range(B):
                at = slice(b * QT, (b + 1) * QT)
                pool.tensor_tensor(k.x[:, at, :], k.x[:, at, :],
                                   row(k, "d_bo").unsqueeze(1).broadcast_to([P, QT, D]),
                                   ALU.add).then_inc(sem["biased"], 1)
            pool.wait_ge(k.w_loaded["e"], 16)
            at, w = COL["e_bq"]
            pool.tensor_scalar(weight(k, "e_q"), weight(k, "e_q"), scale, 1.0, ALU.mult,
                               ALU.mult).then_inc(sem["scaled_w"], 1)
            pool.tensor_scalar(k.cols[:, at:at + w], k.cols[:, at:at + w], scale, 1.0, ALU.mult,
                               ALU.mult).then_inc(sem["scaled_w"], 1)
            pool.memset(k.kvT_high[:, :, S + C:].bitcast(F32), 0.0).then_inc(sem["pad_set"], 1)
            pool.memset(k.kvT_low[:, :, S + C:].bitcast(F32), 0.0).then_inc(sem["pad_set"], 1)
            for b in range(B):
                norm_rstd(pool, k, nm, b)
            for b in range(B):
                norm_rstd(pool, k, n, b)
            for b in range(B):
                pool.wait_ge(nm.ready, b + 1)
                pool.tensor_tensor(nm.out[0:C, b, :], nm.out[0:C, b, :], row(k, "g_med", C),
                                   ALU.mult).then_inc(sem["media_scaled"], 1)
                pool.wait_ge(sem["media_scaled"], b + 1)
                pool.tensor_tensor(nm.out[0:C, b, :], nm.out[0:C, b, :], row(k, "b_med", C),
                                   ALU.add).then_inc(sem["media_shifted"], 1)
            for b in range(B):
                norm_rstd(pool, k, n2, b)

        @block.vector
        def _(dve):
            norm_all(dve, nm, k.media, lambda b: dve.wait_ge(k.media_loaded, 16))
            dve.reciprocal(inverse[:, :, :], k.exp_sum[:, :, :]).then_inc(sem["inv_ready"], 1)
            dve.wait_ge(sem["inv_ready"], 1)
            for b in range(B):
                for q in range(QT):
                    last = dve.tensor_copy(
                        wide[:, b * QT + q, :].rearrange("p (j g d) -> p j g d", j=4, g=4),
                        inverse[:, b * H:(b + 1) * H, q].rearrange("p (g j) -> p j g", j=4).unsqueeze(3)
                        .broadcast_to([P, 4, 4, HD]))
                last.then_inc(sem["wide_ready"], 1)
            for b in range(B):
                dve.wait_ge(sem["invT"], b + 1)
                dve.tensor_tensor(attnT[:, b, :], k.attended[:, b, :], k.ps[:, b, :],
                                  ALU.mult).then_inc(sem["attn_ready"], 1)
            for b in range(B):
                at = slice(b * QT, (b + 1) * QT)
                dve.wait_ge(sem["projected"], b + 1)
                dve.wait_ge(sem["biased"], b + 1)
                dve.tensor_tensor(k.x[:, at, :], k.x[:, at, :],
                                  k.ps[:, 4 + b, :].rearrange("p (q d) -> p q d", d=D),
                                  ALU.add).then_inc(sem["x_ready"], 1)
            norm_all(dve, n, k.x, lambda b: dve.wait_ge(sem["x_ready"], b + 1))
            norm_all(dve, n2, n.out, lambda b: dve.wait_ge(n.ready, b + 1))
            for b in range(B):
                at = slice(b * QT, (b + 1) * QT)
                dve.wait_ge(n2.ready, b + 1)
                dve.tensor_tensor(n2.out[:, at, :], n2.out[:, at, :],
                                  row(k, "g_lat").unsqueeze(1).broadcast_to([P, QT, D]),
                                  ALU.mult).then_inc(sem["scaled"], 1)
            for b in range(B):
                at = slice(b * QT, (b + 1) * QT)
                dve.wait_ge(sem["scaled"], b + 1)
                dve.tensor_tensor(n2.out[:, at, :], n2.out[:, at, :],
                                  row(k, "b_lat").unsqueeze(1).broadcast_to([P, QT, D]),
                                  ALU.add).then_inc(sem["shifted"], 1)
            for b in range(B):
                at = slice(b * QT, (b + 1) * QT)
                dve.wait_ge(sem["high"], b + 1)
                dve.tensor_tensor(k.kvT_low[:, b, 0:S], k.ps[:, b, :], k.kvT_high[:, b, 0:S],
                                  ALU.subtract).then_inc(sem["low"], 1)
                dve.wait_ge(sem["media_high"], b + 1)
                dve.tensor_tensor(k.kvT_low[:, b, S:KV], k.ps[:, 4 + b, 0:C], k.kvT_high[:, b, S:KV],
                                  ALU.subtract).then_inc(sem["media_low"], 1)
                dve.wait_ge(sem["token_high"], b + 1)
                dve.tensor_tensor(k.kv_low[:, b, 0:QT, :], n2.out[:, at, :], k.kv_high[:, b, 0:QT, :],
                                  ALU.subtract)
                dve.wait_ge(sem["media_token_high"], b + 1)
                dve.tensor_tensor(k.kv_low[0:C, b, QT, :], nm.out[0:C, b, :], k.kv_high[0:C, b, QT, :],
                                  ALU.subtract).then_inc(k.kv_ready, 1)
            dve.wait_ge(sem["bias_sum"], 1)
            dve.tensor_scalar(k.out_bias[:, :], k.ps[:, 6, 0:1], col(k, "e_bo"), None,
                              ALU.add).then_inc(k.kv_ready, 1)

        @block.tensor
        def _(pe):
            for b in range(B):
                pe.wait_ge(sem["wide_ready"], b + 1)
                transpose_batch(pe, k, wide, b, b).then_inc(sem["invT"], 1)
            for b in range(B):
                pe.wait_ge(sem["attn_ready"], b + 1)
                for q in range(QT):
                    last = pe.matmul(k.ps[:, 4 + b, q * D:(q + 1) * D], attnT[:, b, q * P:(q + 1) * P],
                                     weight(k, "d_out"), start=True, stop=True)
                last.then_inc(sem["projected"], 1)
            for b in range(B):
                pe.wait_ge(sem["media_shifted"], b + 1)
                pe.wait_ge(sem["x_ready"], b + 1)
                pe.transpose(k.ps[:, 4 + b, 0:C], nm.out[0:C, b, :], k.ident[0:C, 0:C]
                             ).then_inc(sem["media_in_psum"], 1)
            for b in range(B):
                pe.wait_ge(sem["shifted"], b + 1)
                transpose_batch(pe, k, n2.out, b, b).then_inc(sem["in_psum"], 1)
            for g in range(2):
                pe.wait_ge(sem["media_low"], g + 1)
                for j in range(4):
                    h = slice((4 * g + j) * D, (4 * g + j + 1) * D)
                    last = pe.matmul(k.ps[:, 4 + g, j * D:(j + 1) * D], weight(k, "e_vT")[:, h],
                                     weight(k, "e_o")[:, h], start=True, stop=True)
                last.then_inc(sem["folded"], 1)
            pe.wait_ge(sem["media_low"], 3)
            for h in range(XH):
                last = pe.matmul(k.ps[:, 6, 0:1], weight(k, "e_o")[:, h * D:(h + 1) * D], col(k, "e_bv", h),
                                 start=(h == 0), stop=(h == XH - 1))
            last.then_inc(sem["bias_sum"], 1)

        @block.scalar
        def _(act):
            for b in range(B):
                act.wait_ge(sem["media_in_psum"], b + 1)
                act.copy(k.kvT_high[:, b, S:KV], k.ps[:, 4 + b, 0:C]).then_inc(sem["media_high"], 1)
                act.copy(k.kv_high[0:C, b, QT, :], nm.out[0:C, b, :]).then_inc(sem["media_token_high"], 1)
            for b in range(B):
                at = slice(b * QT, (b + 1) * QT)
                act.wait_ge(sem["in_psum"], b + 1)
                act.copy(k.kvT_high[:, b, 0:S], k.ps[:, b, :]).then_inc(sem["high"], 1)
                act.copy(k.kv_high[:, b, 0:QT, :], n2.out[:, at, :]).then_inc(sem["token_high"], 1)
            for g in range(2):
                act.wait_ge(sem["folded"], g + 1)
                act.copy(k.w_vo[:, 4 * g:4 * g + 4, :],
                         k.ps[:, 4 + g, :].rearrange("p (h d) -> p h d", h=4)).then_inc(k.kv_ready, 1)



def xattn1_heads(nc, k):
    with ExitStack() as ctx:
        m = Stage(nc, ctx, "e_", k)
        U = XH * B
        wq = m.sb("wq", [P, 2, D], F32R)
        wk = m.sb("wk", [P, 2, D], F32R)
        wo = m.sb("wo", [P, D])
        qT = m.sb("qT", [P, 2, 2, S], F32R)
        kT = m.sb("kT", [P, 2, 2, KV + 1], F32R)
        probs = m.sb("probs", [P, 2 * QT, KV])
        minus_max, exp_sum, inverse = (m.sb("minus_max", [P, 4]), m.sb("exp_sum", [P, 4]), m.sb("inverse", [P, 4]))
        turned_high = m.sb("turned_high", [P, 2, KT, S], F32R)
        turned_low = m.sb("turned_low", [P, 2, KT, S], F32R)
        attn = weight(k, "e_o").rearrange("p (a t) -> p a t", a=2)
        names = ["w_high", "w_ready", "wo_ready", "q_done", "k_done", "km_done", "q_high", "k_high", "km_high",
                 "q_low", "k_low", "km_low", "scored", "max_ready", "exp_done", "inv_ready", "normed", "turned",
                 "t_high", "t_low", "attended", "attn_ready", "out_done", "added"]
        sem = {x: m.sem(x) for x in names}
        block = ctx.enter_context(nc.Block())
        eq, ek = COLS["e_q"][0], COLS["e_k"][0]
        bq, bk = COL["e_bq"][0], COL["e_bk"][0]

        def pair(q):
            return k.ps[:, 2 * (q % 2):2 * (q % 2) + 2, :].rearrange("p a t -> p (a t)")

        def heads(eng, body):
            for h in (0, None, XH - 1):
                if h is not None:
                    for b in range(B):
                        body(h, b, h == 0, h == XH - 1)
                else:
                    with eng.Fori(1, XH - 1) as i:
                        for b in range(B):
                            body(i, b, False, False)

        @block.gpsimd
        def _(pool):
            m.clear_last(pool)
            def weights(h):
                for w, at in ((wq, eq), (wk, ek)):
                    pool.tensor_copy(w[:, 0, :], k.w[:, bass.ds(at + h * D, D)]).then_inc(sem["w_high"], 1)
                wait_apart(pool, k, sem["w_high"], 2 * h + 2)
                for w, at in ((wq, eq), (wk, ek)):
                    last = pool.tensor_tensor(w[:, 1, :], k.w[:, bass.ds(at + h * D, D)], w[:, 0, :], ALU.subtract)
                last.then_inc(sem["w_ready"], 1)

            def output_weights(h):
                pool.tensor_copy(wo[:, :], k.w_vo[:, bass.ds(h, 1), :].rearrange("p a d -> p (a d)")
                                 ).then_inc(sem["wo_ready"], 1)

            def body(h, b, first, last):
                u = 4 * h + b
                if b == 1 and not first:
                    pool.wait_ge(sem["out_done"], u - 1)
                    output_weights(h)
                for q in range(QT):
                    s = 4 * u + q
                    at = probs[:, (b % 2) * QT + q, :]
                    wait_apart(pool, k, sem["inv_ready"], s + 1)
                    pool.tensor_scalar(at, at, inverse[:, q:q + 1], 1.0, ALU.mult,
                                       ALU.mult).then_inc(sem["normed"], 1)
                    if b == 2 and q == 1 and not last:
                        pool.wait_ge(sem["km_done"], u + 2)
                        weights(h + 1)

            weights(0)
            output_weights(0)
            heads(pool, body)

        @block.tensor
        def _(pe):
            def three(out, high, low, m_high, m_low):
                pe.matmul(out, high, m_high, start=True, stop=False)
                pe.matmul(out, high, m_low, start=False, stop=False)
                return pe.matmul(out, low, m_high, start=False, stop=True)

            def project_q(u, b):
                three(k.ps[:, 6, :], wq[:, 0, :], wq[:, 1, :], k.kvT_high[:, b, 0:S],
                      k.kvT_low[:, b, 0:S]).then_inc(sem["q_done"], 1)

            def project_k(u, b):
                three(k.ps[:, 7, :], wk[:, 0, :], wk[:, 1, :], k.kvT_high[:, b, 0:S],
                      k.kvT_low[:, b, 0:S]).then_inc(sem["k_done"], 1)

            def project_media(u, b):
                three(k.ps[:, 7, 0:C + 1], wk[:, 0, :], wk[:, 1, :], k.kvT_high[:, b, S:KV + 1],
                      k.kvT_low[:, b, S:KV + 1]).then_inc(sem["km_done"], 1)

            def scores(s, b, q):
                v, t = b % 2, slice(q * P, (q + 1) * P)
                for lo, hi in ((0, S), (S, KV + 1)):
                    last = three(pair(q)[:, lo:hi], qT[:, v, 0, t], qT[:, v, 1, t], kT[:, v, 0, lo:hi],
                                 kT[:, v, 1, lo:hi])
                last.then_inc(sem["scored"], 1)

            def turn(u, b, q, free):
                use = 5 * u + q
                bank = 4 + (b + q) % 2
                pe.wait_ge(sem["normed"], 4 * u + min(q, QT - 1) + 1)
                if free:
                    pe.wait_ge(sem["t_low"], use - 1)
                for i in range(QT):
                    if q < QT:
                        out, src = k.ps[:, bank, i * P:(i + 1) * P], probs[:, (b % 2) * QT + q, i * P:(i + 1) * P]
                    else:
                        out, src = k.ps[0:C, bank, i * P:(i + 1) * P], probs[:, (b % 2) * QT + i, S:KV]
                    last = pe.transpose(out, src, k.ident[:, :])
                last.then_inc(sem["turned"], 1)

            def attend(u, b):
                pe.wait_ge(sem["t_low"], 5 * u + 5)
                for i in range(KT):
                    r = P if i < QT else C
                    kv = (k.kv_high[0:r, b, i, :], k.kv_low[0:r, b, i, :])
                    pt = (turned_high[0:r, b % 2, i, :], turned_low[0:r, b % 2, i, :])
                    pe.matmul(k.ps[:, 7, :], kv[0], pt[0], start=(i == 0), stop=False)
                    pe.matmul(k.ps[:, 7, :], kv[0], pt[1], start=False, stop=False)
                    last = pe.matmul(k.ps[:, 7, :], kv[1], pt[0], start=False, stop=(i == KT - 1))
                last.then_inc(sem["attended"], 1)

            def output(u, h, b):
                pe.wait_ge(sem["attn_ready"], u + 1)
                if b == 0:
                    pe.wait_ge(sem["wo_ready"], h + 1)
                pe.matmul(k.ps[:, 6, :], wo[:, :], attn[:, b % 2, :], start=True,
                          stop=True).then_inc(sem["out_done"], 1)

            def body(h, b, first, last):
                u = 4 * h + b
                some1, some2 = not first or b >= 1, not first or b >= 2
                more = not last or b < B - 1
                nb = (b + 1) % B
                pe.wait_ge(sem["q_low"], u + 1)
                pe.wait_ge(sem["km_low"], u + 1)
                for q in range(QT):
                    s = 4 * u + q
                    if not first or b or q >= 2:
                        pe.wait_ge(sem["exp_done"], s - 1)
                    scores(s, b, q)
                    if q == 0:
                        if some2:
                            output(u - 2, h if b >= 2 else h - 1, (b + 2) % B)
                        if some1:
                            turn(u - 1, (b + 3) % B, 2, True)
                        if more:
                            if nb == 0:
                                pe.wait_ge(sem["w_ready"], h + 2)
                            if some2:
                                pe.wait_ge(sem["attn_ready"], u - 1)
                            project_k(u + 1, nb)
                    if q == 1:
                        if some1:
                            turn(u - 1, (b + 3) % B, 3, True)
                            turn(u - 1, (b + 3) % B, 4, True)
                        if more:
                            if some2:
                                pe.wait_ge(sem["added"], u - 1)
                            project_q(u + 1, nb)
                    if q == 2:
                        turn(u, b, 0, some1)
                        if more:
                            pe.wait_ge(sem["k_low"], u + 2)
                            project_media(u + 1, nb)
                    if q == 3:
                        turn(u, b, 1, some1)
                        if some1:
                            if more:
                                pe.wait_ge(sem["km_low"], u + 2)
                            else:
                                pe.wait_ge(sem["attn_ready"], u - 1)
                            attend(u - 1, (b + 3) % B)

            pe.wait_ge(k.kv_ready, B + 3)
            pe.wait_ge(sem["w_ready"], 1)
            project_q(0, 0)
            project_k(0, 0)
            pe.wait_ge(sem["k_low"], 1)
            project_media(0, 0)
            heads(pe, body)
            u = U - 1
            output(u - 1, XH - 1, (u - 1) % B)
            for q in (2, 3, 4):
                turn(u, B - 1, q, True)
            pe.wait_ge(sem["attn_ready"], u)
            attend(u, B - 1)
            pe.wait_ge(sem["added"], u)
            output(u, XH - 1, B - 1)

        def bias_col(at, h):
            return k.cols[:, bass.ds(at + h, 1)]

        @block.scalar
        def _(act):
            def high_q(u, h, b):
                wait_apart(act, k, sem["q_done"], u + 1)
                act.activation(qT[:, b % 2, 0, :], k.ps[:, 6, :], ACT.Identity,
                               bias=bias_col(bq, h)).then_inc(sem["q_high"], 1)

            def high_k(u, h, b):
                wait_apart(act, k, sem["k_done"], u + 1)
                act.activation(kT[:, b % 2, 0, 0:S], k.ps[:, 7, :], ACT.Identity,
                               bias=bias_col(bk, h)).then_inc(sem["k_high"], 1)

            def high_media(u, h, b):
                wait_apart(act, k, sem["km_done"], u + 1)
                act.activation(kT[:, b % 2, 0, S:KV + 1], k.ps[:, 7, 0:C + 1], ACT.Identity,
                               bias=bias_col(bk, h)).then_inc(sem["km_high"], 1)

            def exps(u, b, q, free, free4):
                s = 4 * u + q
                act.wait_ge(sem["max_ready"], s + 1)
                if free:
                    act.wait_ge(sem["turned"], 5 * u - 5)
                act.activation(probs[:, (b % 2) * QT + q, :], pair(q)[:, 0:KV], ACT.Exp,
                               bias=minus_max[:, q:q + 1], accum_out=exp_sum[:, q:q + 1]
                               ).then_inc(sem["exp_done"], 1)

            def high_turned(u, b, q, free):
                use = 5 * u + q
                bank = 4 + (b + q) % 2
                act.wait_ge(sem["turned"], use + 1)
                if free:
                    act.wait_ge(sem["attended"], u - 1)
                if q < QT:
                    act.copy(turned_high[:, b % 2, 0:QT, q * P:(q + 1) * P],
                             k.ps[:, bank, :].rearrange("p (i t) -> p i t", t=P)).then_inc(sem["t_high"], 1)
                else:
                    act.copy(turned_high[0:C, b % 2, QT, :], k.ps[0:C, bank, :]).then_inc(sem["t_high"], 1)

            def take_attended(u, b, free):
                act.wait_ge(sem["attended"], u + 1)
                if free:
                    act.wait_ge(sem["out_done"], u - 1)
                act.copy(attn[:, b % 2, :], k.ps[:, 7, :]).then_inc(sem["attn_ready"], 1)

            def body(h, b, first, last):
                u = 4 * h + b
                some1, some2, some3 = (not first or b >= i for i in (1, 2, 3))
                more = not last or b < B - 1
                nb, nh = (b + 1) % B, h if b < B - 1 else h + 1
                exps(u, b, 0, some2, some1)
                if some1:
                    high_turned(u - 1, (b + 3) % B, 2, some3)
                if more:
                    high_k(u + 1, nh, nb)
                exps(u, b, 1, some2, some1)
                if some1:
                    high_turned(u - 1, (b + 3) % B, 3, some3)
                    high_turned(u - 1, (b + 3) % B, 4, some3)
                if more:
                    high_q(u + 1, nh, nb)
                exps(u, b, 2, some2, some1)
                high_turned(u, b, 0, some2)
                if more:
                    high_media(u + 1, nh, nb)
                exps(u, b, 3, some2, some1)
                high_turned(u, b, 1, some2)
                if some1:
                    take_attended(u - 1, (b + 3) % B, some3)

            high_q(0, 0, 0)
            high_k(0, 0, 0)
            high_media(0, 0, 0)
            heads(act, body)
            for q in (2, 3, 4):
                high_turned(U - 1, B - 1, q, True)
            take_attended(U - 1, B - 1, True)

        @block.vector
        def _(dve):
            def low_part(u, h, b, out, high, bank, at, w, high_sem, low_sem):
                dve.wait_ge(sem[high_sem], u + 1)
                dve.scalar_tensor_tensor(out, k.ps[:, bank, 0:w], bias_col(at, h), high, ALU.add,
                                         ALU.subtract).then_inc(sem[low_sem], 1)

            def low_q(u, h, b):
                low_part(u, h, b, qT[:, b % 2, 1, :], qT[:, b % 2, 0, :], 6, bq, S, "q_high", "q_low")

            def low_k(u, h, b):
                low_part(u, h, b, kT[:, b % 2, 1, 0:S], kT[:, b % 2, 0, 0:S], 7, bk, S, "k_high", "k_low")

            def low_media(u, h, b):
                low_part(u, h, b, kT[:, b % 2, 1, S:KV + 1], kT[:, b % 2, 0, S:KV + 1], 7, bk, C + 1,
                         "km_high", "km_low")

            def invert(s, q, free):
                dve.wait_ge(sem["exp_done"], s + 1)
                if free:
                    dve.wait_ge(sem["normed"], s - 3)
                dve.reciprocal(inverse[:, q:q + 1], exp_sum[:, q:q + 1]).then_inc(sem["inv_ready"], 1)

            def maximum(s, q):
                dve.wait_ge(sem["scored"], s + 1)
                dve.tensor_reduce(minus_max[:, q:q + 1], pair(q)[:, 0:KV], AX_X, ALU.max,
                                  negate=True).then_inc(sem["max_ready"], 1)

            def low_turned(u, b, q):
                use = 5 * u + q
                bank = 4 + (b + q) % 2
                dve.wait_ge(sem["t_high"], use + 1)
                if q < QT:
                    at = slice(q * P, (q + 1) * P)
                    dve.tensor_tensor(turned_low[:, b % 2, 0:QT, at],
                                      k.ps[:, bank, :].rearrange("p (i t) -> p i t", t=P),
                                      turned_high[:, b % 2, 0:QT, at], ALU.subtract).then_inc(sem["t_low"], 1)
                else:
                    dve.tensor_tensor(turned_low[0:C, b % 2, QT, :], k.ps[0:C, bank, :],
                                      turned_high[0:C, b % 2, QT, :], ALU.subtract).then_inc(sem["t_low"], 1)

            def add_output(u, b, first):
                dve.wait_ge(sem["out_done"], u + 1)
                if first:
                    dve.tensor_scalar(k.yT[:, b, :], k.ps[:, 6, :], k.out_bias[:, 0:1], None,
                                      ALU.add).then_inc(sem["added"], 1)
                else:
                    dve.tensor_tensor(k.yT[:, b, :], k.yT[:, b, :], k.ps[:, 6, :],
                                      ALU.add).then_inc(sem["added"], 1)

            def body(h, b, first, last):
                u = 4 * h + b
                some1, some2 = not first or b >= 1, not first or b >= 2
                more = not last or b < B - 1
                nb, nh = (b + 1) % B, h if b < B - 1 else h + 1
                if some1:
                    invert(4 * u - 1, 3, not first or b >= 2)
                maximum(4 * u, 0)
                if some2:
                    add_output(u - 2, (b + 2) % B, first or (isinstance(h, int) and h == 1 and b < 2))
                if some1:
                    low_turned(u - 1, (b + 3) % B, 2)
                if more:
                    low_k(u + 1, nh, nb)
                invert(4 * u, 0, some1)
                maximum(4 * u + 1, 1)
                if some1:
                    low_turned(u - 1, (b + 3) % B, 3)
                    low_turned(u - 1, (b + 3) % B, 4)
                if more:
                    low_q(u + 1, nh, nb)
                invert(4 * u + 1, 1, some1)
                maximum(4 * u + 2, 2)
                low_turned(u, b, 0)
                if more:
                    low_media(u + 1, nh, nb)
                invert(4 * u + 2, 2, some1)
                maximum(4 * u + 3, 3)
                low_turned(u, b, 1)

            low_q(0, 0, 0)
            low_k(0, 0, 0)
            low_media(0, 0, 0)
            for b in range(B):
                body(0, b, True, False)
            for b in range(B):
                body(1, b, False, False)
            with dve.Fori(2, XH - 1) as i:
                for b in range(B):
                    body(i, b, False, False)
            for b in range(B):
                body(XH - 1, b, False, True)
            invert(4 * U - 1, 3, True)
            add_output(U - 2, (U - 2) % B, False)
            for q in (2, 3, 4):
                low_turned(U - 1, B - 1, q)
            add_output(U - 1, B - 1, False)



def xattn1_out(nc, k):
    with ExitStack() as ctx:
        m = Stage(nc, ctx, "f0_", k)
        n = Norm(m, "norm")
        r = Route(m, 32, 6, 8)
        names = ["outT", "x_ready", "in_psum", "x32_ready", "high_ready"]
        sem = {x: m.sem(x) for x in names}
        block = ctx.enter_context(nc.Block())

        @block.gpsimd
        def _(pool):
            m.clear_last(pool)
            for b in range(B):
                norm_rstd(pool, k, n, b)

        @block.vector
        def _(dve):
            for b in range(B):
                at = slice(b * QT, (b + 1) * QT)
                dve.wait_ge(sem["outT"], b + 1)
                dve.tensor_tensor(k.x[:, at, :], k.x[:, at, :],
                                  k.ps[:, b, :].rearrange("p (q d) -> p q d", d=D),
                                  ALU.add).then_inc(sem["x_ready"], 1)
            norm_all(dve, n, k.x, lambda b: dve.wait_ge(sem["x_ready"], b + 1))
            for b in range(B):
                dve.wait_ge(sem["high_ready"], b + 1)
                dve.tensor_tensor(k.x_low[:, b, :], k.xT32[:, b, :], k.x_high[:, b, :],
                                  ALU.subtract).then_inc(k.f_x_ready, 1)
            route_vector(dve, k, r)

        @block.tensor
        def _(pe):
            for b in range(B):
                for q in range(QT):
                    last = pe.transpose(k.ps[:, b, q * P:(q + 1) * P], k.yT[:, b, q * P:(q + 1) * P], k.ident[:, :])
                last.then_inc(sem["outT"], 1)
            for b in range(B):
                pe.wait_ge(n.ready, b + 1)
                pe.wait_ge(sem["x_ready"], b + 1)
                transpose_batch(pe, k, n.out, b, b).then_inc(sem["in_psum"], 1)
            pe.wait_ge(k.w_loaded["f"], 16)
            for b in range(B):
                pe.wait_ge(sem["x32_ready"], b + 1)
                route_tensor_logits(pe, k, r, weight(k, "f_gate"), k.xT32, b, 4 + b)
            pe.wait_ge(r.parts_ready, 1)
            for b in range(B):
                pe.wait_ge(sem["high_ready"], b + 1)
                route_tensor_turn(pe, k, r, b, b)

        @block.scalar
        def _(act):
            for b in range(B):
                act.wait_ge(sem["in_psum"], b + 1)
                act.copy(k.xT32[:, b, :], k.ps[:, b, :]).then_inc(sem["x32_ready"], 1)
                act.copy(k.x_high[:, b, :], k.ps[:, b, :]).then_inc(sem["high_ready"], 1)
            for b in range(B):
                route_scalar_scores(act, k, r, b, 4 + b)
            for b in range(B):
                act.wait_ge(r.turned, b + 1)
                act.copy(k.routeT[0:ROUTE_ROWS, b, :],
                         k.ps[:, b, :].bitcast(BF16)[0:ROUTE_ROWS, 0:S]).then_inc(k.f_route_ready, 1)


def dump_x(nc, k):
    with ExitStack() as ctx:
        m = Stage(nc, ctx, "dump", k)
        stored = m.sem("stored")
        block = ctx.enter_context(nc.Block())

        @block.sync
        def _(sp):
            sp.dma_start(k.out_dram.rearrange("b (q p) d -> p (b q) d", p=P), k.x[:, :, :]).then_inc(stored, 16)
            sp.wait_ge(stored, 16)


def decoder(nc, x, ctx_token, ctxT, side, w, cols, rows, ident, ident16, sel, out, stop_after=99):
    k = Kept()
    k.stage = 0
    k.x_dram, k.ctx_dram, k.ctxT_dram, k.side_dram = x, ctx_token, ctxT, side
    k.w_dram, k.cols_dram, k.rows_dram, k.ident_dram = w, cols, rows, ident
    k.ident16_dram, k.sel_dram, k.out_dram = ident16.bitcast(BF16), sel.bitcast(BF16), out
    k.scratch = nc.dram_tensor("split_scratch", [2, B, PARTS, P, S], BF16).ap()
    with ExitStack() as ctx:
        m = Memory(nc, ctx, "k_")
        k.ps = ctx.enter_context(nc.psum_tensor("banks", [P, 8, S], F32))
        k.x = m.sb("x", [P, T, D])
        k.w = m.sb("w", [P, W_COLS])
        k.cols = m.sb("cols", [P, N_COL])
        k.rows = m.sb("rows", [P, N_ROW])
        k.ident = m.sb("ident", [P, P])
        k.ident16 = m.sb("ident16", [P, P], BF16)
        k.sel = m.sb("sel", [P, 17, D], BF16)
        k.minus_half = m.sb("minus_half", [P, QT])
        k.x_loaded = [m.sem(f"x_loaded{b}") for b in range(B)]
        k.w_loaded = {x: m.sem("w_loaded_" + x) for x in ("ab", "cd", "e", "f")}
        k.small_loaded, k.side_loaded = m.sem("small_loaded"), m.sem("side_loaded")
        k.constants_set, k.passed = m.sem("constants_set"), m.sem("passed")
        k.c_x_ready, k.c_route_ready, k.v_ready = m.sem("c_x_ready"), m.sem("c_route_ready"), m.sem("v_ready")
        k.f_x_ready, k.f_route_ready, k.kv_ready = m.sem("f_x_ready"), m.sem("f_route_ready"), m.sem("kv_ready")
        k.media = m.sb("media", [P, B, D])
        k.media_loaded = m.sem("media_loaded")
        k.d_stored = [m.sem(f"d_stored{b}") for b in range(B)]
        k.d_loaded = m.sem("d_loaded")
        k.a_stored = [m.sem(f"a_stored{b}") for b in range(B)]
        k.a_loaded = [m.sem(f"a_loaded{b}") for b in range(B)]
        with ExitStack() as layer:
            l = Memory(nc, layer, "l0_")
            k.ctxT = l.sb("ctxT", [P, B * C])
            k.ctx_kT = l.sb("ctx_kT", [P, B * C])
            k.ctx_v = l.sb("ctx_v", [P, B, D])
            k.side = l.sb("side", [P, T, C])
            k.vT = l.sb("vT", [P, B, S])
            k.exp_sum = l.sb("exp_sum", [P, B * H, QT])
            with ExitStack() as stacks:
                st = Memory(nc, stacks, "a_")
                k.q_stack = st.sb("q_stack", [P, 2, H, S], BF16)
                k.k_stack = st.sb("k_stack", [P, 2, H, S], BF16)
                attn0_project(nc, k)
                attn0_heads(nc, k)
            k.x_high = l.sb("x_high", [P, B, S], F32R)
            k.x_low = l.sb("x_low", [P, B, S], F32R)
            k.routeT = l.sb("routeT", [P, B, S], BF16)
            with ExitStack() as wide:
                k.xT32 = Memory(nc, wide, "l0_").sb("xT32", [P, B, S])
                attn0_out_xattn0(nc, k)
            if stop_after == 1:
                return dump_x(nc, k)
            moe(nc, k, "c_", "c_gu", "c_down", 9, None, None, False)
        if stop_after == 2:
            return dump_x(nc, k)
        with ExitStack() as layer:
            l = Memory(nc, layer, "l1a_")
            k.exp_sum = l.sb("exp_sum", [P, B * H, QT])
            k.attended = l.sb("attended", [P, B, S])
            with ExitStack() as stacks:
                st = Memory(nc, stacks, "d_")
                k.v_padded = st.sb("v_padded", [P, B, NK // P, 4 * (D + HD)])
                k.q_stack = st.sb("q_stack", [P, 2, H, S], BF16)
                k.k_stack = st.sb("k_stack", [P, 2, H, NK], BF16)
                attn1_project(nc, k)
                attn1_heads(nc, k)
            with ExitStack() as cross:
                e = Memory(nc, cross, "l1b_")
                k.kvT_high = e.sb("kvT_high", [P, B, KV + 1], F32R)
                k.kvT_low = e.sb("kvT_low", [P, B, KV + 1], F32R)
                k.kv_high = e.sb("kv_high", [P, B, KT, D], F32R)
                k.kv_low = e.sb("kv_low", [P, B, KT, D], F32R)
                k.w_vo = weight(k, "e_vT").rearrange("p (h d) -> p h d", h=XH)
                k.out_bias = e.sb("out_bias", [P, 1])
                k.yT = k.attended
                attn1_out_latents(nc, k)
                if stop_after == 3:
                    return dump_x(nc, k)
                xattn1_heads(nc, k)
            k.x_high = l.sb("x_high", [P, B, S], F32R)
            k.x_low = l.sb("x_low", [P, B, S], F32R)
            k.routeT = l.sb("routeT", [P, B, S], BF16)
            with ExitStack() as wide:
                k.xT32 = Memory(nc, wide, "l1_").sb("xT32", [P, B, S])
                xattn1_out(nc, k)
            if stop_after == 4:
                return dump_x(nc, k)
            moe(nc, k, "f_", "f_gu", "f_down", 17, None, None, True)


def pack(i):

    f = {n: np.asarray(a) for n, a in i.items()}

    def pad(a, n, axis):
        shape = list(a.shape)
        shape[axis] = n - a.shape[axis]
        return np.concatenate([a, np.zeros(shape, a.dtype)], axis)

    def pairs_gu(gate, up, shared_gate, shared_up):
        e = gate.shape[0]
        g = gate.reshape(e // 2, 2, D, -1).transpose(2, 0, 1, 3).reshape(D, e // 2, D)
        u = up.reshape(e // 2, 2, D, -1).transpose(2, 0, 1, 3).reshape(D, e // 2, D)
        g = np.concatenate([pad(shared_gate, D, 1)[:, None], g], 1)
        u = np.concatenate([pad(shared_up, D, 1)[:, None], u], 1)
        return np.stack([g, u], 2).reshape(D, -1)

    def pairs_down(down, shared):
        e = down.shape[0]
        d = down.reshape(e // 2, D, D).transpose(1, 0, 2)
        return np.concatenate([pad(shared, D, 0)[:, None], d], 1).reshape(D, -1)

    gu, wkv = f["L1_ffn_experts_gate_up"], f["L1_xattn_Wkv"]
    inner = XH * D
    d_out = f["L1_attn_out_w"].T.reshape(4, 4, HD, D).transpose(1, 0, 2, 3).reshape(D, D)
    w_in = f["L0_attn_w_in"].reshape(H, 3, HD, D).transpose(1, 0, 2, 3)
    b_in = f["L0_attn_b_in"].reshape(H, 3, HD).transpose(1, 0, 2).reshape(-1)
    w = {
        "a_qkv": w_in.reshape(3 * D, D).T, "a_out": f["L0_attn_w_out"].T,
        "b_q": f["L0_xattn_Wq"].T, "b_k": f["L0_xattn_Wk"].T, "b_v": f["L0_xattn_Wv"].T,
        "c_gate": f["L0_ffn_gate_w"].T,
        "c_gu": pairs_gu(f["L0_ffn_w_gate"], f["L0_ffn_w_up"], f["L0_ffn_ws_gate"], f["L0_ffn_ws_up"]),
        "c_down": pairs_down(f["L0_ffn_w_down"], f["L0_ffn_ws_down"]),
        "d_q": f["L1_attn_q_w"].T, "d_k": f["L1_attn_k_w"].T, "d_v": f["L1_attn_v_w"].T, "d_out": d_out,
        "e_q": f["L1_xattn_Wq"], "e_k": wkv[:, 0:inner],
        "e_vT": wkv[:, inner:].reshape(D, XH, D).transpose(2, 1, 0).reshape(D, -1),
        "e_o": f["L1_xattn_Wo"].reshape(XH, D, D).transpose(1, 0, 2).reshape(D, -1),
        "f_gate": f["L1_ffn_gate_weight"].T,
        "f_gu": pairs_gu(gu[:, 0:64].transpose(0, 2, 1), gu[:, 64:].transpose(0, 2, 1),
                         f["L1_ffn_shared_gate_w"].T, f["L1_ffn_shared_up_w"].T),
        "f_down": pairs_down(f["L1_ffn_experts_down"].transpose(0, 2, 1), f["L1_ffn_shared_down_w"].T),
    }
    bkv = f["L1_xattn_bkv"]
    c = {
        "a_bq": b_in[0:D], "a_bk": b_in[D:2 * D], "a_bv": b_in[2 * D:], "b_bq": f["L0_xattn_bq"],
        "b_bk": f["L0_xattn_bk"], "d_bq": f["L1_attn_q_b"], "d_bk": f["L1_attn_k_b"],
        "conv_w": f["L1_attn_conv_w"].reshape(D, 3).T, "conv_b": f["L1_attn_conv_b"],
        "g_lat": f["L1_xattn_gamma_lat"], "b_lat": f["L1_xattn_beta_lat"],
        "g_med": f["L1_xattn_gamma_media"], "b_med": f["L1_xattn_beta_media"], "e_bo": f["L1_xattn_bo"],
        "e_bq": f["L1_xattn_bq"], "e_bk": bkv[0:inner], "e_bv": bkv[inner:],
    }
    r = {
        "a_bo": f["L0_attn_b_out"], "b_bv": f["L0_xattn_bv"], "d_bv": f["L1_attn_v_b"], "d_bo": f["L1_attn_out_b"],
        "g_lat": c["g_lat"], "b_lat": c["b_lat"], "g_med": c["g_med"], "b_med": c["b_med"],
        "e_score": f["L1_ffn_e_score_correction_bias"],
        "betas": np.stack([f["L0_xattn_beta_risk"], f["L0_xattn_beta_prio"], f["L0_xattn_beta_impl"]]),
        "iota": np.arange(32, dtype=np.float32),
    }
    sel = np.zeros((P, 17, D), np.uint16)
    for part in range(PARTS):
        sel[part * SLOT_E + SLOT_E - 1, 0, :] = BF16_ONE
        for e in range(32):
            sel[part * SLOT_E + e, 1 + e // 2, 64 * (e % 2):64 * (e % 2) + 64] = BF16_ONE
    return {
        "x": f["x"], "ctx_token": f["ctx_1024"],
        "ctxT": f["ctx_1024"].transpose(2, 0, 1).reshape(D, B * C), "side": f["fside_BxSxS2_0"],
        "w": np.concatenate([w[n].reshape(D, -1) for n in COLS], 1),
        "cols": np.concatenate([c[n].reshape(-1, D) for n in COL], 0).T,
        "rows": np.concatenate([r[n].reshape(-1) for n in ROW]),
        "ident": np.eye(P, dtype=np.float32), "ident16": np.diag(np.full(P, BF16_ONE, np.uint16)), "sel": sel,
    }


def kernel(**inputs):
    import concourse.bacc as bacc
    from concourse.bass_utils import run_bass_kernel_spmd

    nc = bacc.Bacc("TRN2", target_bir_lowering=False, num_devices=1)
    arrays, args = {}, []
    for name, a in pack(inputs).items():
        a = np.ascontiguousarray(a)
        arrays[f"in_{name}"] = a
        args.append(nc.dram_tensor(f"in_{name}", a.shape, mybir.dt.from_np(a.dtype), kind="ExternalInput").ap())
    args.append(nc.dram_tensor("out", (B, S, D), F32, kind="ExternalOutput").ap())
    decoder(nc, *args)
    return run_bass_kernel_spmd(nc, [arrays], core_ids=[0]).results[0]["out"]
```

```python
from contextlib import ExitStack

import numpy as np

import concourse.bass as bass
from concourse import mybir

F32 = mybir.dt.float32
F32R = mybir.dt.float32r
BF16 = mybir.dt.bfloat16
U32 = mybir.dt.uint32
ACT = mybir.ActivationFunctionType
ALU = mybir.AluOpType
AX_X = mybir.AxisListType.X

P = 128
B = 4
S = 512
D = 128
QT = S // P
T = B * QT
C = 77
H = 16
HD = D // H
XH = 8
NK = S // 2
KV = S + C
KT = KV // P + 1
EPS = 1e-5
BF16_ONE = 0x3F80
PARTS = 3
TERMS_Q = [0, 0, 0, 1, 1, 2]
TERMS_K = [0, 1, 2, 0, 1, 0]
KROWS = 96
SLOT_E = 33
ROUTE_ROWS = PARTS * SLOT_E

COLS = {}
_n = 0
for _name, _w in [("a_qkv", 3 * D), ("a_out", D), ("b_q", D), ("b_k", D), ("b_v", D), ("c_gate", 16),
                  ("c_gu", 9 * 2 * D), ("c_down", 9 * D), ("d_q", D), ("d_k", D), ("d_v", D), ("d_out", D),
                  ("e_q", XH * D), ("e_k", XH * D), ("e_vT", XH * D), ("e_o", XH * D), ("f_gate", 32),
                  ("f_gu", 17 * 2 * D), ("f_down", 17 * D)]:
    COLS[_name] = (_n, _n + _w)
    _n += _w
W_COLS = _n
COL = {}
for _name, _w in [("a_bq", 1), ("a_bk", 1), ("a_bv", 1), ("b_bq", 1), ("b_bk", 1), ("d_bq", 1), ("d_bk", 1),
                  ("conv_w", 3), ("conv_b", 1), ("g_lat", 1), ("b_lat", 1), ("g_med", 1), ("b_med", 1),
                  ("e_bo", 1), ("e_bq", XH), ("e_bk", XH), ("e_bv", XH)]:
    COL[_name] = (sum(w for _, w in COL.values()), _w)
N_COL = sum(w for _, w in COL.values())
ROW = {}
for _name, _w in [("a_bo", D), ("b_bv", D), ("d_bv", D), ("d_bo", D), ("g_lat", D), ("b_lat", D),
                  ("g_med", D), ("b_med", D), ("e_score", 32), ("betas", 3), ("iota", 32)]:
    ROW[_name] = (sum(w for _, w in ROW.values()), _w)
N_ROW = sum(w for _, w in ROW.values())


class Memory:

    def __init__(self, nc, ctx, prefix):
        self.nc, self.ctx, self.prefix = nc, ctx, prefix

    def sb(self, name, shape, dt=F32):
        return self.ctx.enter_context(self.nc.sbuf_tensor(self.prefix + name, shape, dt))

    def sem(self, name):
        return self.ctx.enter_context(self.nc.semaphore(self.prefix + name))


STAGE_SEMS = 55
SEM_SETS = [range(256 - 2 * STAGE_SEMS, 256 - STAGE_SEMS), range(256 - STAGE_SEMS, 256)]


class Stage(Memory):

    def __init__(self, nc, ctx, prefix, k):
        super().__init__(nc, ctx, prefix)
        self.ids = iter(SEM_SETS[k.stage % 2])
        self.last_set = SEM_SETS[(k.stage + 1) % 2] if k.stage else None
        k.stage += 1

    def sem(self, name):
        return self.ctx.enter_context(self.nc.semaphore(self.prefix + name, next(self.ids)))

    def clear_last(self, pool):
        if self.last_set:
            pool.sem_clear(self.last_set)


class Kept:
    pass


def wait_apart(eng, k, sem, value):
    eng.wait_ge(sem, value)
    eng.sem_inc(k.passed, 1)


def col(k, name, i=0, rows=P):
    at = COL[name][0] + i
    return k.cols[0:rows, at:at + 1]


def row(k, name, rows=P):
    at, w = ROW[name]
    return k.rows[0:rows, at:at + w]


def weight(k, name):
    a, b = COLS[name]
    return k.w[:, a:b]



class Norm:

    def __init__(self, m, name, batches=B, tiles=QT, rows=P):
        self.tiles, self.rows = tiles, rows
        n = batches * tiles
        self.stats = m.sb(name + "_stats", [P, n, 6])
        self.mv = m.sb(name + "_mean_var", [P, n, 2])
        self.var_eps = m.sb(name + "_var_eps", [P, n])
        self.rstd = m.sb(name + "_rstd", [P, n])
        self.out = m.sb(name + "_normed", [P, n, D])
        self.stats_done = m.sem(name + "_stats_done")
        self.aggregated = m.sem(name + "_aggregated")
        self.var_ready = m.sem(name + "_var_ready")
        self.rstd_ready = m.sem(name + "_rstd_ready")
        self.ready = m.sem(name + "_ready")


def norm_statistics(dve, n, x, b):
    r, tiles = n.rows, range(b * n.tiles, (b + 1) * n.tiles)
    for t in tiles:
        last = dve.bn_stats(n.stats[0:r, t, :], x[0:r, t, :])
    last.then_inc(n.stats_done, 1)
    dve.wait_ge(n.stats_done, b + 1)
    for t in tiles:
        last = dve.bn_aggr(n.mv[0:r, t, :], n.stats[0:r, t, :])
    last.then_inc(n.aggregated, 1)
    dve.wait_ge(n.aggregated, b + 1)
    at = slice(b * n.tiles, (b + 1) * n.tiles)
    dve.tensor_scalar(n.var_eps[0:r, at], n.mv[0:r, at, 1], EPS, None, ALU.add).then_inc(n.var_ready, 1)


def norm_rstd(pool, k, n, b):
    r, at = n.rows, slice(b * n.tiles, (b + 1) * n.tiles)
    pool.wait_ge(n.var_ready, b + 1)
    pool.tensor_tensor(n.rstd[0:r, at], n.var_eps[0:r, at], k.minus_half[0:r, 0:n.tiles],
                       ALU.pow).then_inc(n.rstd_ready, 1)


def norm_apply(dve, n, x, b):
    r = n.rows
    dve.wait_ge(n.rstd_ready, b + 1)
    for t in range(b * n.tiles, (b + 1) * n.tiles):
        last = dve.tensor_scalar(n.out[0:r, t, :], x[0:r, t, :], n.mv[0:r, t, 0:1], n.rstd[0:r, t:t + 1],
                                 ALU.subtract, ALU.mult)
    last.then_inc(n.ready, 1)


def norm_all(dve, n, x, waits=None):
    for b in range(B):
        if waits:
            waits(b)
        norm_statistics(dve, n, x, b)
    for b in range(B):
        norm_apply(dve, n, x, b)


def transpose_batch(pe, k, src, b, bank):
    for q in range(QT):
        last = pe.transpose(k.ps[:, bank, q * P:(q + 1) * P], src[:, b * QT + q, :], k.ident[:, :])
    return last



RING = 4
PARTS_RING = 6


class Split:

    def __init__(self, m):
        self.full = m.sb("split_full", [P, RING, S])
        self.rest = m.sb("split_rest", [P, RING, S])
        self.parts = m.sb("split_parts", [P, PARTS_RING, PARTS, S], BF16)
        self.full_ready = m.sem("split_full_ready")
        self.high_ready = m.sem("split_high_ready")
        self.rest_ready = m.sem("split_rest_ready")
        self.mid_ready = m.sem("split_mid_ready")
        self.low_ready = m.sem("split_low_ready")


def split_scalar(act, s, widths, stored):
    for i in range(2 * B + 1):
        if i < 2 * B:
            w = widths[i % 2]
            act.wait_ge(s.full_ready, i + 1)
            if i >= PARTS_RING:
                act.wait_ge(stored[(i - PARTS_RING) // 2], 32)
            act.copy(s.parts[:, i % PARTS_RING, 0, 0:w], s.full[:, i % RING, 0:w]).then_inc(s.high_ready, 1)
        if i >= 1:
            j, w = i - 1, widths[(i - 1) % 2]
            act.wait_ge(s.rest_ready, j + 1)
            act.copy(s.parts[:, j % PARTS_RING, 1, 0:w], s.rest[:, j % RING, 0:w]).then_inc(s.mid_ready, 1)


def split_vector(dve, s, widths, make_full):
    for i in range(2 * B + 3):
        if i < 2 * B:
            if i >= RING:
                dve.wait_ge(s.rest_ready, i - RING + 1)
            make_full(i, s.full[:, i % RING, 0:widths[i % 2]]).then_inc(s.full_ready, 1)
        if 1 <= i <= 2 * B:
            j, w = i - 1, widths[(i - 1) % 2]
            dve.wait_ge(s.high_ready, j + 1)
            if j >= RING:
                dve.wait_ge(s.low_ready, j - RING + 1)
            dve.tensor_tensor(s.rest[:, j % RING, 0:w], s.full[:, j % RING, 0:w], s.parts[:, j % PARTS_RING, 0, 0:w],
                              ALU.subtract).then_inc(s.rest_ready, 1)
        if i >= 3:
            j, w = i - 3, widths[(i - 3) % 2]
            dve.wait_ge(s.mid_ready, j + 1)
            dve.tensor_tensor(s.parts[:, j % PARTS_RING, 2, 0:w], s.rest[:, j % RING, 0:w], s.parts[:, j % PARTS_RING, 1, 0:w],
                              ALU.subtract).then_inc(s.low_ready, 1)


def store_parts(sp, k, s, b, widths, stored):
    for i in (0, 1):
        sp.wait_ge(s.low_ready, 2 * b + i + 1)
        w = widths[i]
        sp.dma_start(k.scratch[i, b, :, :, 0:w].rearrange("c p t -> p c t"),
                     s.parts[:, (2 * b + i) % PARTS_RING, :, 0:w]).then_inc(stored[b], 16)


def load_stacks(sp, k, b, widths, stored, signal):
    sp.wait_ge(stored[b], 32)
    for term in range(len(TERMS_Q)):
        at = slice(HD * term, HD * (term + 1))
        for i, (stack, parts) in enumerate(((k.q_stack, TERMS_Q), (k.k_stack, TERMS_K))):
            w = widths[i]
            sp.dma_start(stack[at, b % 2, :, 0:w],
                         k.scratch[i, b, parts[term], :, 0:w].rearrange("(h d) t -> d h t", d=HD)
                         ).then_inc(signal, 16)


STACK_LOADED = 16 * 2 * len(TERMS_Q)



def load_weights(sp, k, name, lo, hi):
    sp.dma_start(k.w[:, lo:hi], k.w_dram[:, lo:hi]).then_inc(k.w_loaded[name], 16)


def attn0_project(nc, k):
    with ExitStack() as ctx:
        m = Stage(nc, ctx, "a_", k)
        n = Norm(m, "norm")
        s = Split(m)
        xT = n.out[:, :, :].rearrange("p (b q) d -> p b (q d)", b=B)
        in_psum, xT_ready = m.sem("x_in_psum"), m.sem("xT_ready")
        q_done, k_done, v_done = m.sem("q_done"), m.sem("k_done"), m.sem("v_done")
        ctx_done, ctx_copied, zeroed = m.sem("ctx_done"), m.sem("ctx_copied"), m.sem("zeroed")
        block = ctx.enter_context(nc.Block())
        scale = float(HD) ** -0.5
        wa = weight(k, "a_qkv")

        @block.sync
        def _(sp):
            x_dram = k.x_dram.rearrange("b (q p) d -> p (b q) d", p=P)
            for b in range(B):
                sp.dma_start(k.x[:, b * QT:(b + 1) * QT, :], x_dram[:, b * QT:(b + 1) * QT, :]
                             ).then_inc(k.x_loaded[b], 16)
            sp.dma_start(k.ident[:, :], k.ident_dram).then_inc(k.small_loaded, 16)
            sp.dma_start(k.cols[:, :], k.cols_dram).then_inc(k.small_loaded, 16)
            sp.dma_start(k.rows[:, :], k.rows_dram.partition_broadcast(P)).then_inc(k.small_loaded, 16)
            sp.dma_start(k.ctxT[:, :], k.ctxT_dram).then_inc(k.small_loaded, 16)
            load_weights(sp, k, "ab", 0, COLS["c_gate"][0])
            for b in range(B):
                store_parts(sp, k, s, b, (S, S), k.a_stored)
                if b == 0:
                    sp.wait_ge(zeroed, 2)
                    load_stacks(sp, k, 0, (S, S), k.a_stored, k.a_loaded[0])

        @block.gpsimd
        def _(pool):
            m.clear_last(pool)
            pool.memset(k.minus_half[:, :], -0.5).then_inc(k.constants_set, 1)
            pool.wait_ge(k.constants_set, 1)
            for b in range(B):
                norm_rstd(pool, k, n, b)
            for b in range(2):
                pool.memset(k.q_stack[0:KROWS, b, :, :].bitcast(F32), 0.0).then_inc(zeroed, 1)
                pool.memset(k.k_stack[0:KROWS, b, :, :].bitcast(F32), 0.0).then_inc(zeroed, 1)

        @block.vector
        def _(dve):
            for i in range(B + 1):
                if i < B:
                    dve.wait_ge(k.x_loaded[i], 16)
                    norm_statistics(dve, n, k.x, i)
                if i >= 1:
                    norm_apply(dve, n, k.x, i - 1)
            dve.wait_ge(ctx_done, 2)
            dve.tensor_tensor(k.ctx_v[0:C, :, :], k.ps[0:C, 7, :].rearrange("c (b d) -> c b d", b=B),
                              row(k, "b_bv", C).unsqueeze(1).broadcast_to([C, B, D]),
                              ALU.add).then_inc(ctx_copied, 1)

            def full(i, out):
                b = i // 2
                if i % 2 == 0:
                    dve.wait_ge(q_done, b + 1)
                    return dve.tensor_scalar(out, k.ps[:, 4 + b, :], col(k, "a_bq"), scale,
                                             ALU.add, ALU.mult)
                dve.wait_ge(k_done, b + 1)
                return dve.tensor_scalar(out, k.ps[:, b, :], col(k, "a_bk"), None, ALU.add)

            split_vector(dve, s, (S, S), full)

        @block.tensor
        def _(pe):
            pe.wait_ge(k.small_loaded, 64)
            pe.wait_ge(k.w_loaded["ab"], 16)
            pe.matmul(k.ps[:, 6, 0:B * C], weight(k, "b_k"), k.ctxT[:, :], start=True,
                      stop=True).then_inc(ctx_done, 1)
            for b in range(B):
                last = pe.matmul(k.ps[0:C, 7, b * D:(b + 1) * D], k.ctxT[:, b * C:(b + 1) * C],
                                 weight(k, "b_v"), start=True, stop=True)
            last.then_inc(ctx_done, 1)
            for i in range(B + 1):
                if i < B:
                    pe.wait_ge(n.ready, i + 1)
                    transpose_batch(pe, k, n.out, i, i).then_inc(in_psum, 1)
                if i == 0:
                    continue
                b = i - 1
                if b == 2:
                    pe.wait_ge(ctx_copied, 2)
                pe.wait_ge(xT_ready, b + 1)
                pe.matmul(k.ps[:, 4 + b, :], wa[:, 0:D], xT[:, b, :], start=True, stop=True).then_inc(q_done, 1)
                pe.matmul(k.ps[:, b, :], wa[:, D:2 * D], xT[:, b, :], start=True, stop=True).then_inc(k_done, 1)
            for b in range(B):
                pe.wait_ge(s.full_ready, 2 * b + 1)
                pe.matmul(k.ps[:, 4 + b, :], wa[:, 2 * D:3 * D], xT[:, b, :], start=True,
                          stop=True).then_inc(v_done, 1)

        @block.scalar
        def _(act):
            act.wait_ge(ctx_done, 1)
            act.activation(k.ctx_kT[:, :], k.ps[:, 6, 0:B * C], ACT.Identity,
                           bias=col(k, "b_bk")).then_inc(ctx_copied, 1)
            for b in range(B):
                act.wait_ge(in_psum, b + 1)
                act.copy(xT[:, b, :], k.ps[:, b, :]).then_inc(xT_ready, 1)
            split_scalar(act, s, (S, S), k.a_stored)
            for b in range(B):
                act.wait_ge(v_done, b + 1)
                act.activation(k.vT[:, b, :], k.ps[:, 4 + b, :], ACT.Identity,
                               bias=col(k, "a_bv")).then_inc(k.v_ready, 1)



def attn0_heads(nc, k):
    with ExitStack() as ctx:
        m = Stage(nc, ctx, "ah_", k)
        minus_max = m.sb("minus_max", [P, B * H, QT])
        scored, max_ready, slots_free = m.sem("scored"), m.sem("max_ready"), m.sem("slots_free")
        stack_used = m.sem("stack_used")
        block = ctx.enter_context(nc.Block())
        PAIRS = H // 2

        @block.gpsimd
        def _(pool):
            m.clear_last(pool)

        @block.sync
        def _(sp):
            load_stacks(sp, k, 1, (S, S), k.a_stored, k.a_loaded[1])
            sp.dma_start(k.side[:, :, :], k.side_dram.rearrange("b (q p) c -> p (b q) c", p=P)
                         ).then_inc(k.side_loaded, 16)
            sp.dma_start(k.sel[:, :, :], k.sel_dram).then_inc(k.side_loaded, 16)
            sp.dma_start(k.ident16[:, :], k.ident16_dram).then_inc(k.side_loaded, 16)
            sp.dma_start(k.media[0:C, :, :], k.ctx_dram.rearrange("b c d -> c b d")
                         ).then_inc(k.media_loaded, 16)
            load_weights(sp, k, "cd", COLS["c_gate"][0], COLS["e_q"][0])
            load_weights(sp, k, "e", COLS["e_q"][0], COLS["f_gate"][0])
            load_weights(sp, k, "f", COLS["f_gate"][0], W_COLS)
            for b in range(2, B):
                sp.wait_ge(stack_used, b - 1)
                load_stacks(sp, k, b, (S, S), k.a_stored, k.a_loaded[b])

        @block.tensor
        def _(pe):
            for b in range(B):
                pe.wait_ge(k.a_loaded[b], STACK_LOADED)
                with pe.Fori(0, PAIRS) as pair:
                    for i in range(4):
                        half = (b * PAIRS + pair) * 4 + i
                        head = pair * 2 + i // 2
                        pe.wait_ge(slots_free, half + 1)
                        for j in range(2):
                            q = 2 * (i % 2) + j
                            last = pe.matmul(k.ps[:, 2 * i + j, :],
                                             k.q_stack[0:KROWS, b % 2, bass.ds(head, 1), q * P:(q + 1) * P]
                                             .rearrange("p a t -> p (a t)"),
                                             k.k_stack[0:KROWS, b % 2, bass.ds(head, 1), :]
                                             .rearrange("p a t -> p (a t)"),
                                             start=True, stop=True)
                        last.then_inc(scored, 1)
                pe.wait_ge(scored, (b + 1) * PAIRS * 4)
                pe.sem_inc(stack_used, 1)

        @block.vector
        def _(dve):
            with dve.Fori(0, B * PAIRS) as pair:
                for i in range(4):
                    dve.wait_ge(scored, pair * 4 + i + 1)
                    dve.tensor_reduce(minus_max[:, bass.ds(pair * 2 + i // 2, 1), 2 * (i % 2):2 * (i % 2) + 2]
                                      .rearrange("p a q -> p (a q)"),
                                      k.ps[:, 2 * i:2 * i + 2, :], AX_X, ALU.max,
                                      negate=True).then_inc(max_ready, 1)

        @block.scalar
        def _(act):
            act.sem_inc(slots_free, 4)
            with act.Fori(0, B * PAIRS) as pair:
                for i in range(4):
                    head = pair * 2 + i // 2
                    wait_apart(act, k, max_ready, pair * 4 + i + 1)
                    for j in range(2):
                        q = 2 * (i % 2) + j
                        last = act.activation(k.ps[:, 2 * i + j, :], k.ps[:, 2 * i + j, :], ACT.Exp,
                                              bias=minus_max[:, bass.ds(head, 1), q:q + 1]
                                              .rearrange("p a q -> p (a q)"),
                                              accum_out=k.exp_sum[:, bass.ds(head, 1), q:q + 1]
                                              .rearrange("p a q -> p (a q)"))
                    last.then_inc(slots_free, 1)



class Route:
    def __init__(self, m, experts, top, groups=0):
        self.experts, self.top, self.groups = experts, top, groups
        e = experts
        self.logits_ready = m.sem("logits_ready")
        self.scores_ready = m.sem("route_scores_ready")
        self.step = m.sem("route_step")
        self.parts_ready = m.sem("route_parts_ready")
        self.turned = m.sem("route_turned")
        self.scores = m.sb("route_scores", [P, T, e])
        self.ranked = m.sb("ranked", [P, T, e])
        self.best = m.sb("best", [P, T, 8])
        self.best_at = m.sb("best_at", [P, T, 8], U32)
        self.best_at_f = m.sb("best_at_f", [P, T, 8])
        self.hits = m.sb("hits", [P, T, e, top])
        self.mask = m.sb("mask", [P, T, e])
        self.chosen = m.sb("chosen", [P, T, e])
        self.total = m.sb("total", [P, T])
        self.inverse = m.sb("route_inverse", [P, T])
        self.route = m.sb("route", [P, T, SLOT_E])
        self.rest = m.sb("route_rest", [P, T, SLOT_E])
        self.parts = m.sb("route_parts", [P, T, PARTS, SLOT_E], BF16)
        if groups:
            self.group_score = m.sb("group_score", [P, T, groups])
            self.group_hits = m.sb("group_hits", [P, T, groups, groups // 2])
            self.group_mask = m.sb("group_mask", [P, T, groups])


def route_vector(dve, k, r):
    e, top = r.experts, r.top
    SCALE = 2.5
    done = [0]

    def step(last):
        done[0] += 1
        last.then_inc(r.step, 1)
        dve.wait_ge(r.step, done[0])

    def top_mask(values, n, count, hits, mask):
        for t in range(T):
            last = dve.max(r.best[:, t, :], values[:, t, :])
        step(last)
        for t in range(T):
            last = dve.max_index(r.best_at[:, t, :], r.best[:, t, :], values[:, t, :])
        step(last)
        step(dve.tensor_copy(r.best_at_f[:, :, :], r.best_at[:, :, :]))
        for b in range(B):
            at = slice(b * QT, (b + 1) * QT)
            last = dve.tensor_tensor(
                hits[:, at, :, :],
                row(k, "iota")[:, 0:n].unsqueeze(1).unsqueeze(3).broadcast_to([P, QT, n, count]),
                r.best_at_f[:, at, 0:count].unsqueeze(2).broadcast_to([P, QT, n, count]), ALU.is_equal)
        step(last)
        step(dve.tensor_reduce(mask[:, :, :], hits[:, :, :, :], AX_X, ALU.add))

    step(dve.memset(r.route[:, :, :], 0.0))
    step(dve.memset(r.route[:, :, SLOT_E - 1:SLOT_E], 1.0))
    dve.wait_ge(r.scores_ready, B)
    values = r.scores
    if r.groups:
        size = e // r.groups
        step(dve.tensor_tensor(r.ranked[:, :, :], r.scores[:, :, :],
                               row(k, "e_score").unsqueeze(1).broadcast_to([P, T, e]), ALU.add))
        step(dve.tensor_reduce(r.group_score[:, :, :],
                               r.ranked[:, :, :].rearrange("p t (g s) -> p t g s", s=size), AX_X, ALU.max))
        top_mask(r.group_score, r.groups, r.groups // 2, r.group_hits, r.group_mask)
        step(dve.tensor_tensor(r.ranked[:, :, :].rearrange("p t (g s) -> p t g s", s=size),
                               r.ranked[:, :, :].rearrange("p t (g s) -> p t g s", s=size),
                               r.group_mask[:, :, :].unsqueeze(3).broadcast_to([P, T, r.groups, size]), ALU.mult))
        values = r.ranked
    top_mask(values, e, top, r.hits, r.mask)
    step(dve.tensor_tensor(r.chosen[:, :, :], r.mask[:, :, :], r.scores[:, :, :], ALU.mult))
    step(dve.tensor_reduce(r.total[:, :], r.chosen[:, :, :], AX_X, ALU.add))
    step(dve.tensor_scalar(r.total[:, :], r.total[:, :], 1e-20, None, ALU.add))
    step(dve.reciprocal(r.inverse[:, :], r.total[:, :]))
    step(dve.scalar_tensor_tensor(r.route[:, :, 0:e], r.chosen[:, :, :], SCALE,
                                  r.inverse[:, :].unsqueeze(2).broadcast_to([P, T, e]), ALU.mult, ALU.mult))
    step(dve.tensor_copy(r.parts[:, :, 0, :], r.route[:, :, :]))
    step(dve.tensor_tensor(r.rest[:, :, :], r.route[:, :, :], r.parts[:, :, 0, :], ALU.subtract))
    step(dve.tensor_copy(r.parts[:, :, 1, :], r.rest[:, :, :]))
    dve.tensor_tensor(r.parts[:, :, 2, :], r.rest[:, :, :], r.parts[:, :, 1, :],
                      ALU.subtract).then_inc(r.parts_ready, 1)


def route_tensor_logits(pe, k, r, gate, xT, b, bank):
    for q in range(QT):
        last = pe.matmul(k.ps[:, bank, q * r.experts:(q + 1) * r.experts], xT[:, b, q * P:(q + 1) * P],
                         gate, start=True, stop=True)
    last.then_inc(r.logits_ready, 1)


def route_scalar_scores(act, k, r, b, bank):
    act.wait_ge(r.logits_ready, b + 1)
    act.activation(r.scores[:, b * QT:(b + 1) * QT, :],
                   k.ps[:, bank, 0:QT * r.experts].rearrange("p (q e) -> p q e", q=QT),
                   ACT.Sigmoid).then_inc(r.scores_ready, 1)


def route_tensor_turn(pe, k, r, b, bank):
    out = k.ps[:, bank, :].bitcast(BF16)
    for q in range(QT):
        last = pe.transpose(out[0:ROUTE_ROWS, q * P:(q + 1) * P],
                            r.parts[:, b * QT + q, :, :].rearrange("p c e -> p (c e)"), k.ident16[:, :])
    last.then_inc(r.turned, 1)



def attn0_out_xattn0(nc, k):
    with ExitStack() as ctx:
        m = Stage(nc, ctx, "b_", k)
        n, n2 = Norm(m, "norm"), Norm(m, "norm2")
        r = Route(m, 16, 2)
        inverse = m.sb("inverse", [P, B * H, QT])
        weight_sum = m.sb("weight_sum", [P, B * H, QT])
        wide = m.sb("wide", [P, T, D])
        attnT = wide[:, :, :].rearrange("p (b q) d -> p b (q d)", b=B)
        xT = n.out[:, :, :].rearrange("p (b q) d -> p b (q d)", b=B)
        qT = m.sb("qT", [P, B, S])
        scores = m.sb("x_scores", [P, T, C])
        minus_max = m.sb("minus_max", [P, T])
        probs = m.sb("probs", [P, T, C])
        exp_sum = m.sb("exp_sum", [P, T])
        x_inverse = m.sb("x_inverse", [P, T])
        probsT = m.sb("probsT", [P, B, S])
        beta = m.sb("beta", [P, 2])
        names = ["inv_ready", "sum_ready", "wide_ready", "sumT", "attn_ready", "projected", "x_ready", "biased",
                 "in_psum", "xT_ready", "q_done", "q_ready", "scored", "beta_ready", "scores_ready", "max_ready",
                 "exp_done", "probsT_done", "probsT_ready", "x_inv_ready", "attended", "x2_ready",
                 "in_psum2", "high_ready", "x32_ready"]
        sem = {x: m.sem(x) for x in names}
        block = ctx.enter_context(nc.Block())
        scale = float(D) ** -0.5

        @block.gpsimd
        def _(pool):
            m.clear_last(pool)
            for b in range(B):
                at = slice(b * QT, (b + 1) * QT)
                pool.tensor_tensor(k.x[:, at, :], k.x[:, at, :],
                                   row(k, "a_bo").unsqueeze(1).broadcast_to([P, QT, D]),
                                   ALU.add).then_inc(sem["biased"], 1)
            for b in range(B):
                norm_rstd(pool, k, n, b)
            for b in range(B):
                norm_rstd(pool, k, n2, b)

        @block.vector
        def _(dve):
            at = ROW["betas"][0]
            dve.tensor_tensor(beta[:, 0:1], k.rows[:, at:at + 1], k.rows[:, at + 1:at + 2],
                              ALU.add).then_inc(sem["beta_ready"], 1)
            dve.reciprocal(inverse[:, :, :], k.exp_sum[:, :, :]).then_inc(sem["inv_ready"], 1)
            dve.wait_ge(sem["beta_ready"], 1)
            dve.tensor_tensor(beta[:, 1:2], beta[:, 0:1], k.rows[:, at + 2:at + 3],
                              ALU.subtract).then_inc(sem["beta_ready"], 1)
            dve.wait_ge(sem["inv_ready"], 1)
            dve.tensor_tensor(weight_sum[:, :, :], k.exp_sum[:, :, :], inverse[:, :, :],
                              ALU.mult).then_inc(sem["sum_ready"], 1)
            dve.wait_ge(sem["sum_ready"], 1)
            for b in range(B):
                dve.tensor_copy(wide[:, b * QT:(b + 1) * QT, :].rearrange("p q (h d) -> p q h d", d=HD),
                                weight_sum[:, b * H:(b + 1) * H, :].rearrange("p h q -> p q h").unsqueeze(3)
                                .broadcast_to([P, QT, H, HD])).then_inc(sem["wide_ready"], 1)
            for b in range(B):
                dve.wait_ge(sem["sumT"], b + 1)
                dve.tensor_tensor(attnT[:, b, :], k.vT[:, b, :], k.ps[:, b, :],
                                  ALU.mult).then_inc(sem["attn_ready"], 1)
            for b in range(B):
                at = slice(b * QT, (b + 1) * QT)
                dve.wait_ge(sem["projected"], b + 1)
                dve.wait_ge(sem["biased"], b + 1)
                dve.tensor_tensor(k.x[:, at, :], k.x[:, at, :],
                                  k.ps[:, 4 + b, :].rearrange("p (q d) -> p q d", d=D),
                                  ALU.add).then_inc(sem["x_ready"], 1)
            norm_all(dve, n, k.x, lambda b: dve.wait_ge(sem["x_ready"], b + 1))
            for b in range(B):
                dve.wait_ge(sem["q_done"], b + 1)
                dve.tensor_scalar(qT[:, b, :], k.ps[:, 4 + b, :], col(k, "b_bq"), scale, ALU.add,
                                  ALU.mult).then_inc(sem["q_ready"], 1)
            dve.wait_ge(k.side_loaded, 48)
            dve.wait_ge(sem["beta_ready"], 2)
            for b in range(B):
                at = slice(b * QT, (b + 1) * QT)
                dve.wait_ge(sem["scored"], b + 1)
                dve.scalar_tensor_tensor(scores[:, at, :], k.side[:, at, :], beta[:, 1:2],
                                         k.ps[:, b, 0:QT * C].rearrange("p (q c) -> p q c", q=QT),
                                         ALU.mult, ALU.add).then_inc(sem["scores_ready"], 1)
                dve.wait_ge(sem["scores_ready"], b + 1)
                dve.tensor_reduce(minus_max[:, at], scores[:, at, :], AX_X, ALU.max,
                                  negate=True).then_inc(sem["max_ready"], 1)
            for b in range(B):
                at = slice(b * QT, (b + 1) * QT)
                dve.wait_ge(sem["exp_done"], b + 1)
                dve.reciprocal(x_inverse[:, at], exp_sum[:, at]).then_inc(sem["x_inv_ready"], 1)
            for b in range(B):
                dve.wait_ge(sem["attended"], b + 1)
                dve.wait_ge(sem["x_inv_ready"], b + 1)
                for q in range(QT):
                    t = b * QT + q
                    last = dve.scalar_tensor_tensor(k.x[:, t, :], k.ps[:, b, q * D:(q + 1) * D],
                                                    x_inverse[:, t:t + 1], k.x[:, t, :], ALU.mult, ALU.add)
                last.then_inc(sem["x2_ready"], 1)
            norm_all(dve, n2, k.x, lambda b: dve.wait_ge(sem["x2_ready"], b + 1))
            for b in range(B):
                dve.wait_ge(sem["high_ready"], b + 1)
                dve.tensor_tensor(k.x_low[:, b, :], k.xT32[:, b, :], k.x_high[:, b, :],
                                  ALU.subtract).then_inc(k.c_x_ready, 1)
            route_vector(dve, k, r)

        @block.tensor
        def _(pe):
            for b in range(B):
                pe.wait_ge(sem["wide_ready"], b + 1)
                transpose_batch(pe, k, wide, b, b).then_inc(sem["sumT"], 1)
            for b in range(B):
                pe.wait_ge(sem["attn_ready"], b + 1)
                for q in range(QT):
                    last = pe.matmul(k.ps[:, 4 + b, q * D:(q + 1) * D], attnT[:, b, q * P:(q + 1) * P],
                                     weight(k, "a_out"), start=True, stop=True)
                last.then_inc(sem["projected"], 1)
            for b in range(B):
                pe.wait_ge(n.ready, b + 1)
                transpose_batch(pe, k, n.out, b, b).then_inc(sem["in_psum"], 1)
            for b in range(B):
                pe.wait_ge(sem["xT_ready"], b + 1)
                pe.wait_ge(sem["x_ready"], b + 1)
                pe.matmul(k.ps[:, 4 + b, :], weight(k, "b_q"), xT[:, b, :], start=True,
                          stop=True).then_inc(sem["q_done"], 1)
            for b in range(B):
                pe.wait_ge(sem["q_ready"], b + 1)
                for q in range(QT):
                    last = pe.matmul(k.ps[:, b, q * C:(q + 1) * C], qT[:, b, q * P:(q + 1) * P],
                                     k.ctx_kT[:, b * C:(b + 1) * C], start=True, stop=True)
                last.then_inc(sem["scored"], 1)
            for b in range(B):
                pe.wait_ge(sem["exp_done"], b + 1)
                for q in range(QT):
                    last = pe.transpose(k.ps[0:C, 4 + b, q * P:(q + 1) * P], probs[:, b * QT + q, :], k.ident[:, :])
                last.then_inc(sem["probsT_done"], 1)
            for b in range(B):
                pe.wait_ge(sem["probsT_ready"], b + 1)
                for q in range(QT):
                    last = pe.matmul(k.ps[:, b, q * D:(q + 1) * D], probsT[0:C, b, q * P:(q + 1) * P],
                                     k.ctx_v[0:C, b, :], start=True, stop=True)
                last.then_inc(sem["attended"], 1)
            for b in range(B):
                pe.wait_ge(n2.ready, b + 1)
                transpose_batch(pe, k, n2.out, b, b).then_inc(sem["in_psum2"], 1)
            pe.wait_ge(k.w_loaded["cd"], 16)
            for b in range(B):
                pe.wait_ge(sem["x32_ready"], b + 1)
                route_tensor_logits(pe, k, r, weight(k, "c_gate"), k.xT32, b, 4 + b)
            pe.wait_ge(r.parts_ready, 1)
            for b in range(B):
                pe.wait_ge(sem["high_ready"], b + 1)
                route_tensor_turn(pe, k, r, b, b)

        @block.scalar
        def _(act):
            for b in range(B):
                act.wait_ge(sem["in_psum"], b + 1)
                act.copy(xT[:, b, :], k.ps[:, b, :]).then_inc(sem["xT_ready"], 1)
            for b in range(B):
                act.wait_ge(sem["max_ready"], b + 1)
                for q in range(QT):
                    t = b * QT + q
                    last = act.activation(probs[:, t, :], scores[:, t, :], ACT.Exp, bias=minus_max[:, t:t + 1],
                                          accum_out=exp_sum[:, t:t + 1])
                last.then_inc(sem["exp_done"], 1)
            for b in range(B):
                act.wait_ge(sem["probsT_done"], b + 1)
                act.copy(probsT[0:C, b, :], k.ps[0:C, 4 + b, :]).then_inc(sem["probsT_ready"], 1)
            for b in range(B):
                act.wait_ge(sem["in_psum2"], b + 1)
                act.copy(k.xT32[:, b, :], k.ps[:, b, :]).then_inc(sem["x32_ready"], 1)
                act.copy(k.x_high[:, b, :], k.ps[:, b, :]).then_inc(sem["high_ready"], 1)
            for b in range(B):
                route_scalar_scores(act, k, r, b, 4 + b)
            for b in range(B):
                act.wait_ge(r.turned, b + 1)
                act.copy(k.routeT[0:ROUTE_ROWS, b, :],
                         k.ps[:, b, :].bitcast(BF16)[0:ROUTE_ROWS, 0:S]).then_inc(k.c_route_ready, 1)



def moe(nc, k, name, gu_name, down_name, units, store):
    with ExitStack() as ctx:
        m = Stage(nc, ctx, name, k)
        gu_high = m.sb("gu_high", [P, 2, 2 * D], F32R)
        gu_low = m.sb("gu_low", [P, 2, 2 * D], F32R)
        down_high = m.sb("down_high", [P, 2, D], F32R)
        down_low = m.sb("down_low", [P, 2, D], F32R)
        gated = m.sb("gated", [P, 2, S])
        inner = m.sb("inner", [P, 2, S])
        inner_high = m.sb("inner_high", [P, 2, S], F32R)
        inner_low = m.sb("inner_low", [P, 2, S], F32R)
        yT = m.sb("yT", [P, B, S])
        gate_done, up_done, routed = m.sem("gate_done"), m.sem("up_done"), m.sem("routed")
        silu_done, up_used, inner_ready = m.sem("silu_done"), m.sem("up_used"), m.sem("inner_ready")
        inner_high_ready, inner_low_ready = m.sem("inner_high_ready"), m.sem("inner_low_ready")
        down_done, high_ready, weights_ready = m.sem("down_done"), m.sem("high_ready"), m.sem("weights_ready")
        y_ready, turned, x_done, stored = m.sem("y_ready"), m.sem("turned"), m.sem("x_done"), m.sem("stored")
        block = ctx.enter_context(nc.Block())
        gu_at, down_at = COLS[gu_name][0], COLS[down_name][0]
        N = units * B
        PAIRS = (units - 1) // 2

        @block.gpsimd
        def _(pool):
            m.clear_last(pool)
            def split(p, buf, free=True):
                if free:
                    pool.wait_ge(down_done, (p - 1) * B)
                raw = k.w[:, bass.ds(gu_at + p * 2 * D, 2 * D)]
                pool.tensor_copy(gu_high[:, buf, :], raw).then_inc(high_ready, 1)
                raw_down = k.w[:, bass.ds(down_at + p * D, D)]
                pool.tensor_copy(down_high[:, buf, :], raw_down).then_inc(high_ready, 1)
                wait_apart(pool, k, high_ready, 2 * p + 2)
                pool.tensor_tensor(gu_low[:, buf, :], raw, gu_high[:, buf, :], ALU.subtract)
                pool.tensor_tensor(down_low[:, buf, :], raw_down, down_high[:, buf, :],
                                   ALU.subtract).then_inc(weights_ready, 1)

            split(0, 0, False)
            split(1, 1, False)
            split(2, 0)
            with pool.Fori(1, PAIRS) as pair:
                split(pair * 2 + 1, 1)
                split(pair * 2 + 2, 0)

        @block.tensor
        def _(pe):
            def down_step(n, b, buf, first):
                pe.wait_ge(inner_low_ready, n + 1)
                for i, (w, x) in enumerate(((down_high, inner_high), (down_high, inner_low), (down_low, inner_high))):
                    last = pe.matmul(k.ps[:, 4 + b, :], w[:, buf, :], x[:, b % 2, :], start=first and i == 0,
                                     stop=True, skip_group_check=True)
                last.then_inc(down_done, 1)

            def unit(p, buf, first=False):
                pe.wait_ge(weights_ready, p + 1)
                for b in range(B):
                    n = p * B + b
                    slots = [(3 * b + i) % 4 for i in range(3)]
                    if not first or b >= 2:
                        pe.wait_ge(inner_ready, n - 1)
                    for half, (slot, done) in enumerate(((slots[0], gate_done), (slots[1], up_done))):
                        if half == 1 and (not first or b >= 1):
                            pe.wait_ge(silu_done, n)
                        w = slice(half * D, (half + 1) * D)
                        pe.matmul(k.ps[:, slot, :], gu_high[:, buf, w], k.x_high[:, b, :], start=True, stop=False)
                        pe.matmul(k.ps[:, slot, :], gu_high[:, buf, w], k.x_low[:, b, :], start=False, stop=False)
                        pe.matmul(k.ps[:, slot, :], gu_low[:, buf, w], k.x_high[:, b, :], start=False,
                                  stop=True).then_inc(done, 1)
                    if not first or b >= 1:
                        pe.wait_ge(up_used, n)
                    pe.matmul(k.ps[:, slots[2], :],
                              k.sel[0:ROUTE_ROWS, bass.ds(p, 1), :].rearrange("r a c -> r (a c)"),
                              k.routeT[0:ROUTE_ROWS, b, :], start=True, stop=True).then_inc(routed, 1)
                    if b >= 2:
                        down_step(n - 2, b - 2, buf, first)
                    elif not first:
                        down_step(n - 2, b + 2, 1 - buf, isinstance(p, int) and p == 1)

            unit(0, 0, first=True)
            unit(1, 1)
            unit(2, 0)
            with pe.Fori(1, PAIRS) as pair:
                unit(pair * 2 + 1, 1)
                unit(pair * 2 + 2, 0)
            down_step(N - 2, B - 2, 0, False)
            down_step(N - 1, B - 1, 0, False)
            for b in range(B):
                pe.wait_ge(y_ready, b + 1)
                for q in range(QT):
                    last = pe.transpose(k.ps[:, b, q * P:(q + 1) * P], yT[:, b, q * P:(q + 1) * P], k.ident[:, :])
                last.then_inc(turned, 1)

        @block.scalar
        def _(act):
            def high_part(n, b, free):
                act.wait_ge(inner_ready, n + 1)
                if free:
                    act.wait_ge(down_done, n - 1)
                act.copy(inner_high[:, b % 2, :], inner[:, b % 2, :]).then_inc(inner_high_ready, 1)

            def unit(p, first=False):
                for b in range(B):
                    n = p * B + b
                    act.wait_ge(gate_done, n + 1)
                    if not first or b >= 2:
                        act.wait_ge(inner_ready, n - 1)
                    act.activation(gated[:, b % 2, :], k.ps[:, (3 * b) % 4, :], ACT.Silu).then_inc(silu_done, 1)
                    if not first or b >= 1:
                        high_part(n - 1, (b + 3) % B, not first or b >= 3)

            unit(0, first=True)
            with act.Fori(1, units) as p:
                unit(p)
            high_part(N - 1, B - 1, True)
            act.wait_ge(down_done, N)
            for b in range(B):
                act.copy(yT[:, b, :], k.ps[:, 4 + b, :]).then_inc(y_ready, 1)

        @block.vector
        def _(dve):
            def low_part(n, b):
                dve.wait_ge(inner_high_ready, n + 1)
                dve.tensor_tensor(inner_low[:, b % 2, :], inner[:, b % 2, :], inner_high[:, b % 2, :],
                                  ALU.subtract).then_inc(inner_low_ready, 1)

            def unit(p, first=False):
                for b in range(B):
                    n = p * B + b
                    dve.wait_ge(silu_done, n + 1)
                    dve.wait_ge(up_done, n + 1)
                    dve.tensor_tensor(gated[:, b % 2, :], gated[:, b % 2, :], k.ps[:, (3 * b + 1) % 4, :],
                                      ALU.mult).then_inc(up_used, 1)
                    if not first or b >= 1:
                        low_part(n - 1, (b + 3) % B)
                    dve.wait_ge(routed, n + 1)
                    dve.wait_ge(up_used, n + 1)
                    if not first or b >= 2:
                        dve.wait_ge(inner_low_ready, n - 1)
                    dve.tensor_tensor(inner[:, b % 2, :], gated[:, b % 2, :], k.ps[:, (3 * b + 2) % 4, :],
                                      ALU.mult).then_inc(inner_ready, 1)

            unit(0, first=True)
            with dve.Fori(1, units) as p:
                unit(p)
            low_part(N - 1, B - 1)
            for b in range(B):
                at = slice(b * QT, (b + 1) * QT)
                dve.wait_ge(turned, b + 1)
                dve.tensor_tensor(k.x[:, at, :], k.x[:, at, :], k.ps[:, b, :].rearrange("p (q d) -> p q d", d=D),
                                  ALU.add).then_inc(x_done, 1)

        @block.sync
        def _(sp):
            if store:
                out = k.out_dram.rearrange("b (q p) d -> p (b q) d", p=P)
                for b in range(B):
                    at = slice(b * QT, (b + 1) * QT)
                    sp.wait_ge(x_done, b + 1)
                    sp.dma_start(out[:, at, :], k.x[:, at, :]).then_inc(stored, 16)
                sp.wait_ge(stored, 16 * B)



def attn1_project(nc, k):
    with ExitStack() as ctx:
        m = Stage(nc, ctx, "d_", k)
        n = Norm(m, "norm")
        s = Split(m)
        x_padded = m.sb("x_padded", [P, B, S + 2])
        conv = n.out[:, :, :].rearrange("p (b q) d -> p b (q d)", b=B)[:, :, 0:NK]
        in_psum, xT_ready = m.sem("x_in_psum"), m.sem("xT_ready")
        q_done, k_done, v_done = m.sem("q_done"), m.sem("k_done"), m.sem("v_done")
        zeroed, v_zeroed, pad_set, v_copied = m.sem("zeroed"), m.sem("v_zeroed"), m.sem("pad_set"), m.sem("v_copied")
        taps = [m.sem(f"tap{i}") for i in range(3)]
        block = ctx.enter_context(nc.Block())
        scale = float(HD) ** -0.5

        @block.sync
        def _(sp):
            for b in range(B):
                store_parts(sp, k, s, b, (S, NK), k.d_stored)
                if b == 0:
                    sp.wait_ge(zeroed, 2)
                    load_stacks(sp, k, 0, (S, NK), k.d_stored, k.d_loaded)

        @block.gpsimd
        def _(pool):
            m.clear_last(pool)
            pool.memset(x_padded[:, :, 0:1], 0.0).then_inc(pad_set, 1)
            for b in range(B):
                norm_rstd(pool, k, n, b)
            for b in range(2):
                pool.memset(k.q_stack[0:KROWS, b, :, :].bitcast(F32), 0.0).then_inc(zeroed, 1)
                pool.memset(k.k_stack[0:KROWS, b, :, :].bitcast(F32), 0.0).then_inc(zeroed, 1)
            pool.memset(k.v_padded[:, :, :, :], 0.0).then_inc(v_zeroed, 1)

        @block.vector
        def _(dve):
            norm_all(dve, n, k.x)
            for b in range(B):
                dve.wait_ge(taps[1], b + 1)
                if b == 0:
                    dve.wait_ge(pad_set, 1)
                dve.scalar_tensor_tensor(conv[:, b, :], x_padded[:, b, 0:S:2], col(k, "conv_w", 0), conv[:, b, :],
                                         ALU.mult, ALU.add).then_inc(taps[0], 1)
                dve.wait_ge(taps[0], b + 1)
                dve.scalar_tensor_tensor(conv[:, b, :], x_padded[:, b, 2:S + 2:2], col(k, "conv_w", 2),
                                         conv[:, b, :], ALU.mult, ALU.add).then_inc(taps[2], 1)

            def full(i, out):
                b = i // 2
                if i % 2 == 0:
                    dve.wait_ge(q_done, b + 1)
                    return dve.tensor_scalar(out, k.ps[:, 4 + b, :], col(k, "d_bq"), scale, ALU.add, ALU.mult)
                dve.wait_ge(k_done, b + 1)
                return dve.tensor_scalar(out, k.ps[:, b, 0:NK], col(k, "d_bk"), None, ALU.add)

            split_vector(dve, s, (S, NK), full)
            dve.wait_ge(v_zeroed, 1)
            bias = row(k, "d_bv").rearrange("p (g j d) -> p g j d", g=4, j=4)
            for b in range(B):
                dve.wait_ge(v_done, b + 1)
                for t in range(NK // P):
                    out = k.v_padded[:, b, t, :].rearrange("p (g x) -> p g x", g=4)[:, :, 0:D]
                    last = dve.tensor_tensor(
                        out.rearrange("p g (j y) -> p g j y", j=4)[:, :, :, 0:HD],
                        k.ps[:, b, t * D:(t + 1) * D].rearrange("p (g j d) -> p g j d", g=4, j=4), bias, ALU.add)
                last.then_inc(v_copied, 1)

        @block.tensor
        def _(pe):
            for b in range(B):
                pe.wait_ge(n.ready, b + 1)
                transpose_batch(pe, k, n.out, b, b).then_inc(in_psum, 1)
            for b in range(B):
                pe.wait_ge(xT_ready, b + 1)
                pe.matmul(k.ps[:, 4 + b, :], weight(k, "d_q"), x_padded[:, b, 1:S + 1], start=True,
                          stop=True).then_inc(q_done, 1)
            for b in range(B):
                pe.wait_ge(taps[2], b + 1)
                pe.matmul(k.ps[:, b, 0:NK], weight(k, "d_k"), conv[:, b, :], start=True,
                          stop=True).then_inc(k_done, 1)
            for b in range(B):
                pe.wait_ge(s.full_ready, 2 * b + 2)
                for t in range(NK // P):
                    last = pe.matmul(k.ps[:, b, t * D:(t + 1) * D], conv[:, b, t * P:(t + 1) * P],
                                     weight(k, "d_v"), start=True, stop=True)
                last.then_inc(v_done, 1)

        @block.scalar
        def _(act):
            for b in range(B):
                act.wait_ge(in_psum, b + 1)
                act.copy(x_padded[:, b, 1:S + 1], k.ps[:, b, :]).then_inc(xT_ready, 1)
                act.wait_ge(xT_ready, b + 1)
                act.activation(conv[:, b, :], x_padded[:, b, 1:S + 1:2], ACT.Identity, bias=col(k, "conv_b"),
                               scale=col(k, "conv_w", 1)).then_inc(taps[1], 1)
            split_scalar(act, s, (S, NK), k.d_stored)



def attn1_heads(nc, k):
    with ExitStack() as ctx:
        m = Stage(nc, ctx, "dh_", k)
        N, BODY = B * H, 8
        minus_max = m.sb("minus_max", [P, N, QT])
        probs = m.sb("probs", [P, 4, QT, NK])
        v = m.sb("v", [P, BODY, NK // P, 32])
        probsT = m.sb("probsT", [P, BODY, NK // P, S])
        scored, max_ready, exp_done = m.sem("scored"), m.sem("max_ready"), m.sem("exp_done")
        turned = [m.sem("turned0"), m.sem("turned1")]
        copied = [m.sem("copied0"), m.sem("copied1")]
        v_ready, attended, quad_added = m.sem("v_ready"), m.sem("attended"), m.sem("quad_added")
        stacks_ready = m.sem("stacks_ready")
        block = ctx.enter_context(nc.Block())

        def scores_of(i):
            return k.ps[:, 2 * (i % 2):2 * (i % 2) + 2, :].rearrange("p a (q t) -> p (a q) t", t=NK)

        def bodies(eng, body):
            body(0, True)
            with eng.Fori(1, N // BODY) as i:
                body(i, False)

        @block.sync
        def _(sp):
            for b in range(B):
                if b >= 2:
                    sp.wait_ge(scored, H * (b - 1))
                if b >= 1:
                    load_stacks(sp, k, b, (S, NK), k.d_stored, k.d_loaded)
                sp.wait_ge(k.d_loaded, STACK_LOADED * (b + 1))
                sp.sem_inc(stacks_ready, H // BODY)

        @block.gpsimd
        def _(pool):
            m.clear_last(pool)
            def body(it, first):
                for i in range(BODY):
                    n = it * BODY + i
                    if not first and i % 4 == 0:
                        pool.wait_ge(attended, it * 2 + i // 4 - 1)
                    b, at = it // 2, (i // 4 + 2 * (it % 2)) * P + 32 * (i % 4)
                    pool.tensor_copy(v[:, i, :, :],
                                     k.v_padded[:, bass.ds(b, 1), :, bass.ds(at, 32)]
                                     .rearrange("p a t c -> p (a t) c")).then_inc(v_ready, 1)

            pool.memset(k.attended[:, :, :], 0.0).then_inc(quad_added, 1)
            bodies(pool, body)

        @block.tensor
        def _(pe):
            def scores(it, i, first):
                n, b = it * BODY + i, it // 2
                head = (it % 2) * BODY + i
                if i == 0:
                    pe.wait_ge(stacks_ready, it + 1)
                if not first or i >= 2:
                    pe.wait_ge(exp_done, n - 1)
                at = (b % 2) * H + head
                q_rows = k.q_stack[0:KROWS, :, :, :].rearrange("p a h t -> p (a h) t")
                k_rows = k.k_stack[0:KROWS, :, :, :].rearrange("p a h t -> p (a h) t")
                for q in range(QT):
                    last = pe.matmul(scores_of(i)[:, q, :],
                                     q_rows[:, bass.ds(at, 1), q * P:(q + 1) * P].rearrange("p a t -> p (a t)"),
                                     k_rows[:, bass.ds(at, 1), :].rearrange("p a t -> p (a t)"),
                                     start=True, stop=True)
                last.then_inc(scored, 1)

            def turn(n, i, first):
                pe.wait_ge(exp_done, n + 1)
                for t in range(NK // P):
                    if not first:
                        pe.wait_ge(copied[t], n)
                    for q in range(QT):
                        last = pe.transpose(k.ps[:, 4 + t, q * P:(q + 1) * P],
                                            probs[:, i % 4, q, t * P:(t + 1) * P], k.ident[:, :])
                    last.then_inc(turned[t], 1)

            def attend(quad, half, t, first):
                if t == 0:
                    if not first:
                        pe.wait_ge(quad_added, quad)
                    pe.wait_ge(v_ready, quad * 4 + 4)
                pe.wait_ge(copied[t], quad * 4 + 4)
                for j in range(4):
                    last = pe.matmul(k.ps[32 * j:32 * j + 32, 6 + half, :], v[:, 4 * half + j, t, :],
                                     probsT[:, 4 * half + j, t, :], start=(t == 0), stop=(t == NK // P - 1))
                if t == NK // P - 1:
                    last.then_inc(attended, 1)

            def body(it, first):
                for i in range(BODY):
                    n = it * BODY + i
                    scores(it, i, first)
                    if not first or i >= 2:
                        turn(n - 2, (i - 2) % BODY, first and i == 2)
                    if i in (2, 3) and not first:
                        attend(it * 2 - 1, 1, i - 2, False)
                    if i in (6, 7):
                        attend(it * 2, 0, i - 6, first)

            bodies(pe, body)
            turn(N - 2, BODY - 2, False)
            turn(N - 1, BODY - 1, False)
            for t in range(NK // P):
                attend(N // 4 - 1, 1, t, False)

        def copy_turned(eng, copy, n, i, t, quad):
            eng.wait_ge(turned[t], n + 1)
            if quad is not None:
                eng.wait_ge(attended, quad - 1)
            copy(probsT[:, i, t, :], k.ps[:, 4 + t, :]).then_inc(copied[t], 1)

        def quad_of(it, i, first):
            return None if first or i < 2 else it * 2 + (i - 2) // 4

        @block.vector
        def _(dve):
            def copies(n, i, quad):
                copy_turned(dve, dve.tensor_copy, n, i, 0, quad)
                if i % 2 == 0:
                    copy_turned(dve, dve.tensor_copy, n, i, 1, quad)

            def add_quad(quad, half, b):
                dve.wait_ge(attended, quad + 1)
                dve.wait_ge(quad_added, quad + 1)
                out = k.attended[:, bass.ds(b, 1), :].rearrange("p a t -> p (a t)")
                dve.tensor_tensor(out, out, k.ps[:, 6 + half, :], ALU.add).then_inc(quad_added, 1)

            def body(it, first):
                for i in range(BODY):
                    n = it * BODY + i
                    dve.wait_ge(scored, n + 1)
                    dve.tensor_reduce(minus_max[:, bass.ds(n, 1), :].rearrange("p a q -> p (a q)"),
                                      scores_of(i), AX_X, ALU.max, negate=True).then_inc(max_ready, 1)
                    if first and i == 2:
                        for b in range(B):
                            dve.wait_ge(k.d_stored[b], 32)
                    if not first or i >= 2:
                        copies(n - 2, (i - 2) % BODY, quad_of(it, i, first))
                    if i % 4 == 0 and not first:
                        add_quad(it * 2 - 2 + i // 4, i // 4, (it - 1) // 2)

            bodies(dve, body)
            for i in (BODY - 2, BODY - 1):
                copies(N - BODY + i, i, None)
            add_quad(N // 4 - 2, 0, B - 1)
            add_quad(N // 4 - 1, 1, B - 1)

        @block.scalar
        def _(act):
            def copies(n, i, quad):
                if i % 2 == 1:
                    copy_turned(act, act.copy, n, i, 1, quad)

            def body(it, first):
                for i in range(BODY):
                    n = it * BODY + i
                    if first and i == 2:
                        for b in range(B):
                            act.wait_ge(k.d_stored[b], 32)
                    if not first or i >= 2:
                        copies(n - 2, (i - 2) % BODY, quad_of(it, i, first))
                    if not first or i >= 4:
                        act.wait_ge(turned[1], n - 3)
                    wait_apart(act, k, max_ready, n + 1)
                    for q in range(QT):
                        last = act.activation(probs[:, i % 4, q, :], scores_of(i)[:, q, :], ACT.Exp,
                                              bias=minus_max[:, bass.ds(n, 1), q:q + 1]
                                              .rearrange("p a q -> p (a q)"),
                                              accum_out=k.exp_sum[:, bass.ds(n, 1), q:q + 1]
                                              .rearrange("p a q -> p (a q)"))
                    last.then_inc(exp_done, 1)

            bodies(act, body)
            copies(N - 1, BODY - 1, None)



def attn1_out_latents(nc, k):
    with ExitStack() as ctx:
        m = Stage(nc, ctx, "e0_", k)
        n, n2 = Norm(m, "norm"), Norm(m, "latent")
        nm = Norm(m, "media", tiles=1, rows=C)
        inverse = m.sb("inverse", [P, B * H, QT])
        wide = m.sb("wide", [P, T, D])
        attnT = wide[:, :, :].rearrange("p (b q) d -> p b (q d)", b=B)
        out_bias = m.sb("out_bias", [P, 1])
        names = ["inv_ready", "wide_ready", "invT", "attn_ready", "projected", "x_ready", "biased", "scaled_w",
                 "scaled", "shifted", "media_scaled", "media_shifted", "in_psum", "media_in_psum", "high", "low",
                 "media_high", "media_low", "token_high", "media_token_high", "folded", "bias_sum", "pad_set"]
        sem = {x: m.sem(x) for x in names}
        block = ctx.enter_context(nc.Block())
        scale = float(D) ** -0.5

        @block.gpsimd
        def _(pool):
            m.clear_last(pool)
            for b in range(B):
                at = slice(b * QT, (b + 1) * QT)
                pool.tensor_tensor(k.x[:, at, :], k.x[:, at, :],
                                   row(k, "d_bo").unsqueeze(1).broadcast_to([P, QT, D]),
                                   ALU.add).then_inc(sem["biased"], 1)
            pool.wait_ge(k.w_loaded["e"], 16)
            at, w = COL["e_bq"]
            pool.tensor_scalar(weight(k, "e_q"), weight(k, "e_q"), scale, 1.0, ALU.mult,
                               ALU.mult).then_inc(sem["scaled_w"], 1)
            pool.tensor_scalar(k.cols[:, at:at + w], k.cols[:, at:at + w], scale, 1.0, ALU.mult,
                               ALU.mult).then_inc(sem["scaled_w"], 1)
            pool.memset(k.kvT_high[:, :, S + C:].bitcast(F32), 0.0).then_inc(sem["pad_set"], 1)
            pool.memset(k.kvT_low[:, :, S + C:].bitcast(F32), 0.0).then_inc(sem["pad_set"], 1)
            for b in range(B):
                norm_rstd(pool, k, nm, b)
            for b in range(B):
                norm_rstd(pool, k, n, b)
            for b in range(B):
                pool.wait_ge(nm.ready, b + 1)
                pool.tensor_tensor(nm.out[0:C, b, :], nm.out[0:C, b, :], row(k, "g_med", C),
                                   ALU.mult).then_inc(sem["media_scaled"], 1)
                pool.wait_ge(sem["media_scaled"], b + 1)
                pool.tensor_tensor(nm.out[0:C, b, :], nm.out[0:C, b, :], row(k, "b_med", C),
                                   ALU.add).then_inc(sem["media_shifted"], 1)
            for b in range(B):
                norm_rstd(pool, k, n2, b)

        @block.vector
        def _(dve):
            norm_all(dve, nm, k.media, lambda b: dve.wait_ge(k.media_loaded, 16))
            dve.reciprocal(inverse[:, :, :], k.exp_sum[:, :, :]).then_inc(sem["inv_ready"], 1)
            dve.wait_ge(sem["inv_ready"], 1)
            for b in range(B):
                for q in range(QT):
                    last = dve.tensor_copy(
                        wide[:, b * QT + q, :].rearrange("p (j g d) -> p j g d", j=4, g=4),
                        inverse[:, b * H:(b + 1) * H, q].rearrange("p (g j) -> p j g", j=4).unsqueeze(3)
                        .broadcast_to([P, 4, 4, HD]))
                last.then_inc(sem["wide_ready"], 1)
            for b in range(B):
                dve.wait_ge(sem["invT"], b + 1)
                dve.tensor_tensor(attnT[:, b, :], k.attended[:, b, :], k.ps[:, b, :],
                                  ALU.mult).then_inc(sem["attn_ready"], 1)
            for b in range(B):
                at = slice(b * QT, (b + 1) * QT)
                dve.wait_ge(sem["projected"], b + 1)
                dve.wait_ge(sem["biased"], b + 1)
                dve.tensor_tensor(k.x[:, at, :], k.x[:, at, :],
                                  k.ps[:, 4 + b, :].rearrange("p (q d) -> p q d", d=D),
                                  ALU.add).then_inc(sem["x_ready"], 1)
            norm_all(dve, n, k.x, lambda b: dve.wait_ge(sem["x_ready"], b + 1))
            norm_all(dve, n2, n.out, lambda b: dve.wait_ge(n.ready, b + 1))
            for b in range(B):
                at = slice(b * QT, (b + 1) * QT)
                dve.wait_ge(n2.ready, b + 1)
                dve.tensor_tensor(n2.out[:, at, :], n2.out[:, at, :],
                                  row(k, "g_lat").unsqueeze(1).broadcast_to([P, QT, D]),
                                  ALU.mult).then_inc(sem["scaled"], 1)
            for b in range(B):
                at = slice(b * QT, (b + 1) * QT)
                dve.wait_ge(sem["scaled"], b + 1)
                dve.tensor_tensor(n2.out[:, at, :], n2.out[:, at, :],
                                  row(k, "b_lat").unsqueeze(1).broadcast_to([P, QT, D]),
                                  ALU.add).then_inc(sem["shifted"], 1)
            for b in range(B):
                at = slice(b * QT, (b + 1) * QT)
                dve.wait_ge(sem["high"], b + 1)
                dve.tensor_tensor(k.kvT_low[:, b, 0:S], k.ps[:, b, :], k.kvT_high[:, b, 0:S],
                                  ALU.subtract).then_inc(sem["low"], 1)
                dve.wait_ge(sem["media_high"], b + 1)
                dve.tensor_tensor(k.kvT_low[:, b, S:KV], k.ps[:, 4 + b, 0:C], k.kvT_high[:, b, S:KV],
                                  ALU.subtract).then_inc(sem["media_low"], 1)
                dve.wait_ge(sem["token_high"], b + 1)
                dve.tensor_tensor(k.kv_low[:, b, 0:QT, :], n2.out[:, at, :], k.kv_high[:, b, 0:QT, :],
                                  ALU.subtract)
                dve.wait_ge(sem["media_token_high"], b + 1)
                dve.tensor_tensor(k.kv_low[0:C, b, QT, :], nm.out[0:C, b, :], k.kv_high[0:C, b, QT, :],
                                  ALU.subtract).then_inc(k.kv_ready, 1)
            dve.wait_ge(sem["bias_sum"], 1)
            dve.tensor_scalar(k.out_bias[:, :], k.ps[:, 6, 0:1], col(k, "e_bo"), None,
                              ALU.add).then_inc(k.kv_ready, 1)

        @block.tensor
        def _(pe):
            for b in range(B):
                pe.wait_ge(sem["wide_ready"], b + 1)
                transpose_batch(pe, k, wide, b, b).then_inc(sem["invT"], 1)
            for b in range(B):
                pe.wait_ge(sem["attn_ready"], b + 1)
                for q in range(QT):
                    last = pe.matmul(k.ps[:, 4 + b, q * D:(q + 1) * D], attnT[:, b, q * P:(q + 1) * P],
                                     weight(k, "d_out"), start=True, stop=True)
                last.then_inc(sem["projected"], 1)
            for b in range(B):
                pe.wait_ge(sem["media_shifted"], b + 1)
                pe.wait_ge(sem["x_ready"], b + 1)
                pe.transpose(k.ps[:, 4 + b, 0:C], nm.out[0:C, b, :], k.ident[0:C, 0:C]
                             ).then_inc(sem["media_in_psum"], 1)
            for b in range(B):
                pe.wait_ge(sem["shifted"], b + 1)
                transpose_batch(pe, k, n2.out, b, b).then_inc(sem["in_psum"], 1)
            for g in range(2):
                pe.wait_ge(sem["media_low"], g + 1)
                for j in range(4):
                    h = slice((4 * g + j) * D, (4 * g + j + 1) * D)
                    last = pe.matmul(k.ps[:, 4 + g, j * D:(j + 1) * D], weight(k, "e_vT")[:, h],
                                     weight(k, "e_o")[:, h], start=True, stop=True)
                last.then_inc(sem["folded"], 1)
            pe.wait_ge(sem["media_low"], 3)
            for h in range(XH):
                last = pe.matmul(k.ps[:, 6, 0:1], weight(k, "e_o")[:, h * D:(h + 1) * D], col(k, "e_bv", h),
                                 start=(h == 0), stop=(h == XH - 1))
            last.then_inc(sem["bias_sum"], 1)

        @block.scalar
        def _(act):
            for b in range(B):
                act.wait_ge(sem["media_in_psum"], b + 1)
                act.copy(k.kvT_high[:, b, S:KV], k.ps[:, 4 + b, 0:C]).then_inc(sem["media_high"], 1)
                act.copy(k.kv_high[0:C, b, QT, :], nm.out[0:C, b, :]).then_inc(sem["media_token_high"], 1)
            for b in range(B):
                at = slice(b * QT, (b + 1) * QT)
                act.wait_ge(sem["in_psum"], b + 1)
                act.copy(k.kvT_high[:, b, 0:S], k.ps[:, b, :]).then_inc(sem["high"], 1)
                act.copy(k.kv_high[:, b, 0:QT, :], n2.out[:, at, :]).then_inc(sem["token_high"], 1)
            for g in range(2):
                act.wait_ge(sem["folded"], g + 1)
                act.copy(k.w_vo[:, 4 * g:4 * g + 4, :],
                         k.ps[:, 4 + g, :].rearrange("p (h d) -> p h d", h=4)).then_inc(k.kv_ready, 1)



def xattn1_heads(nc, k):
    with ExitStack() as ctx:
        m = Stage(nc, ctx, "e_", k)
        U = XH * B
        SPLIT = 3
        wq = m.sb("wq", [P, 2, D], F32R)
        wk = m.sb("wk", [P, 2, D], F32R)
        wo = m.sb("wo", [P, D])
        qT = m.sb("qT", [P, 2, 2, S], F32R)
        kT = m.sb("kT", [P, 2, 2, S], F32R)
        q_full = k.w[:, 0:2 * S].rearrange("p (a t) -> p a t", a=2)
        media_kT = m.sb("media_kT", [P, 2, C + 1])
        probs = m.sb("probs", [P, 2 * QT, KV])
        minus_max, exp_sum, inverse = (m.sb("minus_max", [P, 4]), m.sb("exp_sum", [P, 4]), m.sb("inverse", [P, 4]))
        turned_high = m.sb("turned_high", [P, 2, KT, S], F32R)
        turned_low = m.sb("turned_low", [P, 2, KT, S], F32R)
        attn = weight(k, "e_o").rearrange("p (a t) -> p a t", a=2)
        names = ["w_high", "w_ready", "wo_ready", "q_done", "k_done", "km_done", "q_high", "k_high", "km_ready",
                 "q_low", "k_low", "q_summed", "scored", "max_ready", "exp_done", "inv_ready", "normed", "turned",
                 "t_high", "t_low", "attended", "attn_ready", "out_done", "added"]
        sem = {x: m.sem(x) for x in names}
        block = ctx.enter_context(nc.Block())
        eq, ek = COLS["e_q"][0], COLS["e_k"][0]
        bq, bk = COL["e_bq"][0], COL["e_bk"][0]

        def pair(q):
            return k.ps[:, 2 * (q % 2):2 * (q % 2) + 2, :].rearrange("p a t -> p (a t)")

        def heads(eng, body):
            for h in (0, None, XH - 1):
                if h is not None:
                    for b in range(B):
                        body(h, b, h == 0, h == XH - 1)
                else:
                    with eng.Fori(1, XH - 1) as i:
                        for b in range(B):
                            body(i, b, False, False)

        @block.gpsimd
        def _(pool):
            m.clear_last(pool)
            def weights(h):
                for w, at in ((wq, eq), (wk, ek)):
                    pool.tensor_copy(w[:, 0, :], k.w[:, bass.ds(at + h * D, D)]).then_inc(sem["w_high"], 1)
                wait_apart(pool, k, sem["w_high"], 2 * h + 2)
                for w, at in ((wq, eq), (wk, ek)):
                    last = pool.tensor_tensor(w[:, 1, :], k.w[:, bass.ds(at + h * D, D)], w[:, 0, :], ALU.subtract)
                last.then_inc(sem["w_ready"], 1)

            def sum_q(u, b):
                pool.wait_ge(sem["q_low"], u + 1)
                pool.tensor_tensor(q_full[:, b % 2, :], qT[:, b % 2, 0, :], qT[:, b % 2, 1, :],
                                   ALU.add).then_inc(sem["q_summed"], 1)

            def output_weights(h):
                pool.tensor_copy(wo[:, :], k.w_vo[:, bass.ds(h, 1), :].rearrange("p a d -> p (a d)")
                                 ).then_inc(sem["wo_ready"], 1)

            def body(h, b, first, last):
                u = 4 * h + b
                for q in range(QT):
                    s = 4 * u + q
                    if b == 2 and q == 0 and not first:
                        pool.wait_ge(sem["out_done"], u - 2)
                        output_weights(h)
                    at = probs[:, (b % 2) * QT + q, :]
                    wait_apart(pool, k, sem["inv_ready"], s + 1)
                    pool.tensor_scalar(at, at, inverse[:, q:q + 1], 1.0, ALU.mult,
                                       ALU.mult).then_inc(sem["normed"], 1)
                    if q == 1 and not (last and b == B - 1):
                        sum_q(u + 1, (b + 1) % B)
                    if b == 2 and q == 1 and not last:
                        pool.wait_ge(sem["km_done"], u + 2)
                        weights(h + 1)

            weights(0)
            sum_q(0, 0)
            output_weights(0)
            heads(pool, body)

        @block.tensor
        def _(pe):
            def three(out, high, low, m_high, m_low):
                pe.matmul(out, high, m_high, start=True, stop=False)
                pe.matmul(out, high, m_low, start=False, stop=False)
                return pe.matmul(out, low, m_high, start=False, stop=True)

            def project_q(u, b):
                three(k.ps[:, 6, :], wq[:, 0, :], wq[:, 1, :], k.kvT_high[:, b, 0:S],
                      k.kvT_low[:, b, 0:S]).then_inc(sem["q_done"], 1)

            def project_k(u, b):
                three(k.ps[:, 6, :], wk[:, 0, :], wk[:, 1, :], k.kvT_high[:, b, 0:S],
                      k.kvT_low[:, b, 0:S]).then_inc(sem["k_done"], 1)

            def project_media(u, b):
                three(k.ps[:, 6, 0:C + 1], wk[:, 0, :], wk[:, 1, :], k.kvT_high[:, b, S:KV + 1],
                      k.kvT_low[:, b, S:KV + 1]).then_inc(sem["km_done"], 1)

            def scores(s, b, q):
                v, t = b % 2, slice(q * P, (q + 1) * P)
                three(pair(q)[:, 0:S], qT[:, v, 0, t], qT[:, v, 1, t], kT[:, v, 0, :], kT[:, v, 1, :])
                pe.matmul(pair(q)[:, S:KV], q_full[:, v, t], media_kT[:, v, 0:C], start=True,
                          stop=True).then_inc(sem["scored"], 1)

            def turn(u, b, q, free):
                use = 5 * u + q
                bank = 4 + (b + q) % 2
                pe.wait_ge(sem["normed"], 4 * u + min(q, QT - 1) + 1)
                if free:
                    pe.wait_ge(sem["t_low"], use - 1)
                for i in range(QT):
                    if q < QT:
                        out, src = k.ps[:, bank, i * P:(i + 1) * P], probs[:, (b % 2) * QT + q, i * P:(i + 1) * P]
                    else:
                        out, src = k.ps[0:C, bank, i * P:(i + 1) * P], probs[:, (b % 2) * QT + i, S:KV]
                    last = pe.transpose(out, src, k.ident[:, :])
                last.then_inc(sem["turned"], 1)

            def attend(u, b, first, last):
                pe.wait_ge(sem["t_low"], 5 * u + (5 if last == KT else 4))
                for i in range(first, last):
                    r = P if i < QT else C
                    kv = (k.kv_high[0:r, b, i, :], k.kv_low[0:r, b, i, :])
                    pt = (turned_high[0:r, b % 2, i, :], turned_low[0:r, b % 2, i, :])
                    pe.matmul(k.ps[:, 7, :], kv[0], pt[0], start=(i == 0), stop=False)
                    pe.matmul(k.ps[:, 7, :], kv[0], pt[1], start=False, stop=False)
                    done = pe.matmul(k.ps[:, 7, :], kv[1], pt[0], start=False, stop=(i == KT - 1))
                if last == KT:
                    done.then_inc(sem["attended"], 1)

            def output(u, h, b):
                pe.wait_ge(sem["attn_ready"], u + 1)
                if b == 0:
                    pe.wait_ge(sem["wo_ready"], h + 1)
                pe.matmul(k.ps[:, 7, :], wo[:, :], attn[:, b % 2, :], start=True,
                          stop=True).then_inc(sem["out_done"], 1)

            def body(h, b, first, last):
                u = 4 * h + b
                some1, some2 = not first or b >= 1, not first or b >= 2
                more = not last or b < B - 1
                nb = (b + 1) % B
                b1 = (b + 3) % B
                pe.wait_ge(sem["k_low"], u + 1)
                pe.wait_ge(sem["km_ready"], u + 1)
                pe.wait_ge(sem["q_summed"], u + 1)
                for q in range(QT):
                    s = 4 * u + q
                    if not first or b or q >= 2:
                        pe.wait_ge(sem["exp_done"], s - 1)
                    scores(s, b, q)
                    if q == 0:
                        if more:
                            if nb == 0:
                                pe.wait_ge(sem["w_ready"], h + 2)
                            project_q(u + 1, nb)
                        if some1:
                            turn(u - 1, b1, 2, True)
                        if some2:
                            attend(u - 2, (b + 2) % B, SPLIT, KT)
                    if q == 1:
                        if more:
                            pe.wait_ge(sem["q_low"], u + 2)
                            project_k(u + 1, nb)
                        if some1:
                            turn(u - 1, b1, 3, True)
                            turn(u - 1, b1, 4, True)
                    if q == 2:
                        if some2:
                            output(u - 2, h if b >= 2 else h - 1, (b + 2) % B)
                        if more:
                            pe.wait_ge(sem["k_low"], u + 2)
                            project_media(u + 1, nb)
                        turn(u, b, 0, some1)
                    if q == 3:
                        if some1:
                            if some2:
                                pe.wait_ge(sem["added"], u - 1)
                            attend(u - 1, b1, 0, SPLIT)
                        turn(u, b, 1, some1)

            pe.wait_ge(k.kv_ready, B + 3)
            pe.wait_ge(sem["w_ready"], 1)
            project_q(0, 0)
            pe.wait_ge(sem["q_low"], 1)
            project_k(0, 0)
            pe.wait_ge(sem["k_low"], 1)
            project_media(0, 0)
            heads(pe, body)
            u = U - 1
            turn(u, B - 1, 2, True)
            attend(u - 1, (u - 1) % B, SPLIT, KT)
            turn(u, B - 1, 3, True)
            turn(u, B - 1, 4, True)
            output(u - 1, XH - 1, (u - 1) % B)
            pe.wait_ge(sem["added"], u)
            attend(u, B - 1, 0, KT)
            output(u, XH - 1, B - 1)

        def bias_col(at, h):
            return k.cols[:, bass.ds(at + h, 1)]

        @block.scalar
        def _(act):
            def high_q(u, h, b):
                wait_apart(act, k, sem["q_done"], u + 1)
                act.activation(qT[:, b % 2, 0, :], k.ps[:, 6, :], ACT.Identity,
                               bias=bias_col(bq, h)).then_inc(sem["q_high"], 1)

            def high_k(u, h, b):
                wait_apart(act, k, sem["k_done"], u + 1)
                act.activation(kT[:, b % 2, 0, :], k.ps[:, 6, :], ACT.Identity,
                               bias=bias_col(bk, h)).then_inc(sem["k_high"], 1)

            def media_keys(u, h, b):
                wait_apart(act, k, sem["km_done"], u + 1)
                act.activation(media_kT[:, b % 2, :], k.ps[:, 6, 0:C + 1], ACT.Identity,
                               bias=bias_col(bk, h)).then_inc(sem["km_ready"], 1)

            def exps(u, b, q, free):
                s = 4 * u + q
                act.wait_ge(sem["max_ready"], s + 1)
                if free:
                    act.wait_ge(sem["turned"], 5 * u - 5)
                act.activation(probs[:, (b % 2) * QT + q, :], pair(q)[:, 0:KV], ACT.Exp,
                               bias=minus_max[:, q:q + 1], accum_out=exp_sum[:, q:q + 1]
                               ).then_inc(sem["exp_done"], 1)

            def high_turned(u, b, q, free):
                use = 5 * u + q
                bank = 4 + (b + q) % 2
                act.wait_ge(sem["turned"], use + 1)
                if free:
                    act.wait_ge(sem["attended"], u - 1)
                if q < QT:
                    act.copy(turned_high[:, b % 2, 0:QT, q * P:(q + 1) * P],
                             k.ps[:, bank, :].rearrange("p (i t) -> p i t", t=P)).then_inc(sem["t_high"], 1)
                else:
                    act.copy(turned_high[0:C, b % 2, QT, :], k.ps[0:C, bank, :]).then_inc(sem["t_high"], 1)

            def take_attended(u, b, free):
                act.wait_ge(sem["attended"], u + 1)
                if free:
                    act.wait_ge(sem["out_done"], u - 1)
                act.copy(attn[:, b % 2, :], k.ps[:, 7, :]).then_inc(sem["attn_ready"], 1)

            def body(h, b, first, last):
                u = 4 * h + b
                some1, some2, some3 = (not first or b >= i for i in (1, 2, 3))
                more = not last or b < B - 1
                nb, nh = (b + 1) % B, h if b < B - 1 else h + 1
                b1 = (b + 3) % B
                if some1:
                    high_turned(u - 1, b1, 1, some3)
                if more:
                    high_q(u + 1, nh, nb)
                exps(u, b, 0, some2)
                if some1:
                    high_turned(u - 1, b1, 2, some3)
                if some2:
                    take_attended(u - 2, (b + 2) % B, not first)
                if more:
                    high_k(u + 1, nh, nb)
                exps(u, b, 1, some2)
                if some1:
                    high_turned(u - 1, b1, 3, some3)
                    high_turned(u - 1, b1, 4, some3)
                if more:
                    media_keys(u + 1, nh, nb)
                exps(u, b, 2, some2)
                high_turned(u, b, 0, some2)
                exps(u, b, 3, some2)

            high_q(0, 0, 0)
            high_k(0, 0, 0)
            media_keys(0, 0, 0)
            heads(act, body)
            high_turned(U - 1, B - 1, 1, True)
            high_turned(U - 1, B - 1, 2, True)
            take_attended(U - 2, (U - 2) % B, True)
            high_turned(U - 1, B - 1, 3, True)
            high_turned(U - 1, B - 1, 4, True)
            take_attended(U - 1, B - 1, True)

        @block.vector
        def _(dve):
            def low_part(u, h, b, out, high, bank, at, w, high_sem, low_sem):
                dve.wait_ge(sem[high_sem], u + 1)
                dve.scalar_tensor_tensor(out, k.ps[:, bank, 0:w], bias_col(at, h), high, ALU.add,
                                         ALU.subtract).then_inc(sem[low_sem], 1)

            def low_q(u, h, b):
                low_part(u, h, b, qT[:, b % 2, 1, :], qT[:, b % 2, 0, :], 6, bq, S, "q_high", "q_low")

            def low_k(u, h, b):
                low_part(u, h, b, kT[:, b % 2, 1, :], kT[:, b % 2, 0, :], 6, bk, S, "k_high", "k_low")

            def invert(s, q, free):
                dve.wait_ge(sem["exp_done"], s + 1)
                if free:
                    dve.wait_ge(sem["normed"], s - 3)
                dve.reciprocal(inverse[:, q:q + 1], exp_sum[:, q:q + 1]).then_inc(sem["inv_ready"], 1)

            def maximum(s, q):
                dve.wait_ge(sem["scored"], s + 1)
                dve.tensor_reduce(minus_max[:, q:q + 1], pair(q)[:, 0:KV], AX_X, ALU.max,
                                  negate=True).then_inc(sem["max_ready"], 1)

            def low_turned(u, b, q):
                use = 5 * u + q
                bank = 4 + (b + q) % 2
                dve.wait_ge(sem["t_high"], use + 1)
                if q < QT:
                    at = slice(q * P, (q + 1) * P)
                    dve.tensor_tensor(turned_low[:, b % 2, 0:QT, at],
                                      k.ps[:, bank, :].rearrange("p (i t) -> p i t", t=P),
                                      turned_high[:, b % 2, 0:QT, at], ALU.subtract).then_inc(sem["t_low"], 1)
                else:
                    dve.tensor_tensor(turned_low[0:C, b % 2, QT, :], k.ps[0:C, bank, :],
                                      turned_high[0:C, b % 2, QT, :], ALU.subtract).then_inc(sem["t_low"], 1)

            def add_output(u, b, first):
                dve.wait_ge(sem["out_done"], u + 1)
                if first:
                    dve.tensor_scalar(k.yT[:, b, :], k.ps[:, 7, :], k.out_bias[:, 0:1], None,
                                      ALU.add).then_inc(sem["added"], 1)
                else:
                    dve.tensor_tensor(k.yT[:, b, :], k.yT[:, b, :], k.ps[:, 7, :],
                                      ALU.add).then_inc(sem["added"], 1)

            def body(h, b, first, last):
                u = 4 * h + b
                some1, some2 = not first or b >= 1, not first or b >= 2
                more = not last or b < B - 1
                nb, nh = (b + 1) % B, h if b < B - 1 else h + 1
                b1 = (b + 3) % B
                if some1:
                    invert(4 * u - 1, 3, some2)
                    low_turned(u - 1, b1, 1)
                maximum(4 * u, 0)
                if more:
                    low_q(u + 1, nh, nb)
                invert(4 * u, 0, some1)
                if some1:
                    low_turned(u - 1, b1, 2)
                maximum(4 * u + 1, 1)
                if more:
                    low_k(u + 1, nh, nb)
                invert(4 * u + 1, 1, some1)
                if some1:
                    low_turned(u - 1, b1, 3)
                maximum(4 * u + 2, 2)
                if some2:
                    add_output(u - 2, (b + 2) % B, first or (isinstance(h, int) and h == 1 and b < 2))
                if some1:
                    low_turned(u - 1, b1, 4)
                invert(4 * u + 2, 2, some1)
                low_turned(u, b, 0)
                maximum(4 * u + 3, 3)

            low_q(0, 0, 0)
            low_k(0, 0, 0)
            for h in (0, 1):
                for b in range(B):
                    body(h, b, h == 0, False)
            with dve.Fori(2, XH - 1) as i:
                for b in range(B):
                    body(i, b, False, False)
            for b in range(B):
                body(XH - 1, b, False, True)
            invert(4 * U - 1, 3, True)
            for q in (1, 2, 3, 4):
                low_turned(U - 1, B - 1, q)
            add_output(U - 2, (U - 2) % B, False)
            add_output(U - 1, B - 1, False)



def xattn1_out(nc, k):
    with ExitStack() as ctx:
        m = Stage(nc, ctx, "f0_", k)
        n = Norm(m, "norm")
        r = Route(m, 32, 6, 8)
        names = ["outT", "x_ready", "in_psum", "x32_ready", "high_ready"]
        sem = {x: m.sem(x) for x in names}
        block = ctx.enter_context(nc.Block())

        @block.gpsimd
        def _(pool):
            m.clear_last(pool)
            for b in range(B):
                norm_rstd(pool, k, n, b)

        @block.vector
        def _(dve):
            for b in range(B):
                at = slice(b * QT, (b + 1) * QT)
                dve.wait_ge(sem["outT"], b + 1)
                dve.tensor_tensor(k.x[:, at, :], k.x[:, at, :],
                                  k.ps[:, b, :].rearrange("p (q d) -> p q d", d=D),
                                  ALU.add).then_inc(sem["x_ready"], 1)
            norm_all(dve, n, k.x, lambda b: dve.wait_ge(sem["x_ready"], b + 1))
            for b in range(B):
                dve.wait_ge(sem["high_ready"], b + 1)
                dve.tensor_tensor(k.x_low[:, b, :], k.xT32[:, b, :], k.x_high[:, b, :],
                                  ALU.subtract).then_inc(k.f_x_ready, 1)
            route_vector(dve, k, r)

        @block.tensor
        def _(pe):
            for b in range(B):
                for q in range(QT):
                    last = pe.transpose(k.ps[:, b, q * P:(q + 1) * P], k.yT[:, b, q * P:(q + 1) * P], k.ident[:, :])
                last.then_inc(sem["outT"], 1)
            for b in range(B):
                pe.wait_ge(n.ready, b + 1)
                pe.wait_ge(sem["x_ready"], b + 1)
                transpose_batch(pe, k, n.out, b, b).then_inc(sem["in_psum"], 1)
            pe.wait_ge(k.w_loaded["f"], 16)
            for b in range(B):
                pe.wait_ge(sem["x32_ready"], b + 1)
                route_tensor_logits(pe, k, r, weight(k, "f_gate"), k.xT32, b, 4 + b)
            pe.wait_ge(r.parts_ready, 1)
            for b in range(B):
                pe.wait_ge(sem["high_ready"], b + 1)
                route_tensor_turn(pe, k, r, b, b)

        @block.scalar
        def _(act):
            for b in range(B):
                act.wait_ge(sem["in_psum"], b + 1)
                act.copy(k.xT32[:, b, :], k.ps[:, b, :]).then_inc(sem["x32_ready"], 1)
                act.copy(k.x_high[:, b, :], k.ps[:, b, :]).then_inc(sem["high_ready"], 1)
            for b in range(B):
                route_scalar_scores(act, k, r, b, 4 + b)
            for b in range(B):
                act.wait_ge(r.turned, b + 1)
                act.copy(k.routeT[0:ROUTE_ROWS, b, :],
                         k.ps[:, b, :].bitcast(BF16)[0:ROUTE_ROWS, 0:S]).then_inc(k.f_route_ready, 1)


def dump_x(nc, k):
    with ExitStack() as ctx:
        m = Stage(nc, ctx, "dump", k)
        stored = m.sem("stored")
        block = ctx.enter_context(nc.Block())

        @block.sync
        def _(sp):
            sp.dma_start(k.out_dram.rearrange("b (q p) d -> p (b q) d", p=P), k.x[:, :, :]).then_inc(stored, 16)
            sp.wait_ge(stored, 16)


def decoder(nc, x, ctx_token, ctxT, side, w, cols, rows, ident, ident16, sel, out, stop_after=99):
    k = Kept()
    k.stage = 0
    k.x_dram, k.ctx_dram, k.ctxT_dram, k.side_dram = x, ctx_token, ctxT, side
    k.w_dram, k.cols_dram, k.rows_dram, k.ident_dram = w, cols, rows, ident
    k.ident16_dram, k.sel_dram, k.out_dram = ident16.bitcast(BF16), sel.bitcast(BF16), out
    k.scratch = nc.dram_tensor("split_scratch", [2, B, PARTS, P, S], BF16).ap()
    with ExitStack() as ctx:
        m = Memory(nc, ctx, "k_")
        k.ps = ctx.enter_context(nc.psum_tensor("banks", [P, 8, S], F32))
        k.x = m.sb("x", [P, T, D])
        k.w = m.sb("w", [P, W_COLS])
        k.cols = m.sb("cols", [P, N_COL])
        k.rows = m.sb("rows", [P, N_ROW])
        k.ident = m.sb("ident", [P, P])
        k.ident16 = m.sb("ident16", [P, P], BF16)
        k.sel = m.sb("sel", [P, 17, D], BF16)
        k.minus_half = m.sb("minus_half", [P, QT])
        k.x_loaded = [m.sem(f"x_loaded{b}") for b in range(B)]
        k.w_loaded = {x: m.sem("w_loaded_" + x) for x in ("ab", "cd", "e", "f")}
        k.small_loaded, k.side_loaded = m.sem("small_loaded"), m.sem("side_loaded")
        k.constants_set, k.passed = m.sem("constants_set"), m.sem("passed")
        k.c_x_ready, k.c_route_ready, k.v_ready = m.sem("c_x_ready"), m.sem("c_route_ready"), m.sem("v_ready")
        k.f_x_ready, k.f_route_ready, k.kv_ready = m.sem("f_x_ready"), m.sem("f_route_ready"), m.sem("kv_ready")
        k.media = m.sb("media", [P, B, D])
        k.media_loaded = m.sem("media_loaded")
        k.d_stored = [m.sem(f"d_stored{b}") for b in range(B)]
        k.d_loaded = m.sem("d_loaded")
        k.a_stored = [m.sem(f"a_stored{b}") for b in range(B)]
        k.a_loaded = [m.sem(f"a_loaded{b}") for b in range(B)]
        with ExitStack() as layer:
            l = Memory(nc, layer, "l0_")
            k.ctxT = l.sb("ctxT", [P, B * C])
            k.ctx_kT = l.sb("ctx_kT", [P, B * C])
            k.ctx_v = l.sb("ctx_v", [P, B, D])
            k.side = l.sb("side", [P, T, C])
            k.vT = l.sb("vT", [P, B, S])
            k.exp_sum = l.sb("exp_sum", [P, B * H, QT])
            with ExitStack() as stacks:
                st = Memory(nc, stacks, "a_")
                k.q_stack = st.sb("q_stack", [P, 2, H, S], BF16)
                k.k_stack = st.sb("k_stack", [P, 2, H, S], BF16)
                attn0_project(nc, k)
                attn0_heads(nc, k)
            k.x_high = l.sb("x_high", [P, B, S], F32R)
            k.x_low = l.sb("x_low", [P, B, S], F32R)
            k.routeT = l.sb("routeT", [P, B, S], BF16)
            with ExitStack() as wide:
                k.xT32 = Memory(nc, wide, "l0_").sb("xT32", [P, B, S])
                attn0_out_xattn0(nc, k)
            if stop_after == 1:
                return dump_x(nc, k)
            moe(nc, k, "c_", "c_gu", "c_down", 9, False)
        if stop_after == 2:
            return dump_x(nc, k)
        with ExitStack() as layer:
            l = Memory(nc, layer, "l1a_")
            k.exp_sum = l.sb("exp_sum", [P, B * H, QT])
            k.attended = l.sb("attended", [P, B, S])
            with ExitStack() as stacks:
                st = Memory(nc, stacks, "d_")
                k.v_padded = st.sb("v_padded", [P, B, NK // P, 4 * (D + HD)])
                k.q_stack = st.sb("q_stack", [P, 2, H, S], BF16)
                k.k_stack = st.sb("k_stack", [P, 2, H, NK], BF16)
                attn1_project(nc, k)
                attn1_heads(nc, k)
            with ExitStack() as cross:
                e = Memory(nc, cross, "l1b_")
                k.kvT_high = e.sb("kvT_high", [P, B, KV + 1], F32R)
                k.kvT_low = e.sb("kvT_low", [P, B, KV + 1], F32R)
                k.kv_high = e.sb("kv_high", [P, B, KT, D], F32R)
                k.kv_low = e.sb("kv_low", [P, B, KT, D], F32R)
                k.w_vo = weight(k, "e_vT").rearrange("p (h d) -> p h d", h=XH)
                k.out_bias = e.sb("out_bias", [P, 1])
                k.yT = k.attended
                attn1_out_latents(nc, k)
                if stop_after == 3:
                    return dump_x(nc, k)
                xattn1_heads(nc, k)
            k.x_high = l.sb("x_high", [P, B, S], F32R)
            k.x_low = l.sb("x_low", [P, B, S], F32R)
            k.routeT = l.sb("routeT", [P, B, S], BF16)
            with ExitStack() as wide:
                k.xT32 = Memory(nc, wide, "l1_").sb("xT32", [P, B, S])
                xattn1_out(nc, k)
            if stop_after == 4:
                return dump_x(nc, k)
            moe(nc, k, "f_", "f_gu", "f_down", 17, True)


def pack(i):

    f = {n: np.asarray(a) for n, a in i.items()}

    def pad(a, n, axis):
        shape = list(a.shape)
        shape[axis] = n - a.shape[axis]
        return np.concatenate([a, np.zeros(shape, a.dtype)], axis)

    def pairs_gu(gate, up, shared_gate, shared_up):
        e = gate.shape[0]
        g = gate.reshape(e // 2, 2, D, -1).transpose(2, 0, 1, 3).reshape(D, e // 2, D)
        u = up.reshape(e // 2, 2, D, -1).transpose(2, 0, 1, 3).reshape(D, e // 2, D)
        g = np.concatenate([pad(shared_gate, D, 1)[:, None], g], 1)
        u = np.concatenate([pad(shared_up, D, 1)[:, None], u], 1)
        return np.stack([g, u], 2).reshape(D, -1)

    def pairs_down(down, shared):
        e = down.shape[0]
        d = down.reshape(e // 2, D, D).transpose(1, 0, 2)
        return np.concatenate([pad(shared, D, 0)[:, None], d], 1).reshape(D, -1)

    gu, wkv = f["L1_ffn_experts_gate_up"], f["L1_xattn_Wkv"]
    inner = XH * D
    d_out = f["L1_attn_out_w"].T.reshape(4, 4, HD, D).transpose(1, 0, 2, 3).reshape(D, D)
    w_in = f["L0_attn_w_in"].reshape(H, 3, HD, D).transpose(1, 0, 2, 3)
    b_in = f["L0_attn_b_in"].reshape(H, 3, HD).transpose(1, 0, 2).reshape(-1)
    w = {
        "a_qkv": w_in.reshape(3 * D, D).T, "a_out": f["L0_attn_w_out"].T,
        "b_q": f["L0_xattn_Wq"].T, "b_k": f["L0_xattn_Wk"].T, "b_v": f["L0_xattn_Wv"].T,
        "c_gate": f["L0_ffn_gate_w"].T,
        "c_gu": pairs_gu(f["L0_ffn_w_gate"], f["L0_ffn_w_up"], f["L0_ffn_ws_gate"], f["L0_ffn_ws_up"]),
        "c_down": pairs_down(f["L0_ffn_w_down"], f["L0_ffn_ws_down"]),
        "d_q": f["L1_attn_q_w"].T, "d_k": f["L1_attn_k_w"].T, "d_v": f["L1_attn_v_w"].T, "d_out": d_out,
        "e_q": f["L1_xattn_Wq"], "e_k": wkv[:, 0:inner],
        "e_vT": wkv[:, inner:].reshape(D, XH, D).transpose(2, 1, 0).reshape(D, -1),
        "e_o": f["L1_xattn_Wo"].reshape(XH, D, D).transpose(1, 0, 2).reshape(D, -1),
        "f_gate": f["L1_ffn_gate_weight"].T,
        "f_gu": pairs_gu(gu[:, 0:64].transpose(0, 2, 1), gu[:, 64:].transpose(0, 2, 1),
                         f["L1_ffn_shared_gate_w"].T, f["L1_ffn_shared_up_w"].T),
        "f_down": pairs_down(f["L1_ffn_experts_down"].transpose(0, 2, 1), f["L1_ffn_shared_down_w"].T),
    }
    bkv = f["L1_xattn_bkv"]
    c = {
        "a_bq": b_in[0:D], "a_bk": b_in[D:2 * D], "a_bv": b_in[2 * D:], "b_bq": f["L0_xattn_bq"],
        "b_bk": f["L0_xattn_bk"], "d_bq": f["L1_attn_q_b"], "d_bk": f["L1_attn_k_b"],
        "conv_w": f["L1_attn_conv_w"].reshape(D, 3).T, "conv_b": f["L1_attn_conv_b"],
        "g_lat": f["L1_xattn_gamma_lat"], "b_lat": f["L1_xattn_beta_lat"],
        "g_med": f["L1_xattn_gamma_media"], "b_med": f["L1_xattn_beta_media"], "e_bo": f["L1_xattn_bo"],
        "e_bq": f["L1_xattn_bq"], "e_bk": bkv[0:inner], "e_bv": bkv[inner:],
    }
    r = {
        "a_bo": f["L0_attn_b_out"], "b_bv": f["L0_xattn_bv"], "d_bv": f["L1_attn_v_b"], "d_bo": f["L1_attn_out_b"],
        "g_lat": c["g_lat"], "b_lat": c["b_lat"], "g_med": c["g_med"], "b_med": c["b_med"],
        "e_score": f["L1_ffn_e_score_correction_bias"],
        "betas": np.stack([f["L0_xattn_beta_risk"], f["L0_xattn_beta_prio"], f["L0_xattn_beta_impl"]]),
        "iota": np.arange(32, dtype=np.float32),
    }
    sel = np.zeros((P, 17, D), np.uint16)
    for part in range(PARTS):
        sel[part * SLOT_E + SLOT_E - 1, 0, :] = BF16_ONE
        for e in range(32):
            sel[part * SLOT_E + e, 1 + e // 2, 64 * (e % 2):64 * (e % 2) + 64] = BF16_ONE
    return {
        "x": f["x"], "ctx_token": f["ctx_1024"],
        "ctxT": f["ctx_1024"].transpose(2, 0, 1).reshape(D, B * C), "side": f["fside_BxSxS2_0"],
        "w": np.concatenate([w[n].reshape(D, -1) for n in COLS], 1),
        "cols": np.concatenate([c[n].reshape(-1, D) for n in COL], 0).T,
        "rows": np.concatenate([r[n].reshape(-1) for n in ROW]),
        "ident": np.eye(P, dtype=np.float32), "ident16": np.diag(np.full(P, BF16_ONE, np.uint16)), "sel": sel,
    }


def kernel(**inputs):
    import concourse.bacc as bacc
    from concourse.bass_utils import run_bass_kernel_spmd

    nc = bacc.Bacc("TRN2", target_bir_lowering=False, num_devices=1)
    arrays, args = {}, []
    for name, a in pack(inputs).items():
        a = np.ascontiguousarray(a)
        arrays[f"in_{name}"] = a
        args.append(nc.dram_tensor(f"in_{name}", a.shape, mybir.dt.from_np(a.dtype), kind="ExternalInput").ap())
    args.append(nc.dram_tensor("out", (B, S, D), F32, kind="ExternalOutput").ap())
    decoder(nc, *args)
    return run_bass_kernel_spmd(nc, [arrays], core_ids=[0]).results[0]["out"]
```

```python
from contextlib import ExitStack

import numpy as np

import concourse.bass as bass
from concourse import mybir

F32 = mybir.dt.float32
F32R = mybir.dt.float32r
BF16 = mybir.dt.bfloat16
ACT = mybir.ActivationFunctionType
ALU = mybir.AluOpType
AX_X = mybir.AxisListType.X

P = 128
B = 4
S = 512
D = 128
QT = S // P
T = B * QT
C = 77
H = 16
HD = D // H
XH = 8
NK = S // 2
KV = S + C
KT = KV // P + 1
EPS = 1e-5
BF16_ONE = 0x3F80
PARTS = 3
TERMS_Q = [0, 0, 0, 1, 1, 2]
TERMS_K = [0, 1, 2, 0, 1, 0]
KROWS = 96
SLOT_E = 32
ROUTE_ROWS = PARTS * SLOT_E

COLS = {}
_n = 0
for _name, _w in [("a_qkv", 3 * D), ("a_out", D), ("b_q", D), ("b_k", D), ("b_v", D), ("c_gate", 16),
                  ("c_gu", 9 * 2 * D), ("c_down", 9 * D), ("d_q", D), ("d_k", D), ("d_v", D), ("d_out", D),
                  ("e_q", XH * D), ("e_k", XH * D), ("e_vT", XH * D), ("e_o", XH * D), ("f_gate", 32),
                  ("f_gu", 17 * 2 * D), ("f_down", 17 * D)]:
    COLS[_name] = (_n, _n + _w)
    _n += _w
W_COLS = _n
COL = {}
for _name, _w in [("a_bq", 1), ("a_bk", 1), ("a_bv", 1), ("b_bq", 1), ("b_bk", 1), ("d_bq", 1), ("d_bk", 1),
                  ("conv_w", 3), ("conv_b", 1), ("g_lat", 1), ("b_lat", 1), ("g_med", 1), ("b_med", 1),
                  ("e_bo", 1), ("e_bq", XH), ("e_bk", XH), ("e_bv", XH)]:
    COL[_name] = (sum(w for _, w in COL.values()), _w)
N_COL = sum(w for _, w in COL.values())
ROW = {}
for _name, _w in [("a_bo", D), ("b_bv", D), ("d_bv", D), ("d_bo", D), ("g_lat", D), ("b_lat", D),
                  ("g_med", D), ("b_med", D), ("e_score", 32), ("betas", 3)]:
    ROW[_name] = (sum(w for _, w in ROW.values()), _w)
N_ROW = sum(w for _, w in ROW.values())


class Memory:

    def __init__(self, nc, ctx, prefix):
        self.nc, self.ctx, self.prefix = nc, ctx, prefix

    def sb(self, name, shape, dt=F32):
        return self.ctx.enter_context(self.nc.sbuf_tensor(self.prefix + name, shape, dt))

    def sem(self, name):
        return self.ctx.enter_context(self.nc.semaphore(self.prefix + name))


STAGE_SEMS = 55
SEM_SETS = [range(256 - 2 * STAGE_SEMS, 256 - STAGE_SEMS), range(256 - STAGE_SEMS, 256)]


class Stage(Memory):

    def __init__(self, nc, ctx, prefix, k):
        super().__init__(nc, ctx, prefix)
        self.ids = iter(SEM_SETS[k.stage % 2])
        self.last_set = SEM_SETS[(k.stage + 1) % 2] if k.stage else None
        k.stage += 1

    def sem(self, name):
        return self.ctx.enter_context(self.nc.semaphore(self.prefix + name, next(self.ids)))

    def clear_last(self, pool):
        if self.last_set:
            pool.sem_clear(self.last_set)


class Kept:
    pass


def wait_apart(eng, k, sem, value):
    eng.wait_ge(sem, value)
    eng.sem_inc(k.passed, 1)


def col(k, name, i=0, rows=P):
    at = COL[name][0] + i
    return k.cols[0:rows, at:at + 1]


def row(k, name, rows=P):
    at, w = ROW[name]
    return k.rows[0:rows, at:at + w]


def weight(k, name):
    a, b = COLS[name]
    return k.w[:, a:b]



class Norm:

    def __init__(self, m, name, batches=B, tiles=QT, rows=P):
        self.tiles, self.rows = tiles, rows
        n = batches * tiles
        self.stats = m.sb(name + "_stats", [P, n, 6])
        self.mv = m.sb(name + "_mean_var", [P, n, 2])
        self.var_eps = m.sb(name + "_var_eps", [P, n])
        self.rstd = m.sb(name + "_rstd", [P, n])
        self.minus_mean = m.sb(name + "_minus_mean", [P, n])
        self.shift = m.sb(name + "_shift", [P, n])
        self.out = m.sb(name + "_normed", [P, n, D])
        self.stats_done = m.sem(name + "_stats_done")
        self.aggregated = m.sem(name + "_aggregated")
        self.var_ready = m.sem(name + "_var_ready")
        self.rstd_ready = m.sem(name + "_rstd_ready")
        self.shift_ready = m.sem(name + "_shift_ready")
        self.ready = m.sem(name + "_ready")
        self.scalar_ready = m.sem(name + "_scalar_ready")

    def wait_ready(self, eng, b):
        eng.wait_ge(self.ready, b + 1)
        if self.tiles > 1:
            eng.wait_ge(self.scalar_ready, b + 1)


def norm_statistics(dve, n, x, b):
    r, tiles = n.rows, range(b * n.tiles, (b + 1) * n.tiles)
    for t in tiles:
        last = dve.bn_stats(n.stats[0:r, t, :], x[0:r, t, :])
    last.then_inc(n.stats_done, 1)
    dve.wait_ge(n.stats_done, b + 1)
    for t in tiles:
        last = dve.bn_aggr(n.mv[0:r, t, :], n.stats[0:r, t, :])
    last.then_inc(n.aggregated, 1)
    dve.wait_ge(n.aggregated, b + 1)
    at = slice(b * n.tiles, (b + 1) * n.tiles)
    if n.tiles > 1:
        dve.tensor_scalar(n.minus_mean[0:r, at], n.mv[0:r, at, 0], -1.0, None, ALU.mult)
    dve.tensor_scalar(n.var_eps[0:r, at], n.mv[0:r, at, 1], EPS, None, ALU.add).then_inc(n.var_ready, 1)


def norm_rstd(pool, k, n, b):
    r, at = n.rows, slice(b * n.tiles, (b + 1) * n.tiles)
    pool.wait_ge(n.var_ready, b + 1)
    pool.tensor_tensor(n.rstd[0:r, at], n.var_eps[0:r, at], k.minus_half[0:r, 0:n.tiles],
                       ALU.pow).then_inc(n.rstd_ready, 1)
    if n.tiles > 1:
        pool.wait_ge(n.rstd_ready, b + 1)
        pool.tensor_tensor(n.shift[0:r, at], n.minus_mean[0:r, at], n.rstd[0:r, at],
                           ALU.mult).then_inc(n.shift_ready, 1)


def scalar_tiles(n):
    return n.tiles - n.tiles // 2


def norm_scalar(act, n, x):
    for b in range(B):
        act.wait_ge(n.shift_ready, b + 1)
        for t in range(b * n.tiles + scalar_tiles(n), (b + 1) * n.tiles):
            last = act.activation(n.out[:, t, :], x[:, t, :], ACT.Identity, bias=n.shift[:, t:t + 1],
                                  scale=n.rstd[:, t:t + 1])
        last.then_inc(n.scalar_ready, 1)


def norm_apply(dve, n, x, b):
    r = n.rows
    dve.wait_ge(n.rstd_ready, b + 1)
    for t in range(b * n.tiles, b * n.tiles + scalar_tiles(n)):
        last = dve.tensor_scalar(n.out[0:r, t, :], x[0:r, t, :], n.mv[0:r, t, 0:1], n.rstd[0:r, t:t + 1],
                                 ALU.subtract, ALU.mult)
    last.then_inc(n.ready, 1)


def norm_all(dve, n, x, waits=None):
    for b in range(B):
        if waits:
            waits(b)
        norm_statistics(dve, n, x, b)
    for b in range(B):
        norm_apply(dve, n, x, b)


def transpose_batch(pe, k, src, b, bank):
    for q in range(QT):
        last = pe.transpose(k.ps[:, bank, q * P:(q + 1) * P], src[:, b * QT + q, :], k.ident[:, :])
    return last



RING = 4
PARTS_RING = 6


class Split:

    def __init__(self, m):
        self.full = m.sb("split_full", [P, RING, S])
        self.rest = m.sb("split_rest", [P, RING, S])
        self.parts = m.sb("split_parts", [P, PARTS_RING, PARTS, S], BF16)
        self.full_ready = m.sem("split_full_ready")
        self.high_ready = m.sem("split_high_ready")
        self.rest_ready = m.sem("split_rest_ready")
        self.mid_ready = m.sem("split_mid_ready")
        self.low_ready = m.sem("split_low_ready")


def split_scalar(act, s, widths, stored):
    for i in range(2 * B + 1):
        if i < 2 * B:
            w = widths[i % 2]
            act.wait_ge(s.full_ready, i + 1)
            if i >= PARTS_RING:
                act.wait_ge(stored[(i - PARTS_RING) // 2], 32)
            act.copy(s.parts[:, i % PARTS_RING, 0, 0:w], s.full[:, i % RING, 0:w]).then_inc(s.high_ready, 1)
        if i >= 1:
            j, w = i - 1, widths[(i - 1) % 2]
            act.wait_ge(s.rest_ready, j + 1)
            act.copy(s.parts[:, j % PARTS_RING, 1, 0:w], s.rest[:, j % RING, 0:w]).then_inc(s.mid_ready, 1)


def split_vector(dve, s, widths, make_full):
    for i in range(2 * B + 3):
        if i < 2 * B:
            if i >= RING:
                dve.wait_ge(s.rest_ready, i - RING + 1)
            make_full(i, s.full[:, i % RING, 0:widths[i % 2]]).then_inc(s.full_ready, 1)
        if 1 <= i <= 2 * B:
            j, w = i - 1, widths[(i - 1) % 2]
            dve.wait_ge(s.high_ready, j + 1)
            if j >= RING:
                dve.wait_ge(s.low_ready, j - RING + 1)
            dve.tensor_tensor(s.rest[:, j % RING, 0:w], s.full[:, j % RING, 0:w], s.parts[:, j % PARTS_RING, 0, 0:w],
                              ALU.subtract).then_inc(s.rest_ready, 1)
        if i >= 3:
            j, w = i - 3, widths[(i - 3) % 2]
            dve.wait_ge(s.mid_ready, j + 1)
            dve.tensor_tensor(s.parts[:, j % PARTS_RING, 2, 0:w], s.rest[:, j % RING, 0:w], s.parts[:, j % PARTS_RING, 1, 0:w],
                              ALU.subtract).then_inc(s.low_ready, 1)


def store_parts(sp, k, s, b, widths, stored):
    for i in (0, 1):
        sp.wait_ge(s.low_ready, 2 * b + i + 1)
        w = widths[i]
        sp.dma_start(k.scratch[i, b, :, :, 0:w].rearrange("c p t -> p c t"),
                     s.parts[:, (2 * b + i) % PARTS_RING, :, 0:w]).then_inc(stored[b], 16)


def load_stacks(sp, k, b, widths, stored, signal):
    sp.wait_ge(stored[b], 32)
    for term in range(len(TERMS_Q)):
        at = slice(HD * term, HD * (term + 1))
        for i, (stack, parts) in enumerate(((k.q_stack, TERMS_Q), (k.k_stack, TERMS_K))):
            w = widths[i]
            sp.dma_start(stack[at, b % 2, :, 0:w],
                         k.scratch[i, b, parts[term], :, 0:w].rearrange("(h d) t -> d h t", d=HD)
                         ).then_inc(signal, 16)


STACK_LOADED = 16 * 2 * len(TERMS_Q)



def load_weights(sp, k, name, lo, hi):
    sp.dma_start(k.w[:, lo:hi], k.w_dram[:, lo:hi]).then_inc(k.w_loaded[name], 16)


def attn0_project(nc, k):
    with ExitStack() as ctx:
        m = Stage(nc, ctx, "a_", k)
        n = Norm(m, "norm")
        s = Split(m)
        xT = n.out[:, :, :].rearrange("p (b q) d -> p b (q d)", b=B)
        in_psum, xT_ready = m.sem("x_in_psum"), m.sem("xT_ready")
        q_done, k_done, v_done = m.sem("q_done"), m.sem("k_done"), m.sem("v_done")
        ctx_done, ctx_copied, zeroed = m.sem("ctx_done"), m.sem("ctx_copied"), m.sem("zeroed")
        block = ctx.enter_context(nc.Block())
        scale = float(HD) ** -0.5
        wa = weight(k, "a_qkv")

        @block.sync
        def _(sp):
            x_dram = k.x_dram.rearrange("b (q p) d -> p (b q) d", p=P)
            for b in range(B):
                sp.dma_start(k.x[:, b * QT:(b + 1) * QT, :], x_dram[:, b * QT:(b + 1) * QT, :]
                             ).then_inc(k.x_loaded[b], 16)
            sp.dma_start(k.ident[:, :], k.ident_dram).then_inc(k.small_loaded, 16)
            sp.dma_start(k.cols[:, :], k.cols_dram).then_inc(k.small_loaded, 16)
            sp.dma_start(k.rows[:, :], k.rows_dram.partition_broadcast(P)).then_inc(k.small_loaded, 16)
            sp.dma_start(k.ctxT[:, :], k.ctxT_dram).then_inc(k.small_loaded, 16)
            load_weights(sp, k, "ab", 0, COLS["c_gate"][0])
            for b in range(B):
                store_parts(sp, k, s, b, (S, S), k.a_stored)
                if b == 0:
                    sp.wait_ge(zeroed, 2)
                    load_stacks(sp, k, 0, (S, S), k.a_stored, k.a_loaded[0])

        @block.gpsimd
        def _(pool):
            m.clear_last(pool)
            pool.memset(k.minus_half[:, :], -0.5).then_inc(k.constants_set, 1)
            pool.wait_ge(k.constants_set, 1)
            for b in range(B):
                norm_rstd(pool, k, n, b)
            for b in range(2):
                pool.memset(k.q_stack[0:KROWS, b, :, :].bitcast(F32), 0.0).then_inc(zeroed, 1)
                pool.memset(k.k_stack[0:KROWS, b, :, :].bitcast(F32), 0.0).then_inc(zeroed, 1)

        @block.vector
        def _(dve):
            for i in range(B + 1):
                if i < B:
                    dve.wait_ge(k.x_loaded[i], 16)
                    norm_statistics(dve, n, k.x, i)
                if i >= 1:
                    norm_apply(dve, n, k.x, i - 1)
            dve.wait_ge(ctx_done, 2)
            dve.tensor_tensor(k.ctx_v[0:C, :, :], k.ps[0:C, 7, :].rearrange("c (b d) -> c b d", b=B),
                              row(k, "b_bv", C).unsqueeze(1).broadcast_to([C, B, D]),
                              ALU.add).then_inc(ctx_copied, 1)

            def full(i, out):
                b = i // 2
                if i % 2 == 0:
                    dve.wait_ge(q_done, b + 1)
                    return dve.tensor_scalar(out, k.ps[:, 4 + b, :], col(k, "a_bq"), scale,
                                             ALU.add, ALU.mult)
                dve.wait_ge(k_done, b + 1)
                return dve.tensor_scalar(out, k.ps[:, b, :], col(k, "a_bk"), None, ALU.add)

            split_vector(dve, s, (S, S), full)

        @block.tensor
        def _(pe):
            pe.wait_ge(k.small_loaded, 64)
            pe.wait_ge(k.w_loaded["ab"], 16)
            pe.matmul(k.ps[:, 6, 0:B * C], weight(k, "b_k"), k.ctxT[:, :], start=True,
                      stop=True).then_inc(ctx_done, 1)
            for b in range(B):
                last = pe.matmul(k.ps[0:C, 7, b * D:(b + 1) * D], k.ctxT[:, b * C:(b + 1) * C],
                                 weight(k, "b_v"), start=True, stop=True)
            last.then_inc(ctx_done, 1)
            for i in range(B + 1):
                if i < B:
                    n.wait_ready(pe, i)
                    transpose_batch(pe, k, n.out, i, i).then_inc(in_psum, 1)
                if i == 0:
                    continue
                b = i - 1
                if b == 2:
                    pe.wait_ge(ctx_copied, 2)
                pe.wait_ge(xT_ready, b + 1)
                pe.matmul(k.ps[:, 4 + b, :], wa[:, 0:D], xT[:, b, :], start=True, stop=True).then_inc(q_done, 1)
                pe.matmul(k.ps[:, b, :], wa[:, D:2 * D], xT[:, b, :], start=True, stop=True).then_inc(k_done, 1)
            for b in range(B):
                pe.wait_ge(s.full_ready, 2 * b + 1)
                pe.matmul(k.ps[:, 4 + b, :], wa[:, 2 * D:3 * D], xT[:, b, :], start=True,
                          stop=True).then_inc(v_done, 1)

        @block.scalar
        def _(act):
            norm_scalar(act, n, k.x)
            act.wait_ge(ctx_done, 1)
            act.activation(k.ctx_kT[:, :], k.ps[:, 6, 0:B * C], ACT.Identity,
                           bias=col(k, "b_bk")).then_inc(ctx_copied, 1)
            for b in range(B):
                act.wait_ge(in_psum, b + 1)
                act.copy(xT[:, b, :], k.ps[:, b, :]).then_inc(xT_ready, 1)
            split_scalar(act, s, (S, S), k.a_stored)
            for b in range(B):
                act.wait_ge(v_done, b + 1)
                act.activation(k.vT[:, b, :], k.ps[:, 4 + b, :], ACT.Identity,
                               bias=col(k, "a_bv")).then_inc(k.v_ready, 1)



def attn0_heads(nc, k):
    with ExitStack() as ctx:
        m = Stage(nc, ctx, "ah_", k)
        minus_max = m.sb("minus_max", [P, B * H, QT])
        scored, max_ready, slots_free = m.sem("scored"), m.sem("max_ready"), m.sem("slots_free")
        stack_used = m.sem("stack_used")
        block = ctx.enter_context(nc.Block())
        PAIRS = H // 2

        @block.gpsimd
        def _(pool):
            m.clear_last(pool)

        @block.sync
        def _(sp):
            load_stacks(sp, k, 1, (S, S), k.a_stored, k.a_loaded[1])
            sp.dma_start(k.side[:, :, :], k.side_dram.rearrange("b (q p) c -> p (b q) c", p=P)
                         ).then_inc(k.side_loaded, 16)
            sp.dma_start(k.sel[:, :, :], k.sel_dram).then_inc(k.side_loaded, 16)
            sp.dma_start(k.ident16[:, :], k.ident16_dram).then_inc(k.side_loaded, 16)
            sp.dma_start(k.media[0:C, :, :], k.ctx_dram.rearrange("b c d -> c b d")
                         ).then_inc(k.media_loaded, 16)
            load_weights(sp, k, "cd", COLS["c_gate"][0], COLS["e_q"][0])
            load_weights(sp, k, "e", COLS["e_q"][0], COLS["f_gate"][0])
            load_weights(sp, k, "f", COLS["f_gate"][0], W_COLS)
            for b in range(2, B):
                sp.wait_ge(stack_used, b - 1)
                load_stacks(sp, k, b, (S, S), k.a_stored, k.a_loaded[b])

        @block.tensor
        def _(pe):
            for b in range(B):
                pe.wait_ge(k.a_loaded[b], STACK_LOADED)
                with pe.Fori(0, PAIRS) as pair:
                    for i in range(4):
                        half = (b * PAIRS + pair) * 4 + i
                        head = pair * 2 + i // 2
                        pe.wait_ge(slots_free, half + 1)
                        for j in range(2):
                            q = 2 * (i % 2) + j
                            last = pe.matmul(k.ps[:, 2 * i + j, :],
                                             k.q_stack[0:KROWS, b % 2, bass.ds(head, 1), q * P:(q + 1) * P]
                                             .rearrange("p a t -> p (a t)"),
                                             k.k_stack[0:KROWS, b % 2, bass.ds(head, 1), :]
                                             .rearrange("p a t -> p (a t)"),
                                             start=True, stop=True)
                        last.then_inc(scored, 1)
                pe.wait_ge(scored, (b + 1) * PAIRS * 4)
                pe.sem_inc(stack_used, 1)

        @block.vector
        def _(dve):
            with dve.Fori(0, B * PAIRS) as pair:
                for i in range(4):
                    dve.wait_ge(scored, pair * 4 + i + 1)
                    dve.tensor_reduce(minus_max[:, bass.ds(pair * 2 + i // 2, 1), 2 * (i % 2):2 * (i % 2) + 2]
                                      .rearrange("p a q -> p (a q)"),
                                      k.ps[:, 2 * i:2 * i + 2, :], AX_X, ALU.max,
                                      negate=True).then_inc(max_ready, 1)

        @block.scalar
        def _(act):
            act.sem_inc(slots_free, 4)
            with act.Fori(0, B * PAIRS) as pair:
                for i in range(4):
                    head = pair * 2 + i // 2
                    wait_apart(act, k, max_ready, pair * 4 + i + 1)
                    for j in range(2):
                        q = 2 * (i % 2) + j
                        last = act.activation(k.ps[:, 2 * i + j, :], k.ps[:, 2 * i + j, :], ACT.Exp,
                                              bias=minus_max[:, bass.ds(head, 1), q:q + 1]
                                              .rearrange("p a q -> p (a q)"),
                                              accum_out=k.exp_sum[:, bass.ds(head, 1), q:q + 1]
                                              .rearrange("p a q -> p (a q)"))
                    last.then_inc(slots_free, 1)



SENTINEL, REPLACED = -3.0e38, -3.2e38

def scores_width(experts, top):
    return experts + 8 - top


class Scores:

    def __init__(self, m, k, experts):
        self.experts, self.scores = experts, k.route_scores
        self.logits_ready = m.sem("logits_ready")
        self.scores_ready = m.sem("route_scores_ready")


class Route:
    def __init__(self, m, k, experts, top, groups):
        self.experts, self.top, self.groups = experts, top, groups
        self.scores = k.route_scores
        e = experts
        self.ready = m.sem("route_ready")
        self.step = m.sem("route_step")
        self.parts_ready = m.sem("route_parts_ready")
        self.turned = m.sem("route_turned")
        self.ranked = m.sb("ranked", [P, T, scores_width(e, top)])
        self.best = m.sb("best", [P, T, 8])
        self.replaced = m.sb("replaced", [P, T, scores_width(e, top)])
        self.mask = m.sb("mask", [P, T, e])
        self.chosen = m.sb("chosen", [P, T, e])
        self.total = m.sb("total", [P, T])
        self.inverse = m.sb("route_inverse", [P, T])
        self.route = m.sb("route", [P, T, SLOT_E])
        self.rest = m.sb("route_rest", [P, T, SLOT_E])
        self.parts = m.sb("route_parts", [P, T, PARTS, SLOT_E], BF16)
        if groups:
            self.group_score = m.sb("group_score", [P, T, scores_width(groups, groups // 2)])
            self.group_replaced = m.sb("group_replaced", [P, T, scores_width(groups, groups // 2)])
            self.group_mask = m.sb("group_mask", [P, T, groups])


def route_vector(dve, k, r):
    e, top = r.experts, r.top
    SCALE = 2.5
    done = [0]

    def step(last):
        done[0] += 1
        last.then_inc(r.step, 1)
        dve.wait_ge(r.step, done[0])

    def top_mask(values, n, count, replaced, mask):
        for t in range(T):
            last = dve.max(r.best[:, t, :], values[:, t, :])
        step(last)
        step(dve.memset(r.best[:, :, count:], SENTINEL))
        for t in range(T):
            last = dve.match_replace(replaced[:, t, :], r.best[:, t, :], values[:, t, :], REPLACED)
        step(last)
        step(dve.tensor_tensor(mask[:, :, :], values[:, :, 0:n], replaced[:, :, 0:n], ALU.not_equal))

    step(dve.memset(r.route[:, :, :], 0.0))
    values = r.ranked if r.groups else r.scores
    step(dve.memset(values[:, :, e:], SENTINEL))
    if r.groups:
        step(dve.memset(r.group_score[:, :, r.groups:], SENTINEL))
    if r.groups:
        size = e // r.groups
        ranked = r.ranked[:, :, 0:e]
        by_group = ranked.rearrange("p t (g s) -> p t g s", s=size)
        step(dve.tensor_tensor(ranked, r.scores[:, :, 0:e],
                               row(k, "e_score").unsqueeze(1).broadcast_to([P, T, e]), ALU.add))
        step(dve.tensor_reduce(r.group_score[:, :, 0:r.groups], by_group, AX_X, ALU.max))
        top_mask(r.group_score, r.groups, r.groups // 2, r.group_replaced, r.group_mask)
        step(dve.tensor_tensor(by_group, by_group,
                               r.group_mask[:, :, :].unsqueeze(3).broadcast_to([P, T, r.groups, size]), ALU.mult))
    top_mask(values, e, top, r.replaced, r.mask)
    step(dve.tensor_tensor(r.chosen[:, :, :], r.mask[:, :, :], r.scores[:, :, 0:e], ALU.mult))
    step(dve.tensor_reduce(r.total[:, :], r.chosen[:, :, :], AX_X, ALU.add))
    step(dve.tensor_scalar(r.total[:, :], r.total[:, :], 1e-20, None, ALU.add))
    step(dve.reciprocal(r.inverse[:, :], r.total[:, :]))
    step(dve.scalar_tensor_tensor(r.route[:, :, 0:e], r.chosen[:, :, :], SCALE,
                                  r.inverse[:, :].unsqueeze(2).broadcast_to([P, T, e]), ALU.mult, ALU.mult))
    step(dve.tensor_copy(r.parts[:, :, 0, :], r.route[:, :, :]))
    step(dve.tensor_tensor(r.rest[:, :, :], r.route[:, :, :], r.parts[:, :, 0, :], ALU.subtract))
    step(dve.tensor_copy(r.parts[:, :, 1, :], r.rest[:, :, :]))
    dve.tensor_tensor(r.parts[:, :, 2, :], r.rest[:, :, :], r.parts[:, :, 1, :],
                      ALU.subtract).then_inc(r.parts_ready, 1)


def route_tensor_logits(pe, k, r, gate, xT, b, bank):
    for q in range(QT):
        last = pe.matmul(k.ps[:, bank, q * r.experts:(q + 1) * r.experts], xT[:, b, q * P:(q + 1) * P],
                         gate, start=True, stop=True)
    last.then_inc(r.logits_ready, 1)


def route_scalar_scores(act, k, r, b, bank):
    act.wait_ge(r.logits_ready, b + 1)
    act.activation(r.scores[:, b * QT:(b + 1) * QT, 0:r.experts],
                   k.ps[:, bank, 0:QT * r.experts].rearrange("p (q e) -> p q e", q=QT),
                   ACT.Sigmoid).then_inc(r.scores_ready, 1)


def route_tensor_turn(pe, k, r, b, bank):
    out = k.ps[:, bank, :].bitcast(BF16)
    for q in range(QT):
        last = pe.transpose(out[0:ROUTE_ROWS, q * P:(q + 1) * P],
                            r.parts[:, b * QT + q, :, :].rearrange("p c e -> p (c e)"), k.ident16[:, :])
    last.then_inc(r.turned, 1)



def attn0_out_xattn0(nc, k):
    with ExitStack() as ctx:
        m = Stage(nc, ctx, "b_", k)
        n, n2 = Norm(m, "norm"), Norm(m, "norm2")
        r = Scores(m, k, 16)
        inverse = m.sb("inverse", [P, B * H, QT])
        weight_sum = m.sb("weight_sum", [P, B * H, QT])
        wide = m.sb("wide", [P, T, D])
        attnT = wide[:, :, :].rearrange("p (b q) d -> p b (q d)", b=B)
        xT = n.out[:, :, :].rearrange("p (b q) d -> p b (q d)", b=B)
        qT = m.sb("qT", [P, B, S])
        scores = m.sb("x_scores", [P, T, C])
        minus_max = m.sb("minus_max", [P, T])
        probs = m.sb("probs", [P, T, C])
        exp_sum = m.sb("exp_sum", [P, T])
        x_inverse = m.sb("x_inverse", [P, T])
        probsT = m.sb("probsT", [P, B, S])
        beta = m.sb("beta", [P, 2])
        names = ["inv_ready", "sum_ready", "wide_ready", "sumT", "attn_ready", "projected", "x_ready", "biased",
                 "in_psum", "xT_ready", "q_done", "q_ready", "scored", "beta_ready", "scores_ready", "max_ready",
                 "exp_done", "probsT_done", "probsT_ready", "x_inv_ready", "attended", "x2_ready",
                 "in_psum2", "high_ready", "x32_ready"]
        sem = {x: m.sem(x) for x in names}
        block = ctx.enter_context(nc.Block())
        scale = float(D) ** -0.5

        @block.gpsimd
        def _(pool):
            m.clear_last(pool)
            for b in range(B):
                at = slice(b * QT, (b + 1) * QT)
                pool.tensor_tensor(k.x[:, at, :], k.x[:, at, :],
                                   row(k, "a_bo").unsqueeze(1).broadcast_to([P, QT, D]),
                                   ALU.add).then_inc(sem["biased"], 1)
            for b in range(B):
                norm_rstd(pool, k, n, b)
            pool.wait_ge(k.w_loaded["cd"], 16)
            split_first_units(pool, k, m, "c_")
            for b in range(B):
                norm_rstd(pool, k, n2, b)

        @block.vector
        def _(dve):
            at = ROW["betas"][0]
            dve.tensor_tensor(beta[:, 0:1], k.rows[:, at:at + 1], k.rows[:, at + 1:at + 2],
                              ALU.add).then_inc(sem["beta_ready"], 1)
            dve.reciprocal(inverse[:, :, :], k.exp_sum[:, :, :]).then_inc(sem["inv_ready"], 1)
            dve.wait_ge(sem["beta_ready"], 1)
            dve.tensor_tensor(beta[:, 1:2], beta[:, 0:1], k.rows[:, at + 2:at + 3],
                              ALU.subtract).then_inc(sem["beta_ready"], 1)
            dve.wait_ge(sem["inv_ready"], 1)
            dve.tensor_tensor(weight_sum[:, :, :], k.exp_sum[:, :, :], inverse[:, :, :],
                              ALU.mult).then_inc(sem["sum_ready"], 1)
            dve.wait_ge(sem["sum_ready"], 1)
            for b in range(B):
                dve.tensor_copy(wide[:, b * QT:(b + 1) * QT, :].rearrange("p q (h d) -> p q h d", d=HD),
                                weight_sum[:, b * H:(b + 1) * H, :].rearrange("p h q -> p q h").unsqueeze(3)
                                .broadcast_to([P, QT, H, HD])).then_inc(sem["wide_ready"], 1)
            for b in range(B):
                dve.wait_ge(sem["sumT"], b + 1)
                dve.tensor_tensor(attnT[:, b, :], k.vT[:, b, :], k.ps[:, b, :],
                                  ALU.mult).then_inc(sem["attn_ready"], 1)
            for b in range(B):
                at = slice(b * QT, (b + 1) * QT)
                dve.wait_ge(sem["projected"], b + 1)
                dve.wait_ge(sem["biased"], b + 1)
                dve.tensor_tensor(k.x[:, at, :], k.x[:, at, :],
                                  k.ps[:, 4 + b, :].rearrange("p (q d) -> p q d", d=D),
                                  ALU.add).then_inc(sem["x_ready"], 1)
            norm_all(dve, n, k.x, lambda b: dve.wait_ge(sem["x_ready"], b + 1))
            for b in range(B):
                dve.wait_ge(sem["q_done"], b + 1)
                dve.tensor_scalar(qT[:, b, :], k.ps[:, 4 + b, :], col(k, "b_bq"), scale, ALU.add,
                                  ALU.mult).then_inc(sem["q_ready"], 1)
            dve.wait_ge(k.side_loaded, 48)
            dve.wait_ge(sem["beta_ready"], 2)
            for b in range(B):
                at = slice(b * QT, (b + 1) * QT)
                dve.wait_ge(sem["scored"], b + 1)
                dve.scalar_tensor_tensor(scores[:, at, :], k.side[:, at, :], beta[:, 1:2],
                                         k.ps[:, b, 0:QT * C].rearrange("p (q c) -> p q c", q=QT),
                                         ALU.mult, ALU.add).then_inc(sem["scores_ready"], 1)
                dve.wait_ge(sem["scores_ready"], b + 1)
                dve.tensor_reduce(minus_max[:, at], scores[:, at, :], AX_X, ALU.max,
                                  negate=True).then_inc(sem["max_ready"], 1)
            for b in range(B):
                at = slice(b * QT, (b + 1) * QT)
                dve.wait_ge(sem["exp_done"], b + 1)
                dve.reciprocal(x_inverse[:, at], exp_sum[:, at]).then_inc(sem["x_inv_ready"], 1)
            for b in range(B):
                dve.wait_ge(sem["attended"], b + 1)
                dve.wait_ge(sem["x_inv_ready"], b + 1)
                for q in range(QT):
                    t = b * QT + q
                    last = dve.scalar_tensor_tensor(k.x[:, t, :], k.ps[:, b, q * D:(q + 1) * D],
                                                    x_inverse[:, t:t + 1], k.x[:, t, :], ALU.mult, ALU.add)
                last.then_inc(sem["x2_ready"], 1)
            norm_all(dve, n2, k.x, lambda b: dve.wait_ge(sem["x2_ready"], b + 1))
            for b in range(B):
                dve.wait_ge(sem["high_ready"], b + 1)
                dve.tensor_tensor(k.x_low[:, b, :], k.xT32[:, b, :], k.x_high[:, b, :],
                                  ALU.subtract).then_inc(k.c_x_ready, 1)

        @block.tensor
        def _(pe):
            for b in range(B):
                pe.wait_ge(sem["wide_ready"], b + 1)
                transpose_batch(pe, k, wide, b, b).then_inc(sem["sumT"], 1)
            for b in range(B):
                pe.wait_ge(sem["attn_ready"], b + 1)
                for q in range(QT):
                    last = pe.matmul(k.ps[:, 4 + b, q * D:(q + 1) * D], attnT[:, b, q * P:(q + 1) * P],
                                     weight(k, "a_out"), start=True, stop=True)
                last.then_inc(sem["projected"], 1)
            for b in range(B):
                n.wait_ready(pe, b)
                transpose_batch(pe, k, n.out, b, b).then_inc(sem["in_psum"], 1)
            for b in range(B):
                pe.wait_ge(sem["xT_ready"], b + 1)
                pe.wait_ge(sem["x_ready"], b + 1)
                pe.matmul(k.ps[:, 4 + b, :], weight(k, "b_q"), xT[:, b, :], start=True,
                          stop=True).then_inc(sem["q_done"], 1)
            for b in range(B):
                pe.wait_ge(sem["q_ready"], b + 1)
                for q in range(QT):
                    last = pe.matmul(k.ps[:, b, q * C:(q + 1) * C], qT[:, b, q * P:(q + 1) * P],
                                     k.ctx_kT[:, b * C:(b + 1) * C], start=True, stop=True)
                last.then_inc(sem["scored"], 1)
            for b in range(B):
                pe.wait_ge(sem["exp_done"], b + 1)
                for q in range(QT):
                    last = pe.transpose(k.ps[0:C, 4 + b, q * P:(q + 1) * P], probs[:, b * QT + q, :], k.ident[:, :])
                last.then_inc(sem["probsT_done"], 1)
            for b in range(B):
                pe.wait_ge(sem["probsT_ready"], b + 1)
                for q in range(QT):
                    last = pe.matmul(k.ps[:, b, q * D:(q + 1) * D], probsT[0:C, b, q * P:(q + 1) * P],
                                     k.ctx_v[0:C, b, :], start=True, stop=True)
                last.then_inc(sem["attended"], 1)
            for b in range(B):
                n2.wait_ready(pe, b)
                transpose_batch(pe, k, n2.out, b, b).then_inc(sem["in_psum2"], 1)
            pe.wait_ge(k.w_loaded["cd"], 16)
            for b in range(B):
                pe.wait_ge(sem["x32_ready"], b + 1)
                route_tensor_logits(pe, k, r, weight(k, "c_gate"), k.xT32, b, 4 + b)

        @block.scalar
        def _(act):
            norm_scalar(act, n, k.x)
            for b in range(B):
                act.wait_ge(sem["in_psum"], b + 1)
                act.copy(xT[:, b, :], k.ps[:, b, :]).then_inc(sem["xT_ready"], 1)
            for b in range(B):
                act.wait_ge(sem["max_ready"], b + 1)
                for q in range(QT):
                    t = b * QT + q
                    last = act.activation(probs[:, t, :], scores[:, t, :], ACT.Exp, bias=minus_max[:, t:t + 1],
                                          accum_out=exp_sum[:, t:t + 1])
                last.then_inc(sem["exp_done"], 1)
            for b in range(B):
                act.wait_ge(sem["probsT_done"], b + 1)
                act.copy(probsT[0:C, b, :], k.ps[0:C, 4 + b, :]).then_inc(sem["probsT_ready"], 1)
            norm_scalar(act, n2, k.x)
            for b in range(B):
                act.wait_ge(sem["in_psum2"], b + 1)
                act.copy(k.xT32[:, b, :], k.ps[:, b, :]).then_inc(sem["x32_ready"], 1)
                act.copy(k.x_high[:, b, :], k.ps[:, b, :]).then_inc(sem["high_ready"], 1)
            for b in range(B):
                route_scalar_scores(act, k, r, b, 4 + b)


class UnitWeights:

    def __init__(self, m):
        self.gu_high, self.gu_low = m.sb("gu_high", [P, 2, 2 * D], F32R), m.sb("gu_low", [P, 2, 2 * D], F32R)
        self.down_high, self.down_low = m.sb("down_high", [P, 2, D], F32R), m.sb("down_low", [P, 2, D], F32R)


def split_unit(pool, k, gu_name, down_name, p, buf, high_ready, done_before, weights_ready):
    w = k.unit_weights
    raw = k.w[:, bass.ds(COLS[gu_name][0] + p * 2 * D, 2 * D)]
    raw_down = k.w[:, bass.ds(COLS[down_name][0] + p * D, D)]
    pool.tensor_copy(w.gu_high[:, buf, :], raw).then_inc(high_ready, 1)
    pool.tensor_copy(w.down_high[:, buf, :], raw_down).then_inc(high_ready, 1)
    wait_apart(pool, k, high_ready, done_before + 2)
    pool.tensor_tensor(w.gu_low[:, buf, :], raw, w.gu_high[:, buf, :], ALU.subtract)
    pool.tensor_tensor(w.down_low[:, buf, :], raw_down, w.down_high[:, buf, :],
                       ALU.subtract).then_inc(weights_ready, 1)


def split_first_units(pool, k, m, prefix):
    high_ready, weights_ready = m.sem("weights_high_ready"), m.sem("weights_ready")
    for p in range(2):
        split_unit(pool, k, prefix + "gu", prefix + "down", p, p, high_ready, 2 * p, weights_ready)



def moe(nc, k, name, experts, top, groups, store):
    with ExitStack() as ctx:
        m = Stage(nc, ctx, name, k)
        units = 1 + experts // 2
        r = Route(m, k, experts, top, groups)
        up = m.sb("up", [P, 2, S])
        w = k.unit_weights
        gated = m.sb("gated", [P, 2, S])
        inner = m.sb("inner", [P, 2, S])
        inner_high = m.sb("inner_high", [P, 2, S], F32R)
        inner_low = m.sb("inner_low", [P, 2, S], F32R)
        yT = m.sb("yT", [P, B, S])
        gate_done, up_done, routed = m.sem("gate_done"), m.sem("up_done"), m.sem("routed")
        silu_done, up_used, inner_ready = m.sem("silu_done"), m.sem("up_used"), m.sem("inner_ready")
        inner_high_ready, inner_low_ready = m.sem("inner_high_ready"), m.sem("inner_low_ready")
        down_done, high_ready, weights_ready = m.sem("down_done"), m.sem("high_ready"), m.sem("weights_ready")
        y_ready, turned, x_done, stored = m.sem("y_ready"), m.sem("turned"), m.sem("x_done"), m.sem("stored")
        block = ctx.enter_context(nc.Block())
        N = units * B
        PAIRS = (units - 1) // 2

        @block.gpsimd
        def _(pool):
            m.clear_last(pool)
            def shared_inner(b):
                pool.wait_ge(silu_done, b + 1)
                pool.wait_ge(up_used, b + 1)
                if b >= 2:
                    pool.wait_ge(inner_low_ready, b - 1)
                pool.tensor_tensor(inner[:, b % 2, :], gated[:, b % 2, :], up[:, b % 2, :],
                                   ALU.mult).then_inc(inner_ready, 1)

            def shared_low(b):
                pool.wait_ge(inner_high_ready, b + 1)
                pool.tensor_tensor(inner_low[:, b % 2, :], inner[:, b % 2, :], inner_high[:, b % 2, :],
                                   ALU.subtract).then_inc(inner_low_ready, 1)

            shared_inner(0)
            shared_inner(1)
            shared_low(0)
            shared_inner(2)
            shared_low(1)
            shared_inner(3)
            def split(p, buf):
                pool.wait_ge(down_done, (p - 1) * B)
                split_unit(pool, k, name + "gu", name + "down", p, buf, high_ready, 2 * (p - 2), weights_ready)

            split(2, 0)
            with pool.Fori(1, PAIRS) as pair:
                split(pair * 2 + 1, 1)
                split(pair * 2 + 2, 0)

        @block.tensor
        def _(pe):
            def down_step(n, b, buf, first):
                pe.wait_ge(inner_low_ready, n + 1)
                for i, (down, x) in enumerate(((w.down_high, inner_high), (w.down_high, inner_low),
                                            (w.down_low, inner_high))):
                    last = pe.matmul(k.ps[:, 4 + b, :], down[:, buf, :], x[:, b % 2, :], start=first and i == 0,
                                     stop=True, skip_group_check=True)
                last.then_inc(down_done, 1)

            def gate_up(b, buf, half, slot, done):
                at = slice(half * D, (half + 1) * D)
                pe.matmul(k.ps[:, slot, :], w.gu_high[:, buf, at], k.x_high[:, b, :], start=True, stop=False)
                pe.matmul(k.ps[:, slot, :], w.gu_high[:, buf, at], k.x_low[:, b, :], start=False, stop=False)
                pe.matmul(k.ps[:, slot, :], w.gu_low[:, buf, at], k.x_high[:, b, :], start=False,
                          stop=True).then_inc(done, 1)

            def unit(p, buf, split_before=False):
                if not split_before:
                    pe.wait_ge(weights_ready, p - 1)
                for b in range(B):
                    n = p * B + b
                    slots = [(3 * b + i) % 4 for i in range(3)]
                    pe.wait_ge(inner_ready, n - 1)
                    gate_up(b, buf, 0, slots[0], gate_done)
                    pe.wait_ge(silu_done, n)
                    gate_up(b, buf, 1, slots[1], up_done)
                    pe.wait_ge(up_used, n)
                    pe.matmul(k.ps[:, slots[2], :],
                              k.sel[0:ROUTE_ROWS, bass.ds(p - 1, 1), :].rearrange("r a c -> r (a c)"),
                              k.routeT[0:ROUTE_ROWS, b, :], start=True, stop=True).then_inc(routed, 1)
                    if b >= 2:
                        down_step(n - 2, b - 2, buf, False)
                    else:
                        down_step(n - 2, b + 2, 1 - buf, isinstance(p, int) and p == 1)

            for b in range(B):
                if b >= 2:
                    pe.wait_ge(silu_done, b - 1)
                gate_up(b, 0, 0, 2 * (b % 2), gate_done)
                if b >= 2:
                    pe.wait_ge(up_used, b - 1)
                gate_up(b, 0, 1, 2 * (b % 2) + 1, up_done)
                if b >= 2:
                    down_step(b - 2, b - 2, 0, True)
            pe.wait_ge(r.parts_ready, 1)
            pe.wait_ge(silu_done, B)
            pe.wait_ge(up_used, B)
            for b in range(B):
                route_tensor_turn(pe, k, r, b, b)
            pe.wait_ge(r.ready, B)
            unit(1, 1, split_before=True)
            unit(2, 0)
            with pe.Fori(1, PAIRS) as pair:
                unit(pair * 2 + 1, 1)
                unit(pair * 2 + 2, 0)
            down_step(N - 2, B - 2, 0, False)
            down_step(N - 1, B - 1, 0, False)
            for b in range(B):
                pe.wait_ge(y_ready, b + 1)
                for q in range(QT):
                    last = pe.transpose(k.ps[:, b, q * P:(q + 1) * P], yT[:, b, q * P:(q + 1) * P], k.ident[:, :])
                last.then_inc(turned, 1)

        @block.scalar
        def _(act):
            def high_part(n, b, free):
                act.wait_ge(inner_ready, n + 1)
                if free:
                    act.wait_ge(down_done, n - 1)
                act.copy(inner_high[:, b % 2, :], inner[:, b % 2, :]).then_inc(inner_high_ready, 1)

            def unit(p):
                for b in range(B):
                    n = p * B + b
                    act.wait_ge(gate_done, n + 1)
                    act.wait_ge(inner_ready, n - 1)
                    act.activation(gated[:, b % 2, :], k.ps[:, (3 * b) % 4, :], ACT.Silu).then_inc(silu_done, 1)
                    high_part(n - 1, (b + 3) % B, True)

            for b in range(B):
                act.wait_ge(gate_done, b + 1)
                if b >= 2:
                    act.wait_ge(inner_ready, b - 1)
                act.activation(gated[:, b % 2, :], k.ps[:, 2 * (b % 2), :], ACT.Silu).then_inc(silu_done, 1)
                act.wait_ge(up_done, b + 1)
                act.copy(up[:, b % 2, :], k.ps[:, 2 * (b % 2) + 1, :]).then_inc(up_used, 1)
                if b >= 1:
                    high_part(b - 1, b - 1, b >= 3)
            for b in range(B):
                act.wait_ge(r.turned, b + 1)
                act.copy(k.routeT[0:ROUTE_ROWS, b, :],
                         k.ps[:, b, :].bitcast(BF16)[0:ROUTE_ROWS, 0:S]).then_inc(r.ready, 1)
            with act.Fori(1, units) as p:
                unit(p)
            high_part(N - 1, B - 1, True)
            act.wait_ge(down_done, N)
            for b in range(B):
                act.copy(yT[:, b, :], k.ps[:, 4 + b, :]).then_inc(y_ready, 1)

        @block.vector
        def _(dve):
            def low_part(n, b):
                dve.wait_ge(inner_high_ready, n + 1)
                dve.tensor_tensor(inner_low[:, b % 2, :], inner[:, b % 2, :], inner_high[:, b % 2, :],
                                  ALU.subtract).then_inc(inner_low_ready, 1)

            def unit(p):
                for b in range(B):
                    n = p * B + b
                    dve.wait_ge(silu_done, n + 1)
                    dve.wait_ge(up_done, n + 1)
                    dve.tensor_tensor(gated[:, b % 2, :], gated[:, b % 2, :], k.ps[:, (3 * b + 1) % 4, :],
                                      ALU.mult).then_inc(up_used, 1)
                    low_part(n - 1, (b + 3) % B)
                    dve.wait_ge(routed, n + 1 - B)
                    dve.wait_ge(up_used, n + 1)
                    dve.wait_ge(inner_low_ready, n - 1)
                    dve.tensor_tensor(inner[:, b % 2, :], gated[:, b % 2, :], k.ps[:, (3 * b + 2) % 4, :],
                                      ALU.mult).then_inc(inner_ready, 1)

            route_vector(dve, k, r)
            dve.wait_ge(inner_low_ready, 2)
            low_part(2, 2)
            with dve.Fori(1, units) as p:
                unit(p)
            low_part(N - 1, B - 1)
            for b in range(B):
                at = slice(b * QT, (b + 1) * QT)
                dve.wait_ge(turned, b + 1)
                dve.tensor_tensor(k.x[:, at, :], k.x[:, at, :], k.ps[:, b, :].rearrange("p (q d) -> p q d", d=D),
                                  ALU.add).then_inc(x_done, 1)

        @block.sync
        def _(sp):
            if store:
                out = k.out_dram.rearrange("b (q p) d -> p (b q) d", p=P)
                for b in range(B):
                    at = slice(b * QT, (b + 1) * QT)
                    sp.wait_ge(x_done, b + 1)
                    sp.dma_start(out[:, at, :], k.x[:, at, :]).then_inc(stored, 16)
                sp.wait_ge(stored, 16 * B)



def attn1_project(nc, k):
    with ExitStack() as ctx:
        m = Stage(nc, ctx, "d_", k)
        n = Norm(m, "norm")
        s = Split(m)
        x_padded = m.sb("x_padded", [P, B, S + 2])
        conv = n.out[:, :, :].rearrange("p (b q) d -> p b (q d)", b=B)[:, :, 0:NK]
        in_psum, xT_ready = m.sem("x_in_psum"), m.sem("xT_ready")
        q_done, k_done, v_done = m.sem("q_done"), m.sem("k_done"), m.sem("v_done")
        zeroed, v_zeroed, pad_set, v_copied = m.sem("zeroed"), m.sem("v_zeroed"), m.sem("pad_set"), m.sem("v_copied")
        taps = [m.sem(f"tap{i}") for i in range(3)]
        block = ctx.enter_context(nc.Block())
        scale = float(HD) ** -0.5

        @block.sync
        def _(sp):
            for b in range(B):
                store_parts(sp, k, s, b, (S, NK), k.d_stored)
                if b == 0:
                    sp.wait_ge(zeroed, 2)
                    load_stacks(sp, k, 0, (S, NK), k.d_stored, k.d_loaded)

        @block.gpsimd
        def _(pool):
            m.clear_last(pool)
            pool.memset(x_padded[:, :, 0:1], 0.0).then_inc(pad_set, 1)
            for b in range(B):
                norm_rstd(pool, k, n, b)
            for b in range(2):
                pool.memset(k.q_stack[0:KROWS, b, :, :].bitcast(F32), 0.0).then_inc(zeroed, 1)
                pool.memset(k.k_stack[0:KROWS, b, :, :].bitcast(F32), 0.0).then_inc(zeroed, 1)
            pool.memset(k.v_padded[:, :, :, :], 0.0).then_inc(v_zeroed, 1)

        @block.vector
        def _(dve):
            norm_all(dve, n, k.x)
            for b in range(B):
                dve.wait_ge(taps[1], b + 1)
                if b == 0:
                    dve.wait_ge(pad_set, 1)
                dve.scalar_tensor_tensor(conv[:, b, :], x_padded[:, b, 0:S:2], col(k, "conv_w", 0), conv[:, b, :],
                                         ALU.mult, ALU.add).then_inc(taps[0], 1)
                dve.wait_ge(taps[0], b + 1)
                dve.scalar_tensor_tensor(conv[:, b, :], x_padded[:, b, 2:S + 2:2], col(k, "conv_w", 2),
                                         conv[:, b, :], ALU.mult, ALU.add).then_inc(taps[2], 1)

            def full(i, out):
                b = i // 2
                if i % 2 == 0:
                    dve.wait_ge(q_done, b + 1)
                    return dve.tensor_scalar(out, k.ps[:, 4 + b, :], col(k, "d_bq"), scale, ALU.add, ALU.mult)
                dve.wait_ge(k_done, b + 1)
                return dve.tensor_scalar(out, k.ps[:, b, 0:NK], col(k, "d_bk"), None, ALU.add)

            split_vector(dve, s, (S, NK), full)
            dve.wait_ge(v_zeroed, 1)
            bias = row(k, "d_bv").rearrange("p (g j d) -> p g j d", g=4, j=4)
            for b in range(B):
                dve.wait_ge(v_done, b + 1)
                for t in range(NK // P):
                    out = k.v_padded[:, b, t, :].rearrange("p (g x) -> p g x", g=4)[:, :, 0:D]
                    last = dve.tensor_tensor(
                        out.rearrange("p g (j y) -> p g j y", j=4)[:, :, :, 0:HD],
                        k.ps[:, b, t * D:(t + 1) * D].rearrange("p (g j d) -> p g j d", g=4, j=4), bias, ALU.add)
                last.then_inc(v_copied, 1)

        @block.tensor
        def _(pe):
            for b in range(B):
                n.wait_ready(pe, b)
                transpose_batch(pe, k, n.out, b, b).then_inc(in_psum, 1)
            for b in range(B):
                pe.wait_ge(xT_ready, b + 1)
                pe.matmul(k.ps[:, 4 + b, :], weight(k, "d_q"), x_padded[:, b, 1:S + 1], start=True,
                          stop=True).then_inc(q_done, 1)
            for b in range(B):
                pe.wait_ge(taps[2], b + 1)
                pe.matmul(k.ps[:, b, 0:NK], weight(k, "d_k"), conv[:, b, :], start=True,
                          stop=True).then_inc(k_done, 1)
            for b in range(B):
                pe.wait_ge(s.full_ready, 2 * b + 2)
                for t in range(NK // P):
                    last = pe.matmul(k.ps[:, b, t * D:(t + 1) * D], conv[:, b, t * P:(t + 1) * P],
                                     weight(k, "d_v"), start=True, stop=True)
                last.then_inc(v_done, 1)

        @block.scalar
        def _(act):
            norm_scalar(act, n, k.x)
            for b in range(B):
                act.wait_ge(in_psum, b + 1)
                act.copy(x_padded[:, b, 1:S + 1], k.ps[:, b, :]).then_inc(xT_ready, 1)
                act.wait_ge(xT_ready, b + 1)
                act.activation(conv[:, b, :], x_padded[:, b, 1:S + 1:2], ACT.Identity, bias=col(k, "conv_b"),
                               scale=col(k, "conv_w", 1)).then_inc(taps[1], 1)
            split_scalar(act, s, (S, NK), k.d_stored)



def attn1_heads(nc, k):
    with ExitStack() as ctx:
        m = Stage(nc, ctx, "dh_", k)
        N, BODY = B * H, 8
        minus_max = m.sb("minus_max", [P, N, QT])
        probs = m.sb("probs", [P, 4, QT, NK])
        v = m.sb("v", [P, BODY, NK // P, 32])
        probsT = m.sb("probsT", [P, BODY, NK // P, S])
        scored, max_ready, exp_done = m.sem("scored"), m.sem("max_ready"), m.sem("exp_done")
        turned = [m.sem("turned0"), m.sem("turned1")]
        copied = [m.sem("copied0"), m.sem("copied1")]
        v_ready, attended, quad_added = m.sem("v_ready"), m.sem("attended"), m.sem("quad_added")
        stacks_ready = m.sem("stacks_ready")
        block = ctx.enter_context(nc.Block())

        def scores_of(i):
            return k.ps[:, 2 * (i % 2):2 * (i % 2) + 2, :].rearrange("p a (q t) -> p (a q) t", t=NK)

        def bodies(eng, body):
            body(0, True)
            with eng.Fori(1, N // BODY) as i:
                body(i, False)

        @block.sync
        def _(sp):
            for b in range(B):
                if b >= 2:
                    sp.wait_ge(scored, H * (b - 1))
                if b >= 1:
                    load_stacks(sp, k, b, (S, NK), k.d_stored, k.d_loaded)
                sp.wait_ge(k.d_loaded, STACK_LOADED * (b + 1))
                sp.sem_inc(stacks_ready, H // BODY)

        @block.gpsimd
        def _(pool):
            m.clear_last(pool)
            def body(it, first):
                for i in range(BODY):
                    n = it * BODY + i
                    if not first and i % 4 == 0:
                        pool.wait_ge(attended, it * 2 + i // 4 - 1)
                    b, at = it // 2, (i // 4 + 2 * (it % 2)) * P + 32 * (i % 4)
                    pool.tensor_copy(v[:, i, :, :],
                                     k.v_padded[:, bass.ds(b, 1), :, bass.ds(at, 32)]
                                     .rearrange("p a t c -> p (a t) c")).then_inc(v_ready, 1)

            pool.memset(k.attended[:, :, :], 0.0).then_inc(quad_added, 1)
            bodies(pool, body)

        @block.tensor
        def _(pe):
            def scores(it, i, first):
                n, b = it * BODY + i, it // 2
                head = (it % 2) * BODY + i
                if i == 0:
                    pe.wait_ge(stacks_ready, it + 1)
                if not first or i >= 2:
                    pe.wait_ge(exp_done, n - 1)
                at = (b % 2) * H + head
                q_rows = k.q_stack[0:KROWS, :, :, :].rearrange("p a h t -> p (a h) t")
                k_rows = k.k_stack[0:KROWS, :, :, :].rearrange("p a h t -> p (a h) t")
                for q in range(QT):
                    last = pe.matmul(scores_of(i)[:, q, :],
                                     q_rows[:, bass.ds(at, 1), q * P:(q + 1) * P].rearrange("p a t -> p (a t)"),
                                     k_rows[:, bass.ds(at, 1), :].rearrange("p a t -> p (a t)"),
                                     start=True, stop=True)
                last.then_inc(scored, 1)

            def turn(n, i, first):
                pe.wait_ge(exp_done, n + 1)
                for t in range(NK // P):
                    if not first:
                        pe.wait_ge(copied[t], n)
                    for q in range(QT):
                        last = pe.transpose(k.ps[:, 4 + t, q * P:(q + 1) * P],
                                            probs[:, i % 4, q, t * P:(t + 1) * P], k.ident[:, :])
                    last.then_inc(turned[t], 1)

            def attend(quad, half, t, first):
                if t == 0:
                    if not first:
                        pe.wait_ge(quad_added, quad)
                    pe.wait_ge(v_ready, quad * 4 + 4)
                pe.wait_ge(copied[t], quad * 4 + 4)
                for j in range(4):
                    last = pe.matmul(k.ps[32 * j:32 * j + 32, 6 + half, :], v[:, 4 * half + j, t, :],
                                     probsT[:, 4 * half + j, t, :], start=(t == 0), stop=(t == NK // P - 1))
                if t == NK // P - 1:
                    last.then_inc(attended, 1)

            def body(it, first):
                for i in range(BODY):
                    n = it * BODY + i
                    scores(it, i, first)
                    if not first or i >= 2:
                        turn(n - 2, (i - 2) % BODY, first and i == 2)
                    if i in (2, 3) and not first:
                        attend(it * 2 - 1, 1, i - 2, False)
                    if i in (6, 7):
                        attend(it * 2, 0, i - 6, first)

            bodies(pe, body)
            turn(N - 2, BODY - 2, False)
            turn(N - 1, BODY - 1, False)
            for t in range(NK // P):
                attend(N // 4 - 1, 1, t, False)

        def copy_turned(eng, copy, n, i, t, quad):
            eng.wait_ge(turned[t], n + 1)
            if quad is not None:
                eng.wait_ge(attended, quad - 1)
            copy(probsT[:, i, t, :], k.ps[:, 4 + t, :]).then_inc(copied[t], 1)

        def quad_of(it, i, first):
            return None if first or i < 2 else it * 2 + (i - 2) // 4

        @block.vector
        def _(dve):
            def copies(n, i, quad):
                copy_turned(dve, dve.tensor_copy, n, i, 0, quad)
                if i % 4 == 0:
                    copy_turned(dve, dve.tensor_copy, n, i, 1, quad)

            def add_quad(quad, half, b):
                dve.wait_ge(attended, quad + 1)
                dve.wait_ge(quad_added, quad + 1)
                out = k.attended[:, bass.ds(b, 1), :].rearrange("p a t -> p (a t)")
                dve.tensor_tensor(out, out, k.ps[:, 6 + half, :], ALU.add).then_inc(quad_added, 1)

            def body(it, first):
                for i in range(BODY):
                    n = it * BODY + i
                    dve.wait_ge(scored, n + 1)
                    dve.tensor_reduce(minus_max[:, bass.ds(n, 1), :].rearrange("p a q -> p (a q)"),
                                      scores_of(i), AX_X, ALU.max, negate=True).then_inc(max_ready, 1)
                    if first and i == 2:
                        for b in range(B):
                            dve.wait_ge(k.d_stored[b], 32)
                    if not first or i >= 2:
                        copies(n - 2, (i - 2) % BODY, quad_of(it, i, first))
                    if i % 4 == 0 and not first:
                        add_quad(it * 2 - 2 + i // 4, i // 4, (it - 1) // 2)

            bodies(dve, body)
            for i in (BODY - 2, BODY - 1):
                copies(N - BODY + i, i, None)
            add_quad(N // 4 - 2, 0, B - 1)
            add_quad(N // 4 - 1, 1, B - 1)

        @block.scalar
        def _(act):
            def copies(n, i, quad):
                if i % 4 != 0:
                    copy_turned(act, act.copy, n, i, 1, quad)

            def body(it, first):
                for i in range(BODY):
                    n = it * BODY + i
                    if first and i == 2:
                        for b in range(B):
                            act.wait_ge(k.d_stored[b], 32)
                    if not first or i >= 2:
                        copies(n - 2, (i - 2) % BODY, quad_of(it, i, first))
                    if not first or i >= 4:
                        act.wait_ge(turned[1], n - 3)
                    wait_apart(act, k, max_ready, n + 1)
                    for q in range(QT):
                        last = act.activation(probs[:, i % 4, q, :], scores_of(i)[:, q, :], ACT.Exp,
                                              bias=minus_max[:, bass.ds(n, 1), q:q + 1]
                                              .rearrange("p a q -> p (a q)"),
                                              accum_out=k.exp_sum[:, bass.ds(n, 1), q:q + 1]
                                              .rearrange("p a q -> p (a q)"))
                    last.then_inc(exp_done, 1)

            bodies(act, body)
            for i in (BODY - 2, BODY - 1):
                copies(N - BODY + i, i, None)



def attn1_out_latents(nc, k):
    with ExitStack() as ctx:
        m = Stage(nc, ctx, "e0_", k)
        n, n2 = Norm(m, "norm"), Norm(m, "latent")
        nm = Norm(m, "media", tiles=1, rows=C)
        inverse = m.sb("inverse", [P, B * H, QT])
        wide = m.sb("wide", [P, T, D])
        attnT = wide[:, :, :].rearrange("p (b q) d -> p b (q d)", b=B)
        names = ["inv_ready", "wide_ready", "invT", "attn_ready", "projected", "x_ready", "biased", "scaled_w",
                 "scaled", "shifted", "media_scaled", "media_shifted", "in_psum", "media_in_psum", "high", "low",
                 "media_high", "media_low", "token_high", "media_token_high", "folded", "bias_sum", "pad_set", "w_high", "w_ready"]
        sem = {x: m.sem(x) for x in names}
        block = ctx.enter_context(nc.Block())
        scale = float(D) ** -0.5

        @block.gpsimd
        def _(pool):
            m.clear_last(pool)
            for b in range(B):
                at = slice(b * QT, (b + 1) * QT)
                pool.tensor_tensor(k.x[:, at, :], k.x[:, at, :],
                                   row(k, "d_bo").unsqueeze(1).broadcast_to([P, QT, D]),
                                   ALU.add).then_inc(sem["biased"], 1)
            for b in range(B):
                norm_rstd(pool, k, nm, b)
            pool.wait_ge(k.w_loaded["e"], 16)
            at, w = COL["e_bq"]
            pool.tensor_scalar(weight(k, "e_q"), weight(k, "e_q"), scale, 1.0, ALU.mult,
                               ALU.mult).then_inc(sem["scaled_w"], 1)
            pool.tensor_scalar(k.cols[:, at:at + w], k.cols[:, at:at + w], scale, 1.0, ALU.mult,
                               ALU.mult).then_inc(sem["scaled_w"], 1)
            pool.memset(k.kvT_high[:, :, S + C:].bitcast(F32), 0.0).then_inc(sem["pad_set"], 1)
            pool.memset(k.kvT_low[:, :, S + C:].bitcast(F32), 0.0).then_inc(sem["pad_set"], 1)
            for b in range(B):
                norm_rstd(pool, k, n, b)
            pool.wait_ge(sem["scaled_w"], 1)
            split_query_key(pool, k, 0, sem["w_high"], 0, sem["w_ready"])
            for b in range(B):
                nm.wait_ready(pool, b)
                pool.tensor_tensor(nm.out[0:C, b, :], nm.out[0:C, b, :], row(k, "g_med", C),
                                   ALU.mult).then_inc(sem["media_scaled"], 1)
                pool.wait_ge(sem["media_scaled"], b + 1)
                pool.tensor_tensor(nm.out[0:C, b, :], nm.out[0:C, b, :], row(k, "b_med", C),
                                   ALU.add).then_inc(sem["media_shifted"], 1)
            for b in range(B):
                norm_rstd(pool, k, n2, b)
            for b in range(B):
                at = slice(b * QT, (b + 1) * QT)
                pool.wait_ge(sem["token_high"], b + 1)
                pool.tensor_tensor(k.kv_low[:, b, 0:QT, :], n2.out[:, at, :], k.kv_high[:, b, 0:QT, :],
                                   ALU.subtract).then_inc(k.kv_ready, 1)

        @block.vector
        def _(dve):
            dve.reciprocal(inverse[:, :, :], k.exp_sum[:, :, :]).then_inc(sem["inv_ready"], 1)
            dve.wait_ge(sem["inv_ready"], 1)
            for b in range(B):
                for q in range(QT):
                    last = dve.tensor_copy(
                        wide[:, b * QT + q, :].rearrange("p (j g d) -> p j g d", j=4, g=4),
                        inverse[:, b * H:(b + 1) * H, q].rearrange("p (g j) -> p j g", j=4).unsqueeze(3)
                        .broadcast_to([P, 4, 4, HD]))
                last.then_inc(sem["wide_ready"], 1)
            norm_all(dve, nm, k.media, lambda b: dve.wait_ge(k.media_loaded, 16))
            for b in range(B):
                dve.wait_ge(sem["invT"], b + 1)
                dve.tensor_tensor(attnT[:, b, :], k.attended[:, b, :], k.ps[:, b, :],
                                  ALU.mult).then_inc(sem["attn_ready"], 1)
            for b in range(B):
                at = slice(b * QT, (b + 1) * QT)
                dve.wait_ge(sem["projected"], b + 1)
                dve.wait_ge(sem["biased"], b + 1)
                dve.tensor_tensor(k.x[:, at, :], k.x[:, at, :],
                                  k.ps[:, 4 + b, :].rearrange("p (q d) -> p q d", d=D),
                                  ALU.add).then_inc(sem["x_ready"], 1)
            norm_all(dve, n, k.x, lambda b: dve.wait_ge(sem["x_ready"], b + 1))
            norm_all(dve, n2, n.out, lambda b: n.wait_ready(dve, b))
            for b in range(B):
                at = slice(b * QT, (b + 1) * QT)
                n2.wait_ready(dve, b)
                dve.tensor_tensor(n2.out[:, at, :], n2.out[:, at, :],
                                  row(k, "g_lat").unsqueeze(1).broadcast_to([P, QT, D]),
                                  ALU.mult).then_inc(sem["scaled"], 1)
            for b in range(B):
                at = slice(b * QT, (b + 1) * QT)
                dve.wait_ge(sem["scaled"], b + 1)
                dve.tensor_tensor(n2.out[:, at, :], n2.out[:, at, :],
                                  row(k, "b_lat").unsqueeze(1).broadcast_to([P, QT, D]),
                                  ALU.add).then_inc(sem["shifted"], 1)
            for b in range(B):
                at = slice(b * QT, (b + 1) * QT)
                dve.wait_ge(sem["high"], b + 1)
                dve.tensor_tensor(k.kvT_low[:, b, 0:S], k.ps[:, b, :], k.kvT_high[:, b, 0:S],
                                  ALU.subtract).then_inc(sem["low"], 1)
                dve.wait_ge(sem["media_high"], b + 1)
                dve.tensor_tensor(k.kvT_low[:, b, S:KV], k.ps[:, 4 + b, 0:C], k.kvT_high[:, b, S:KV],
                                  ALU.subtract).then_inc(sem["media_low"], 1)
                dve.wait_ge(sem["media_token_high"], b + 1)
                dve.tensor_tensor(k.kv_low[0:C, b, QT, :], nm.out[0:C, b, :], k.kv_high[0:C, b, QT, :],
                                  ALU.subtract).then_inc(k.kv_ready, 1)
            dve.wait_ge(sem["bias_sum"], 1)
            dve.tensor_scalar(k.out_bias[:, :], k.ps[:, 6, 0:1], col(k, "e_bo"), None,
                              ALU.add).then_inc(k.kv_ready, 1)

        @block.tensor
        def _(pe):
            for b in range(B):
                pe.wait_ge(sem["wide_ready"], b + 1)
                transpose_batch(pe, k, wide, b, b).then_inc(sem["invT"], 1)
            for b in range(B):
                pe.wait_ge(sem["attn_ready"], b + 1)
                for q in range(QT):
                    last = pe.matmul(k.ps[:, 4 + b, q * D:(q + 1) * D], attnT[:, b, q * P:(q + 1) * P],
                                     weight(k, "d_out"), start=True, stop=True)
                last.then_inc(sem["projected"], 1)
            for b in range(B):
                pe.wait_ge(sem["media_shifted"], b + 1)
                pe.wait_ge(sem["x_ready"], b + 1)
                pe.transpose(k.ps[:, 4 + b, 0:C], nm.out[0:C, b, :], k.ident[0:C, 0:C]
                             ).then_inc(sem["media_in_psum"], 1)
            for b in range(B):
                pe.wait_ge(sem["shifted"], b + 1)
                transpose_batch(pe, k, n2.out, b, b).then_inc(sem["in_psum"], 1)
            for g in range(2):
                pe.wait_ge(sem["media_low"], g + 1)
                for j in range(4):
                    h = slice((4 * g + j) * D, (4 * g + j + 1) * D)
                    last = pe.matmul(k.ps[:, 4 + g, j * D:(j + 1) * D], weight(k, "e_vT")[:, h],
                                     weight(k, "e_o")[:, h], start=True, stop=True)
                last.then_inc(sem["folded"], 1)
            pe.wait_ge(sem["media_low"], 3)
            for h in range(XH):
                last = pe.matmul(k.ps[:, 6, 0:1], weight(k, "e_o")[:, h * D:(h + 1) * D], col(k, "e_bv", h),
                                 start=(h == 0), stop=(h == XH - 1))
            last.then_inc(sem["bias_sum"], 1)

        @block.scalar
        def _(act):
            norm_scalar(act, n, k.x)
            for b in range(B):
                act.wait_ge(sem["media_in_psum"], b + 1)
                act.copy(k.kvT_high[:, b, S:KV], k.ps[:, 4 + b, 0:C]).then_inc(sem["media_high"], 1)
                act.copy(k.kv_high[0:C, b, QT, :], nm.out[0:C, b, :]).then_inc(sem["media_token_high"], 1)
            norm_scalar(act, n2, n.out)
            for b in range(B):
                at = slice(b * QT, (b + 1) * QT)
                act.wait_ge(sem["in_psum"], b + 1)
                act.copy(k.kvT_high[:, b, 0:S], k.ps[:, b, :]).then_inc(sem["high"], 1)
                act.copy(k.kv_high[:, b, 0:QT, :], n2.out[:, at, :]).then_inc(sem["token_high"], 1)
            for g in range(2):
                act.wait_ge(sem["folded"], g + 1)
                act.copy(k.w_vo[:, 4 * g:4 * g + 4, :],
                         k.ps[:, 4 + g, :].rearrange("p (h d) -> p h d", h=4)).then_inc(k.kv_ready, 1)


def split_query_key(pool, k, h, w_high, done_before, w_ready):
    pairs = ((k.wq, COLS["e_q"][0]), (k.wk, COLS["e_k"][0]))
    for w, at in pairs:
        pool.tensor_copy(w[:, 0, :], k.w[:, bass.ds(at + h * D, D)]).then_inc(w_high, 1)
    wait_apart(pool, k, w_high, done_before + 2)
    for w, at in pairs:
        last = pool.tensor_tensor(w[:, 1, :], k.w[:, bass.ds(at + h * D, D)], w[:, 0, :], ALU.subtract)
    last.then_inc(w_ready, 1)



def xattn1_heads(nc, k):
    with ExitStack() as ctx:
        m = Stage(nc, ctx, "e_", k)
        U = XH * B
        SPLIT = 3
        wq, wk = k.wq, k.wk
        wo = m.sb("wo", [P, D])
        qT = m.sb("qT", [P, 2, 2, S], F32R)
        kT = m.sb("kT", [P, 2, 2, S], F32R)
        q_full = k.w[:, 0:2 * S].rearrange("p (a t) -> p a t", a=2)
        media_kT = k.w[:, 2 * S:2 * S + 2 * B * (C + 1)].rearrange("p (v b c) -> p v b c", v=2, b=B)
        probs = m.sb("probs", [P, 2 * QT, KV])
        minus_max, exp_sum, inverse = (m.sb("minus_max", [P, 4]), m.sb("exp_sum", [P, 4]), m.sb("inverse", [P, 4]))
        turned_high = m.sb("turned_high", [P, 2, KT, S], F32R)
        turned_low = m.sb("turned_low", [P, 2, KT, S], F32R)
        attn = weight(k, "e_o").rearrange("p (a t) -> p a t", a=2)
        names = ["w_high", "w_ready", "wo_ready", "q_done", "k_done", "km_done", "q_high", "k_high", "km_ready",
                 "q_low", "k_low", "q_summed", "scored", "max_ready", "exp_done", "inv_ready", "normed", "turned",
                 "t_high", "t_low", "attended", "attn_ready", "out_done", "added"]
        sem = {x: m.sem(x) for x in names}
        block = ctx.enter_context(nc.Block())
        bq, bk = COL["e_bq"][0], COL["e_bk"][0]

        def pair(q):
            return k.ps[:, 2 * (q % 2):2 * (q % 2) + 2, :].rearrange("p a t -> p (a t)")

        def heads(eng, body):
            for h in (0, None, XH - 1):
                if h is not None:
                    for b in range(B):
                        body(h, b, h == 0, h == XH - 1)
                else:
                    with eng.Fori(1, XH - 1) as i:
                        for b in range(B):
                            body(i, b, False, False)

        @block.gpsimd
        def _(pool):
            m.clear_last(pool)
            def weights(h):
                split_query_key(pool, k, h, sem["w_high"], 2 * h - 2, sem["w_ready"])

            def sum_q(u, b):
                pool.wait_ge(sem["q_low"], u + 1)
                pool.tensor_tensor(q_full[:, b % 2, :], qT[:, b % 2, 0, :], qT[:, b % 2, 1, :],
                                   ALU.add).then_inc(sem["q_summed"], 1)

            def output_weights(h):
                pool.tensor_copy(wo[:, :], k.w_vo[:, bass.ds(h, 1), :].rearrange("p a d -> p (a d)")
                                 ).then_inc(sem["wo_ready"], 1)

            def body(h, b, first, last):
                u = 4 * h + b
                for q in range(QT):
                    s = 4 * u + q
                    if b == 2 and q == 0 and not first:
                        pool.wait_ge(sem["out_done"], u - 2)
                        output_weights(h)
                    at = probs[:, (b % 2) * QT + q, :]
                    wait_apart(pool, k, sem["inv_ready"], s + 1)
                    pool.tensor_scalar(at, at, inverse[:, q:q + 1], 1.0, ALU.mult,
                                       ALU.mult).then_inc(sem["normed"], 1)
                    if q == 1 and not (last and b == B - 1):
                        sum_q(u + 1, (b + 1) % B)
                    if b == 2 and q == 1 and not last:
                        pool.wait_ge(sem["k_done"], u + 2)
                        weights(h + 1)

            sum_q(0, 0)
            output_weights(0)
            heads(pool, body)

        @block.tensor
        def _(pe):
            def three(out, high, low, m_high, m_low):
                pe.matmul(out, high, m_high, start=True, stop=False)
                pe.matmul(out, high, m_low, start=False, stop=False)
                return pe.matmul(out, low, m_high, start=False, stop=True)

            def project_q(u, b):
                three(k.ps[:, 6, :], wq[:, 0, :], wq[:, 1, :], k.kvT_high[:, b, 0:S],
                      k.kvT_low[:, b, 0:S]).then_inc(sem["q_done"], 1)

            def project_k(u, b):
                three(k.ps[:, 6, :], wk[:, 0, :], wk[:, 1, :], k.kvT_high[:, b, 0:S],
                      k.kvT_low[:, b, 0:S]).then_inc(sem["k_done"], 1)

            def project_media():
                three(k.ps[:, 6, 0:B * (C + 1)].rearrange("p (b c) -> p b c", b=B), wk[:, 0, :], wk[:, 1, :],
                      k.kvT_high[:, :, S:KV + 1], k.kvT_low[:, :, S:KV + 1]).then_inc(sem["km_done"], 1)

            def scores(s, h, b, q):
                v, t = b % 2, slice(q * P, (q + 1) * P)
                three(pair(q)[:, 0:S], qT[:, v, 0, t], qT[:, v, 1, t], kT[:, v, 0, :], kT[:, v, 1, :])
                pe.matmul(pair(q)[:, S:KV], q_full[:, v, t],
                          media_kT[:, bass.ds(h % 2, 1), b, 0:C].rearrange("p a c -> p (a c)"), start=True,
                          stop=True).then_inc(sem["scored"], 1)

            def turn(u, b, q, free):
                use = 5 * u + q
                bank = 4 + (b + q) % 2
                pe.wait_ge(sem["normed"], 4 * u + min(q, QT - 1) + 1)
                if free:
                    pe.wait_ge(sem["t_low"], use - 1)
                for i in range(QT):
                    if q < QT:
                        out, src = k.ps[:, bank, i * P:(i + 1) * P], probs[:, (b % 2) * QT + q, i * P:(i + 1) * P]
                    else:
                        out, src = k.ps[0:C, bank, i * P:(i + 1) * P], probs[:, (b % 2) * QT + i, S:KV]
                    last = pe.transpose(out, src, k.ident[:, :])
                last.then_inc(sem["turned"], 1)

            def attend(u, b, first, last):
                pe.wait_ge(sem["t_low"], 5 * u + (5 if last == KT else 4))
                for i in range(first, last):
                    r = P if i < QT else C
                    kv = (k.kv_high[0:r, b, i, :], k.kv_low[0:r, b, i, :])
                    pt = (turned_high[0:r, b % 2, i, :], turned_low[0:r, b % 2, i, :])
                    pe.matmul(k.ps[:, 7, :], kv[0], pt[0], start=(i == 0), stop=False)
                    pe.matmul(k.ps[:, 7, :], kv[0], pt[1], start=False, stop=False)
                    done = pe.matmul(k.ps[:, 7, :], kv[1], pt[0], start=False, stop=(i == KT - 1))
                if last == KT:
                    done.then_inc(sem["attended"], 1)

            def output(u, h, b):
                pe.wait_ge(sem["attn_ready"], u + 1)
                if b == 0:
                    pe.wait_ge(sem["wo_ready"], h + 1)
                pe.matmul(k.ps[:, 7, :], wo[:, :], attn[:, b % 2, :], start=True,
                          stop=True).then_inc(sem["out_done"], 1)

            def body(h, b, first, last):
                u = 4 * h + b
                some1, some2 = not first or b >= 1, not first or b >= 2
                more = not last or b < B - 1
                nb = (b + 1) % B
                b1 = (b + 3) % B
                pe.wait_ge(sem["k_low"], u + 1)
                if b == 0:
                    pe.wait_ge(sem["km_ready"], h + 1)
                pe.wait_ge(sem["q_summed"], u + 1)
                for q in range(QT):
                    s = 4 * u + q
                    if not first or b or q >= 2:
                        pe.wait_ge(sem["exp_done"], s - 1)
                    scores(s, h, b, q)
                    if q == 0:
                        if more:
                            if nb == 0:
                                pe.wait_ge(sem["w_ready"], h + 1)
                            project_q(u + 1, nb)
                        if some1:
                            turn(u - 1, b1, 2, True)
                        if some2:
                            attend(u - 2, (b + 2) % B, SPLIT, KT)
                    if q == 1:
                        if some1:
                            turn(u - 1, b1, 3, True)
                        if more:
                            pe.wait_ge(sem["q_low"], u + 2)
                            project_k(u + 1, nb)
                        if some1:
                            turn(u - 1, b1, 4, True)
                    if q == 2:
                        if some2:
                            output(u - 2, h if b >= 2 else h - 1, (b + 2) % B)
                        if b == B - 1 and not last:
                            pe.wait_ge(sem["k_low"], u + 2)
                            project_media()
                        turn(u, b, 0, some1)
                    if q == 3:
                        if some1:
                            if some2:
                                pe.wait_ge(sem["added"], u - 1)
                            attend(u - 1, b1, 0, SPLIT)
                        turn(u, b, 1, some1)

            pe.wait_ge(k.kv_ready, 2 * B + 3)
            project_q(0, 0)
            pe.wait_ge(sem["q_low"], 1)
            project_k(0, 0)
            pe.wait_ge(sem["k_low"], 1)
            project_media()
            heads(pe, body)
            u = U - 1
            turn(u, B - 1, 2, True)
            attend(u - 1, (u - 1) % B, SPLIT, KT)
            turn(u, B - 1, 3, True)
            turn(u, B - 1, 4, True)
            output(u - 1, XH - 1, (u - 1) % B)
            pe.wait_ge(sem["added"], u)
            attend(u, B - 1, 0, KT)
            output(u, XH - 1, B - 1)

        def bias_col(at, h):
            return k.cols[:, bass.ds(at + h, 1)]

        @block.scalar
        def _(act):
            def high_q(u, h, b):
                wait_apart(act, k, sem["q_done"], u + 1)
                act.activation(qT[:, b % 2, 0, :], k.ps[:, 6, :], ACT.Identity,
                               bias=bias_col(bq, h)).then_inc(sem["q_high"], 1)

            def high_k(u, h, b):
                wait_apart(act, k, sem["k_done"], u + 1)
                act.activation(kT[:, b % 2, 0, :], k.ps[:, 6, :], ACT.Identity,
                               bias=bias_col(bk, h)).then_inc(sem["k_high"], 1)

            def media_keys(h):
                wait_apart(act, k, sem["km_done"], h + 1)
                act.activation(media_kT[:, bass.ds(h % 2, 1), :, :].rearrange("p a b c -> p (a b c)"),
                               k.ps[:, 6, 0:B * (C + 1)], ACT.Identity,
                               bias=bias_col(bk, h)).then_inc(sem["km_ready"], 1)

            def exps(u, b, q, free):
                s = 4 * u + q
                act.wait_ge(sem["max_ready"], s + 1)
                if free:
                    act.wait_ge(sem["turned"], 5 * u - 5)
                act.activation(probs[:, (b % 2) * QT + q, :], pair(q)[:, 0:KV], ACT.Exp,
                               bias=minus_max[:, q:q + 1], accum_out=exp_sum[:, q:q + 1]
                               ).then_inc(sem["exp_done"], 1)

            def high_turned(u, b, q, free):
                use = 5 * u + q
                bank = 4 + (b + q) % 2
                act.wait_ge(sem["turned"], use + 1)
                if free:
                    act.wait_ge(sem["attended"], u - 1)
                if q < QT:
                    act.copy(turned_high[:, b % 2, 0:QT, q * P:(q + 1) * P],
                             k.ps[:, bank, :].rearrange("p (i t) -> p i t", t=P)).then_inc(sem["t_high"], 1)
                else:
                    act.copy(turned_high[0:C, b % 2, QT, :], k.ps[0:C, bank, :]).then_inc(sem["t_high"], 1)

            def take_attended(u, b, free):
                act.wait_ge(sem["attended"], u + 1)
                if free:
                    act.wait_ge(sem["out_done"], u - 1)
                act.copy(attn[:, b % 2, :], k.ps[:, 7, :]).then_inc(sem["attn_ready"], 1)

            def body(h, b, first, last):
                u = 4 * h + b
                some1, some2, some3 = (not first or b >= i for i in (1, 2, 3))
                more = not last or b < B - 1
                nb, nh = (b + 1) % B, h if b < B - 1 else h + 1
                b1 = (b + 3) % B
                if some1:
                    high_turned(u - 1, b1, 1, some3)
                if more:
                    high_q(u + 1, nh, nb)
                exps(u, b, 0, some2)
                if some1:
                    high_turned(u - 1, b1, 2, some3)
                if some2:
                    take_attended(u - 2, (b + 2) % B, not first)
                if some1:
                    high_turned(u - 1, b1, 3, some3)
                if more:
                    high_k(u + 1, nh, nb)
                exps(u, b, 1, some2)
                if some1:
                    high_turned(u - 1, b1, 4, some3)
                if b == B - 1 and not last:
                    media_keys(nh)
                exps(u, b, 2, some2)
                high_turned(u, b, 0, some2)
                exps(u, b, 3, some2)

            high_q(0, 0, 0)
            high_k(0, 0, 0)
            media_keys(0)
            heads(act, body)
            high_turned(U - 1, B - 1, 1, True)
            high_turned(U - 1, B - 1, 2, True)
            take_attended(U - 2, (U - 2) % B, True)
            high_turned(U - 1, B - 1, 3, True)
            high_turned(U - 1, B - 1, 4, True)
            take_attended(U - 1, B - 1, True)

        @block.vector
        def _(dve):
            def low_part(u, h, b, out, high, bank, at, w, high_sem, low_sem):
                dve.wait_ge(sem[high_sem], u + 1)
                dve.scalar_tensor_tensor(out, k.ps[:, bank, 0:w], bias_col(at, h), high, ALU.add,
                                         ALU.subtract).then_inc(sem[low_sem], 1)

            def low_q(u, h, b):
                low_part(u, h, b, qT[:, b % 2, 1, :], qT[:, b % 2, 0, :], 6, bq, S, "q_high", "q_low")

            def low_k(u, h, b):
                low_part(u, h, b, kT[:, b % 2, 1, :], kT[:, b % 2, 0, :], 6, bk, S, "k_high", "k_low")

            def invert(s, q, free):
                dve.wait_ge(sem["exp_done"], s + 1)
                if free:
                    dve.wait_ge(sem["normed"], s - 3)
                dve.reciprocal(inverse[:, q:q + 1], exp_sum[:, q:q + 1]).then_inc(sem["inv_ready"], 1)

            def maximum(s, q):
                dve.wait_ge(sem["scored"], s + 1)
                dve.tensor_reduce(minus_max[:, q:q + 1], pair(q)[:, 0:KV], AX_X, ALU.max,
                                  negate=True).then_inc(sem["max_ready"], 1)

            def low_turned(u, b, q):
                use = 5 * u + q
                bank = 4 + (b + q) % 2
                dve.wait_ge(sem["t_high"], use + 1)
                if q < QT:
                    at = slice(q * P, (q + 1) * P)
                    dve.tensor_tensor(turned_low[:, b % 2, 0:QT, at],
                                      k.ps[:, bank, :].rearrange("p (i t) -> p i t", t=P),
                                      turned_high[:, b % 2, 0:QT, at], ALU.subtract).then_inc(sem["t_low"], 1)
                else:
                    dve.tensor_tensor(turned_low[0:C, b % 2, QT, :], k.ps[0:C, bank, :],
                                      turned_high[0:C, b % 2, QT, :], ALU.subtract).then_inc(sem["t_low"], 1)

            def add_output(u, b, first):
                dve.wait_ge(sem["out_done"], u + 1)
                if first:
                    dve.tensor_scalar(k.yT[:, b, :], k.ps[:, 7, :], k.out_bias[:, 0:1], None,
                                      ALU.add).then_inc(sem["added"], 1)
                else:
                    dve.tensor_tensor(k.yT[:, b, :], k.yT[:, b, :], k.ps[:, 7, :],
                                      ALU.add).then_inc(sem["added"], 1)

            def body(h, b, first, last):
                u = 4 * h + b
                some1, some2 = not first or b >= 1, not first or b >= 2
                more = not last or b < B - 1
                nb, nh = (b + 1) % B, h if b < B - 1 else h + 1
                b1 = (b + 3) % B
                if some1:
                    invert(4 * u - 1, 3, some2)
                    low_turned(u - 1, b1, 1)
                maximum(4 * u, 0)
                if more:
                    low_q(u + 1, nh, nb)
                invert(4 * u, 0, some1)
                if some1:
                    low_turned(u - 1, b1, 2)
                maximum(4 * u + 1, 1)
                if some1:
                    low_turned(u - 1, b1, 3)
                if more:
                    low_k(u + 1, nh, nb)
                invert(4 * u + 1, 1, some1)
                maximum(4 * u + 2, 2)
                if some2:
                    add_output(u - 2, (b + 2) % B, first or (isinstance(h, int) and h == 1 and b < 2))
                if some1:
                    low_turned(u - 1, b1, 4)
                invert(4 * u + 2, 2, some1)
                low_turned(u, b, 0)
                maximum(4 * u + 3, 3)

            low_q(0, 0, 0)
            low_k(0, 0, 0)
            for h in (0, 1):
                for b in range(B):
                    body(h, b, h == 0, False)
            with dve.Fori(2, XH - 1) as i:
                for b in range(B):
                    body(i, b, False, False)
            for b in range(B):
                body(XH - 1, b, False, True)
            invert(4 * U - 1, 3, True)
            for q in (1, 2, 3, 4):
                low_turned(U - 1, B - 1, q)
            add_output(U - 2, (U - 2) % B, False)
            add_output(U - 1, B - 1, False)



def xattn1_out(nc, k):
    with ExitStack() as ctx:
        m = Stage(nc, ctx, "f0_", k)
        n = Norm(m, "norm")
        r = Scores(m, k, 32)
        names = ["outT", "x_ready", "in_psum", "x32_ready", "high_ready"]
        sem = {x: m.sem(x) for x in names}
        block = ctx.enter_context(nc.Block())

        @block.gpsimd
        def _(pool):
            m.clear_last(pool)
            for b in range(B):
                norm_rstd(pool, k, n, b)
            pool.wait_ge(k.w_loaded["f"], 16)
            split_first_units(pool, k, m, "f_")

        @block.vector
        def _(dve):
            for b in range(B):
                at = slice(b * QT, (b + 1) * QT)
                dve.wait_ge(sem["outT"], b + 1)
                dve.tensor_tensor(k.x[:, at, :], k.x[:, at, :],
                                  k.ps[:, b, :].rearrange("p (q d) -> p q d", d=D),
                                  ALU.add).then_inc(sem["x_ready"], 1)
            norm_all(dve, n, k.x, lambda b: dve.wait_ge(sem["x_ready"], b + 1))
            for b in range(B):
                dve.wait_ge(sem["high_ready"], b + 1)
                dve.tensor_tensor(k.x_low[:, b, :], k.xT32[:, b, :], k.x_high[:, b, :],
                                  ALU.subtract).then_inc(k.f_x_ready, 1)

        @block.tensor
        def _(pe):
            for b in range(B):
                for q in range(QT):
                    last = pe.transpose(k.ps[:, b, q * P:(q + 1) * P], k.yT[:, b, q * P:(q + 1) * P], k.ident[:, :])
                last.then_inc(sem["outT"], 1)
            for b in range(B):
                n.wait_ready(pe, b)
                pe.wait_ge(sem["x_ready"], b + 1)
                transpose_batch(pe, k, n.out, b, b).then_inc(sem["in_psum"], 1)
            pe.wait_ge(k.w_loaded["f"], 16)
            for b in range(B):
                pe.wait_ge(sem["x32_ready"], b + 1)
                route_tensor_logits(pe, k, r, weight(k, "f_gate"), k.xT32, b, 4 + b)

        @block.scalar
        def _(act):
            norm_scalar(act, n, k.x)
            for b in range(B):
                act.wait_ge(sem["in_psum"], b + 1)
                act.copy(k.xT32[:, b, :], k.ps[:, b, :]).then_inc(sem["x32_ready"], 1)
                act.copy(k.x_high[:, b, :], k.ps[:, b, :]).then_inc(sem["high_ready"], 1)
            for b in range(B):
                route_scalar_scores(act, k, r, b, 4 + b)


def decoder(nc, x, ctx_token, ctxT, side, w, cols, rows, ident, ident16, sel, out):
    k = Kept()
    k.stage = 0
    k.x_dram, k.ctx_dram, k.ctxT_dram, k.side_dram = x, ctx_token, ctxT, side
    k.w_dram, k.cols_dram, k.rows_dram, k.ident_dram = w, cols, rows, ident
    k.ident16_dram, k.sel_dram, k.out_dram = ident16.bitcast(BF16), sel.bitcast(BF16), out
    k.scratch = nc.dram_tensor("split_scratch", [2, B, PARTS, P, S], BF16).ap()
    with ExitStack() as ctx:
        m = Memory(nc, ctx, "k_")
        k.ps = ctx.enter_context(nc.psum_tensor("banks", [P, 8, S], F32))
        k.x = m.sb("x", [P, T, D])
        k.w = m.sb("w", [P, W_COLS])
        k.cols = m.sb("cols", [P, N_COL])
        k.rows = m.sb("rows", [P, N_ROW])
        k.ident = m.sb("ident", [P, P])
        k.ident16 = m.sb("ident16", [P, P], BF16)
        k.sel = m.sb("sel", [P, 16, D], BF16)
        k.minus_half = m.sb("minus_half", [P, QT])
        k.x_loaded = [m.sem(f"x_loaded{b}") for b in range(B)]
        k.w_loaded = {x: m.sem("w_loaded_" + x) for x in ("ab", "cd", "e", "f")}
        k.small_loaded, k.side_loaded = m.sem("small_loaded"), m.sem("side_loaded")
        k.constants_set, k.passed = m.sem("constants_set"), m.sem("passed")
        k.c_x_ready, k.f_x_ready = m.sem("c_x_ready"), m.sem("f_x_ready")
        k.v_ready, k.kv_ready = m.sem("v_ready"), m.sem("kv_ready")
        k.media = m.sb("media", [P, B, D])
        k.media_loaded = m.sem("media_loaded")
        k.d_stored = [m.sem(f"d_stored{b}") for b in range(B)]
        k.d_loaded = m.sem("d_loaded")
        k.a_stored = [m.sem(f"a_stored{b}") for b in range(B)]
        k.a_loaded = [m.sem(f"a_loaded{b}") for b in range(B)]
        with ExitStack() as layer:
            l = Memory(nc, layer, "l0_")
            k.ctxT = l.sb("ctxT", [P, B * C])
            k.ctx_kT = l.sb("ctx_kT", [P, B * C])
            k.ctx_v = l.sb("ctx_v", [P, B, D])
            k.side = l.sb("side", [P, T, C])
            k.vT = l.sb("vT", [P, B, S])
            k.exp_sum = l.sb("exp_sum", [P, B * H, QT])
            with ExitStack() as stacks:
                st = Memory(nc, stacks, "a_")
                k.q_stack = st.sb("q_stack", [P, 2, H, S], BF16)
                k.k_stack = st.sb("k_stack", [P, 2, H, S], BF16)
                attn0_project(nc, k)
                attn0_heads(nc, k)
            k.x_high = l.sb("x_high", [P, B, S], F32R)
            k.x_low = l.sb("x_low", [P, B, S], F32R)
            k.unit_weights = UnitWeights(l)
            k.routeT = l.sb("routeT", [P, B, S], BF16)
            k.route_scores = l.sb("route_scores", [P, T, scores_width(16, 2)])
            with ExitStack() as wide:
                k.xT32 = Memory(nc, wide, "l0_").sb("xT32", [P, B, S])
                attn0_out_xattn0(nc, k)
            moe(nc, k, "c_", 16, 2, 0, False)
        with ExitStack() as layer:
            l = Memory(nc, layer, "l1a_")
            k.exp_sum = l.sb("exp_sum", [P, B * H, QT])
            k.attended = l.sb("attended", [P, B, S])
            with ExitStack() as stacks:
                st = Memory(nc, stacks, "d_")
                k.v_padded = st.sb("v_padded", [P, B, NK // P, 4 * (D + HD)])
                k.q_stack = st.sb("q_stack", [P, 2, H, S], BF16)
                k.k_stack = st.sb("k_stack", [P, 2, H, NK], BF16)
                attn1_project(nc, k)
                attn1_heads(nc, k)
            with ExitStack() as cross:
                e = Memory(nc, cross, "l1b_")
                k.kvT_high = e.sb("kvT_high", [P, B, KV + 1], F32R)
                k.kvT_low = e.sb("kvT_low", [P, B, KV + 1], F32R)
                k.kv_high = e.sb("kv_high", [P, B, KT, D], F32R)
                k.kv_low = e.sb("kv_low", [P, B, KT, D], F32R)
                k.w_vo = weight(k, "e_vT").rearrange("p (h d) -> p h d", h=XH)
                k.wq, k.wk = e.sb("wq", [P, 2, D], F32R), e.sb("wk", [P, 2, D], F32R)
                k.out_bias = e.sb("out_bias", [P, 1])
                k.yT = k.attended
                attn1_out_latents(nc, k)
                xattn1_heads(nc, k)
            k.x_high = l.sb("x_high", [P, B, S], F32R)
            k.x_low = l.sb("x_low", [P, B, S], F32R)
            k.unit_weights = UnitWeights(l)
            k.routeT = l.sb("routeT", [P, B, S], BF16)
            k.route_scores = l.sb("route_scores", [P, T, scores_width(32, 6)])
            with ExitStack() as wide:
                k.xT32 = Memory(nc, wide, "l1_").sb("xT32", [P, B, S])
                xattn1_out(nc, k)
            moe(nc, k, "f_", 32, 6, 8, True)


def pack(i):

    f = {n: np.asarray(a) for n, a in i.items()}

    def pad(a, n, axis):
        shape = list(a.shape)
        shape[axis] = n - a.shape[axis]
        return np.concatenate([a, np.zeros(shape, a.dtype)], axis)

    def pairs_gu(gate, up, shared_gate, shared_up):
        e = gate.shape[0]
        g = gate.reshape(e // 2, 2, D, -1).transpose(2, 0, 1, 3).reshape(D, e // 2, D)
        u = up.reshape(e // 2, 2, D, -1).transpose(2, 0, 1, 3).reshape(D, e // 2, D)
        g = np.concatenate([pad(shared_gate, D, 1)[:, None], g], 1)
        u = np.concatenate([pad(shared_up, D, 1)[:, None], u], 1)
        return np.stack([g, u], 2).reshape(D, -1)

    def pairs_down(down, shared):
        e = down.shape[0]
        d = down.reshape(e // 2, D, D).transpose(1, 0, 2)
        return np.concatenate([pad(shared, D, 0)[:, None], d], 1).reshape(D, -1)

    gu, wkv = f["L1_ffn_experts_gate_up"], f["L1_xattn_Wkv"]
    inner = XH * D
    d_out = f["L1_attn_out_w"].T.reshape(4, 4, HD, D).transpose(1, 0, 2, 3).reshape(D, D)
    w_in = f["L0_attn_w_in"].reshape(H, 3, HD, D).transpose(1, 0, 2, 3)
    b_in = f["L0_attn_b_in"].reshape(H, 3, HD).transpose(1, 0, 2).reshape(-1)
    w = {
        "a_qkv": w_in.reshape(3 * D, D).T, "a_out": f["L0_attn_w_out"].T,
        "b_q": f["L0_xattn_Wq"].T, "b_k": f["L0_xattn_Wk"].T, "b_v": f["L0_xattn_Wv"].T,
        "c_gate": f["L0_ffn_gate_w"].T,
        "c_gu": pairs_gu(f["L0_ffn_w_gate"], f["L0_ffn_w_up"], f["L0_ffn_ws_gate"], f["L0_ffn_ws_up"]),
        "c_down": pairs_down(f["L0_ffn_w_down"], f["L0_ffn_ws_down"]),
        "d_q": f["L1_attn_q_w"].T, "d_k": f["L1_attn_k_w"].T, "d_v": f["L1_attn_v_w"].T, "d_out": d_out,
        "e_q": f["L1_xattn_Wq"], "e_k": wkv[:, 0:inner],
        "e_vT": wkv[:, inner:].reshape(D, XH, D).transpose(2, 1, 0).reshape(D, -1),
        "e_o": f["L1_xattn_Wo"].reshape(XH, D, D).transpose(1, 0, 2).reshape(D, -1),
        "f_gate": f["L1_ffn_gate_weight"].T,
        "f_gu": pairs_gu(gu[:, 0:64].transpose(0, 2, 1), gu[:, 64:].transpose(0, 2, 1),
                         f["L1_ffn_shared_gate_w"].T, f["L1_ffn_shared_up_w"].T),
        "f_down": pairs_down(f["L1_ffn_experts_down"].transpose(0, 2, 1), f["L1_ffn_shared_down_w"].T),
    }
    bkv = f["L1_xattn_bkv"]
    c = {
        "a_bq": b_in[0:D], "a_bk": b_in[D:2 * D], "a_bv": b_in[2 * D:], "b_bq": f["L0_xattn_bq"],
        "b_bk": f["L0_xattn_bk"], "d_bq": f["L1_attn_q_b"], "d_bk": f["L1_attn_k_b"],
        "conv_w": f["L1_attn_conv_w"].reshape(D, 3).T, "conv_b": f["L1_attn_conv_b"],
        "g_lat": f["L1_xattn_gamma_lat"], "b_lat": f["L1_xattn_beta_lat"],
        "g_med": f["L1_xattn_gamma_media"], "b_med": f["L1_xattn_beta_media"], "e_bo": f["L1_xattn_bo"],
        "e_bq": f["L1_xattn_bq"], "e_bk": bkv[0:inner], "e_bv": bkv[inner:],
    }
    r = {
        "a_bo": f["L0_attn_b_out"], "b_bv": f["L0_xattn_bv"], "d_bv": f["L1_attn_v_b"], "d_bo": f["L1_attn_out_b"],
        "g_lat": c["g_lat"], "b_lat": c["b_lat"], "g_med": c["g_med"], "b_med": c["b_med"],
        "e_score": f["L1_ffn_e_score_correction_bias"],
        "betas": np.stack([f["L0_xattn_beta_risk"], f["L0_xattn_beta_prio"], f["L0_xattn_beta_impl"]]),
    }
    sel = np.zeros((P, 16, D), np.uint16)
    for part in range(PARTS):
        for e in range(32):
            sel[part * SLOT_E + e, e // 2, 64 * (e % 2):64 * (e % 2) + 64] = BF16_ONE
    return {
        "x": f["x"], "ctx_token": f["ctx_1024"],
        "ctxT": f["ctx_1024"].transpose(2, 0, 1).reshape(D, B * C), "side": f["fside_BxSxS2_0"],
        "w": np.concatenate([w[n].reshape(D, -1) for n in COLS], 1),
        "cols": np.concatenate([c[n].reshape(-1, D) for n in COL], 0).T,
        "rows": np.concatenate([r[n].reshape(-1) for n in ROW]),
        "ident": np.eye(P, dtype=np.float32), "ident16": np.diag(np.full(P, BF16_ONE, np.uint16)), "sel": sel,
    }


def kernel(**inputs):
    import concourse.bacc as bacc
    from concourse.bass_utils import run_bass_kernel_spmd

    nc = bacc.Bacc("TRN2", target_bir_lowering=False, num_devices=1)
    arrays, args = {}, []
    for name, a in pack(inputs).items():
        a = np.ascontiguousarray(a)
        arrays[f"in_{name}"] = a
        args.append(nc.dram_tensor(f"in_{name}", a.shape, mybir.dt.from_np(a.dtype), kind="ExternalInput").ap())
    args.append(nc.dram_tensor("out", (B, S, D), F32, kind="ExternalOutput").ap())
    decoder(nc, *args)
    return run_bass_kernel_spmd(nc, [arrays], core_ids=[0]).results[0]["out"]
```
